# Optimizing a Trainium2 kernel written in Bass

```python
import numpy as np
import jax
import jax.numpy as jnp

def _softmax(x, axis=-1):
    return jax.nn.softmax(x, axis=axis)

def _gelu(x):
    return jax.nn.gelu(x, approximate=True)

def _silu(x):
    return jax.nn.silu(x)

def _sigmoid(x):
    return jax.nn.sigmoid(x)

def _layernorm(x, axis=-1, eps=1e-05):
    m = jnp.mean(x, axis=axis, keepdims=True)
    v = jnp.var(x, axis=axis, keepdims=True)
    return (x - m) / jnp.sqrt(v + eps)

def _scatter_add(tgt, idx, src, axis=0):
    return tgt.at[idx].add(src)

def _segment_sum(src, seg, n):
    return jax.ops.segment_sum(src, seg, n)
kernel_name = 'mk_xattn_ffn_d4_seqx_r8_bc3993'

def setup_inputs(seed: int=0):
    np.random.seed(seed)
    _w = jnp.asarray

    def _rec_inputs():
        import jax
        import jax.numpy as jnp
        _rk = jax.random.key(seed)
        x = -0.0005146 + 1 * jax.random.normal(jax.random.fold_in(_rk, 1), (32, 128, 128), jnp.float32)
        _lenS = 128 - jax.random.randint(jax.random.fold_in(_rk, 7), (32,), 0, max(1, 128 // 4) + 1, jnp.int32)
        _lenS2 = 128 - jax.random.randint(jax.random.fold_in(_rk, 8), (32,), 0, max(1, 128 // 4) + 1, jnp.int32)
        _ctx_1024P = jax.random.normal(jax.random.fold_in(_rk, 11), (32, 16, 128), jnp.float32)
        _ctx_1024c = jax.random.dirichlet(jax.random.fold_in(_rk, 511), 0.3 * jnp.ones((16,), jnp.float32), (32, 128))
        _ctx_1024t = jnp.einsum('bsk,bkd->bsd', _ctx_1024c, _ctx_1024P)
        _ctx_1024t = _ctx_1024t * jax.lax.rsqrt(jnp.mean(jnp.square(_ctx_1024t)) + 1e-12) * 0.953939
        ctx_1024 = -7.10856e-05 + 0.999911 * (_ctx_1024t + 0.3 * jax.random.normal(jax.random.fold_in(_rk, 611), (32, 128, 128), jnp.float32))
        _validS = jnp.arange(128)[None, :] < _lenS[:, None]
        _validS2 = jnp.arange(128)[None, :] < _lenS2[:, None]
        _causal = jnp.tril(jnp.ones((128, 128), dtype=bool))
        mask_BxS2_if1 = jnp.where(jnp.ones((32, 128), dtype=bool), 1, 0).astype(jnp.int32)
        mask_BxS2_ik1 = jnp.where(jnp.broadcast_to(_validS2[:, :], (32, 128)), 1, 0).astype(jnp.int32)
        return (x, ctx_1024, mask_BxS2_if1, mask_BxS2_ik1)
    x, ctx_1024, mask_BxS2_if1, mask_BxS2_ik1 = _rec_inputs()

    def _L0_xattn_setup():
        import jax, jax.numpy as jnp
        import numpy as np
        B, L, P, D = (32, 256, 64, 128)
        MAX_HOP = 2
        key = jax.random.key(seed)
        k1, k2, k3, k4 = jax.random.split(key, 4)
        return {'context': jax.random.normal(k1, (B, L, D), dtype=jnp.float32), 'mem0': jax.random.normal(k2, (B, P, D), dtype=jnp.float32), 'W0': jax.random.normal(k3, (D, D), dtype=jnp.float32) * 0.02, 'W1': jax.random.normal(k4, (D, D), dtype=jnp.float32) * 0.02, 'mask': jnp.ones((B, L), dtype=jnp.int32)}
    _L0_xattn_all = _L0_xattn_setup()
    _L0_xattn_in = {k: v for k, v in _L0_xattn_all.items() if k in ('W0', 'W1')}
    del _L0_xattn_all

    def _L0_ffn_setup():
        import jax, jax.numpy as jnp
        import numpy as np
        TOP_K = 2
        key = jax.random.key(seed)
        ks = jax.random.split(key, 6)
        B, T, H, E, F = (2, 256, 128, 8, 512)
        s = 0.02
        return {'hidden_states': jax.random.normal(ks[0], (B, T, H), dtype=jnp.float32), 'router_w': jax.random.normal(ks[1], (E, H), dtype=jnp.float32) * s, 'w1': jax.random.normal(ks[2], (E, F, H), dtype=jnp.float32) * s, 'b1': jax.random.normal(ks[3], (E, F), dtype=jnp.float32) * s, 'w2': jax.random.normal(ks[4], (E, H, F), dtype=jnp.float32) * s, 'b2': jax.random.normal(ks[5], (E, H), dtype=jnp.float32) * s}
    _L0_ffn_all = _L0_ffn_setup()
    _L0_ffn_in = {k: v for k, v in _L0_ffn_all.items() if k in ('router_w', 'w1', 'b1', 'w2', 'b2')}
    del _L0_ffn_all

    def _L1_xattn_setup():
        import jax, jax.numpy as jnp
        import numpy as np
        B, T, C, H = (4, 512, 128, 16)
        D = C // H

        def _heads(t):
            b, n, c = t.shape
            return t.reshape(b, n, H, D).transpose(0, 2, 1, 3)
        key = jax.random.key(seed)
        ks = jax.random.split(key, 10)
        s = 1.0 / np.sqrt(C)
        return {'x': jax.random.normal(ks[0], (B, T, C), jnp.float32), 'y': jax.random.normal(ks[1], (B, T, C), jnp.float32), 'Wq': jax.random.normal(ks[2], (C, C), jnp.float32) * s, 'bq': jnp.zeros((C,), jnp.float32), 'Wk': jax.random.normal(ks[3], (C, C), jnp.float32) * s, 'bk': jnp.zeros((C,), jnp.float32), 'Wv': jax.random.normal(ks[4], (C, C), jnp.float32) * s, 'bv': jnp.zeros((C,), jnp.float32), 'Wp': jax.random.normal(ks[5], (C, C), jnp.float32) * s, 'bp': jnp.zeros((C,), jnp.float32)}
    _L1_xattn_all = _L1_xattn_setup()
    _L1_xattn_in = {k: v for k, v in _L1_xattn_all.items() if k in ('Wq', 'bq', 'Wk', 'bk', 'Wv', 'bv', 'Wp', 'bp')}
    del _L1_xattn_all

    def _L1_ffn_setup():
        import jax, jax.numpy as jnp
        import numpy as np
        B, T = (2, 256)
        D_MODEL, D_HIDDEN = (128, 256)
        N_EXPERTS, TOP_K = (8, 2)
        N_TOKENS = B * T
        CAPACITY = 2 * N_TOKENS * TOP_K // N_EXPERTS
        key = jax.random.key(seed)
        k_x, k_rw, k_w, k_v, k_o = jax.random.split(key, 5)
        x = jax.random.normal(k_x, (B, T, D_MODEL), jnp.float32)
        router_w = jax.random.normal(k_rw, (N_EXPERTS, D_MODEL), jnp.float32) * D_MODEL ** (-0.5)
        router_b = jnp.zeros((N_EXPERTS,), jnp.float32)
        W = jax.random.normal(k_w, (N_EXPERTS, D_MODEL, D_HIDDEN), jnp.float32) * D_MODEL ** (-0.5)
        V = jax.random.normal(k_v, (N_EXPERTS, D_MODEL, D_HIDDEN), jnp.float32) * D_MODEL ** (-0.5)
        W_out = jax.random.normal(k_o, (N_EXPERTS, D_HIDDEN, D_MODEL), jnp.float32) * D_HIDDEN ** (-0.5)
        return {'x': x, 'router_w': router_w, 'router_b': router_b, 'W': W, 'V': V, 'W_out': W_out}
    _L1_ffn_all = _L1_ffn_setup()
    _L1_ffn_in = {k: v for k, v in _L1_ffn_all.items() if k in ('router_w', 'router_b', 'W', 'V', 'W_out')}
    del _L1_ffn_all

    def _L2_xattn_setup():
        import jax, jax.numpy as jnp
        import numpy as np
        DIM = 128
        HEADS = 16
        DIM_HEAD = 64
        INNER = HEADS * DIM_HEAD
        EPS = 1e-05

        def _layernorm(t, w, b):
            mu = jnp.mean(t, axis=-1, keepdims=True)
            var = jnp.mean(jnp.square(t - mu), axis=-1, keepdims=True)
            return (t - mu) * jax.lax.rsqrt(var + EPS) * w + b
        key = jax.random.key(seed)
        ks = jax.random.split(key, 8)
        b, n, l = (8, 512, 64)
        x = jax.random.normal(ks[0], (b, n, DIM), dtype=jnp.float32)
        latents = jax.random.normal(ks[1], (b, l, DIM), dtype=jnp.float32)
        ln1_w = jnp.ones((DIM,), jnp.float32)
        ln1_b = jnp.zeros((DIM,), jnp.float32)
        ln2_w = jnp.ones((DIM,), jnp.float32)
        ln2_b = jnp.zeros((DIM,), jnp.float32)
        Wq = jax.random.normal(ks[2], (DIM, INNER), dtype=jnp.float32) / np.sqrt(DIM)
        Wkv = jax.random.normal(ks[3], (DIM, 2 * INNER), dtype=jnp.float32) / np.sqrt(DIM)
        Wo = jax.random.normal(ks[4], (INNER, DIM), dtype=jnp.float32) / np.sqrt(INNER)
        return {'x': x, 'latents': latents, 'ln1_w': ln1_w, 'ln1_b': ln1_b, 'ln2_w': ln2_w, 'ln2_b': ln2_b, 'Wq': Wq, 'Wkv': Wkv, 'Wo': Wo}
    _L2_xattn_all = _L2_xattn_setup()
    _L2_xattn_in = {k: v for k, v in _L2_xattn_all.items() if k in ('ln1_w', 'ln1_b', 'ln2_w', 'ln2_b', 'Wq', 'Wkv', 'Wo')}
    del _L2_xattn_all

    def _L2_ffn_setup():
        import jax, jax.numpy as jnp
        import numpy as np
        FF_DIM = 256
        TOP_K = 2
        key = jax.random.key(seed)
        k1, k2, k3, k4 = jax.random.split(key, 4)
        B, S, D, E, F = (2, 256, 128, 8, FF_DIM)
        std = 0.006
        return {'x': jax.random.normal(k1, (B, S, D), dtype=jnp.float32), 'gate_w': jax.random.normal(k2, (D, E), dtype=jnp.float32) * 0.02, 'gate_up_w': jax.random.normal(k3, (E, D, 2 * F), dtype=jnp.float32) * std, 'down_w': jax.random.normal(k4, (E, F, D), dtype=jnp.float32) * std}
    _L2_ffn_all = _L2_ffn_setup()
    _L2_ffn_in = {k: v for k, v in _L2_ffn_all.items() if k in ('gate_w', 'gate_up_w', 'down_w')}
    del _L2_ffn_all

    def _L3_xattn_setup():
        import jax, jax.numpy as jnp
        import numpy as np
        D = 128
        B, LQ, LK = (8, 256, 256)
        NEG = -1000000000.0
        key = jax.random.key(seed)
        ks = jax.random.split(key, 8)
        query = jax.random.normal(ks[0], (B, LQ, D), dtype=jnp.float32)
        k_in = jax.random.normal(ks[1], (B, LK, D), dtype=jnp.float32)
        value = jax.random.normal(ks[2], (B, LK, D), dtype=jnp.float32)
        mask = jax.random.randint(ks[3], (B, LK), 0, 2, dtype=jnp.int32)
        s = 1.0 / np.sqrt(D)
        Wq_w = jax.random.normal(ks[4], (D, D), dtype=jnp.float32) * s
        Wq_b = jnp.zeros((D,), dtype=jnp.float32)
        Wk_w = jax.random.normal(ks[5], (D, D), dtype=jnp.float32) * s
        Wk_b = jnp.zeros((D,), dtype=jnp.float32)
        return {'query': query, 'key': k_in, 'value': value, 'mask': mask, 'Wq_w': Wq_w, 'Wq_b': Wq_b, 'Wk_w': Wk_w, 'Wk_b': Wk_b}
    _L3_xattn_all = _L3_xattn_setup()
    _L3_xattn_in = {k: v for k, v in _L3_xattn_all.items() if k in ('Wq_w', 'Wq_b', 'Wk_w', 'Wk_b')}
    del _L3_xattn_all

    def _L3_ffn_setup():
        import jax, jax.numpy as jnp
        import numpy as np
        NUM_EXPERTS = 8
        N_EMBD = 128
        D_FF = 4 * N_EMBD
        B, S = (4, 256)
        key = jax.random.key(seed)
        ks = jax.random.split(key, 6)
        x = jax.random.normal(ks[0], (B, S, N_EMBD), dtype=jnp.float32)
        gate_w = jax.random.normal(ks[1], (N_EMBD, NUM_EXPERTS), dtype=jnp.float32) * 0.02
        w1 = jax.random.normal(ks[2], (NUM_EXPERTS, N_EMBD, D_FF), dtype=jnp.float32) * 0.02
        b1 = jnp.zeros((NUM_EXPERTS, D_FF), dtype=jnp.float32)
        w2 = jax.random.normal(ks[3], (NUM_EXPERTS, D_FF, N_EMBD), dtype=jnp.float32) * 0.02
        b2 = jnp.zeros((NUM_EXPERTS, N_EMBD), dtype=jnp.float32)
        return {'x': x, 'gate_w': gate_w, 'w1': w1, 'b1': b1, 'w2': w2, 'b2': b2}
    _L3_ffn_all = _L3_ffn_setup()
    _L3_ffn_in = {k: v for k, v in _L3_ffn_all.items() if k in ('gate_w', 'w1', 'b1', 'w2', 'b2')}
    del _L3_ffn_all
    return {'x': x, 'ctx_1024': ctx_1024, 'mask_BxS2_if1': mask_BxS2_if1, 'mask_BxS2_ik1': mask_BxS2_ik1, 'L0_xattn_W0': _L0_xattn_in['W0'], 'L0_xattn_W1': _L0_xattn_in['W1'], 'L0_ffn_router_w': _L0_ffn_in['router_w'], 'L0_ffn_w1': _L0_ffn_in['w1'], 'L0_ffn_b1': _L0_ffn_in['b1'], 'L0_ffn_w2': _L0_ffn_in['w2'], 'L0_ffn_b2': _L0_ffn_in['b2'], 'L1_xattn_Wq': _L1_xattn_in['Wq'], 'L1_xattn_bq': _L1_xattn_in['bq'], 'L1_xattn_Wk': _L1_xattn_in['Wk'], 'L1_xattn_bk': _L1_xattn_in['bk'], 'L1_xattn_Wv': _L1_xattn_in['Wv'], 'L1_xattn_bv': _L1_xattn_in['bv'], 'L1_xattn_Wp': _L1_xattn_in['Wp'], 'L1_xattn_bp': _L1_xattn_in['bp'], 'L1_ffn_router_w': _L1_ffn_in['router_w'], 'L1_ffn_router_b': _L1_ffn_in['router_b'], 'L1_ffn_W': _L1_ffn_in['W'], 'L1_ffn_V': _L1_ffn_in['V'], 'L1_ffn_W_out': _L1_ffn_in['W_out'], 'L2_xattn_ln1_w': _L2_xattn_in['ln1_w'], 'L2_xattn_ln1_b': _L2_xattn_in['ln1_b'], 'L2_xattn_ln2_w': _L2_xattn_in['ln2_w'], 'L2_xattn_ln2_b': _L2_xattn_in['ln2_b'], 'L2_xattn_Wq': _L2_xattn_in['Wq'], 'L2_xattn_Wkv': _L2_xattn_in['Wkv'], 'L2_xattn_Wo': _L2_xattn_in['Wo'], 'L2_ffn_gate_w': _L2_ffn_in['gate_w'], 'L2_ffn_gate_up_w': _L2_ffn_in['gate_up_w'], 'L2_ffn_down_w': _L2_ffn_in['down_w'], 'L3_xattn_Wq_w': _L3_xattn_in['Wq_w'], 'L3_xattn_Wq_b': _L3_xattn_in['Wq_b'], 'L3_xattn_Wk_w': _L3_xattn_in['Wk_w'], 'L3_xattn_Wk_b': _L3_xattn_in['Wk_b'], 'L3_ffn_gate_w': _L3_ffn_in['gate_w'], 'L3_ffn_w1': _L3_ffn_in['w1'], 'L3_ffn_b1': _L3_ffn_in['b1'], 'L3_ffn_w2': _L3_ffn_in['w2'], 'L3_ffn_b2': _L3_ffn_in['b2']}

def reference(x, ctx_1024, mask_BxS2_if1, mask_BxS2_ik1, L0_xattn_W0, L0_xattn_W1, L0_ffn_router_w, L0_ffn_w1, L0_ffn_b1, L0_ffn_w2, L0_ffn_b2, L1_xattn_Wq, L1_xattn_bq, L1_xattn_Wk, L1_xattn_bk, L1_xattn_Wv, L1_xattn_bv, L1_xattn_Wp, L1_xattn_bp, L1_ffn_router_w, L1_ffn_router_b, L1_ffn_W, L1_ffn_V, L1_ffn_W_out, L2_xattn_ln1_w, L2_xattn_ln1_b, L2_xattn_ln2_w, L2_xattn_ln2_b, L2_xattn_Wq, L2_xattn_Wkv, L2_xattn_Wo, L2_ffn_gate_w, L2_ffn_gate_up_w, L2_ffn_down_w, L3_xattn_Wq_w, L3_xattn_Wq_b, L3_xattn_Wk_w, L3_xattn_Wk_b, L3_ffn_gate_w, L3_ffn_w1, L3_ffn_b1, L3_ffn_w2, L3_ffn_b2):
    import jax
    import jax.numpy as jnp

    def _L0_xattn_ref(context, mem0, W0, W1, mask):
        import jax, jax.numpy as jnp
        import numpy as np
        B, L, P, D = (32, 256, 64, 128)
        MAX_HOP = 2
        m = (mask == 0)[:, None, :]
        neg_inf = jnp.finfo(context.dtype).min
        u = mem0
        for W in (W0, W1):
            key_ = jnp.einsum('bpd,md->bpm', u, W)
            attn = jnp.einsum('bpm,blm->bpl', key_, context)
            attn = jnp.where(m, neg_inf, attn)
            w = jax.nn.softmax(attn, axis=-1)
            o = jnp.einsum('bpl,bld->bpd', w, context)
            u = u + o
        return u

    def _L0_ffn_ref(hidden_states, router_w, w1, b1, w2, b2):
        import jax, jax.numpy as jnp
        import numpy as np
        TOP_K = 2
        x = hidden_states
        router_logits = jnp.einsum('bth,eh->bte', x, router_w)
        topk_values, topk_indices = jax.lax.top_k(router_logits, TOP_K)
        topk_weights = jax.nn.softmax(topk_values.astype(jnp.float32), axis=-1).astype(x.dtype)
        h1 = jnp.einsum('bth,efh->btef', x, w1) + b1
        h1 = jax.nn.gelu(h1, approximate=False)
        expert_outputs = jnp.einsum('btef,ehf->bteh', h1, w2) + b2
        gather_idx = topk_indices[..., None]
        topk_expert_outputs = jnp.take_along_axis(expert_outputs, gather_idx, axis=2)
        mixed_output = jnp.sum(topk_expert_outputs * topk_weights[..., None], axis=2)
        return mixed_output

    def _L1_xattn_ref(x, y, Wq, bq, Wk, bk, Wv, bv, Wp, bp):
        import jax, jax.numpy as jnp
        import numpy as np
        B, T, C, H = (4, 512, 128, 16)
        D = C // H

        def _heads(t):
            b, n, c = t.shape
            return t.reshape(b, n, H, D).transpose(0, 2, 1, 3)
        q = jax.nn.softmax(_heads(x @ Wq.T + bq), axis=-1)
        k = jax.nn.softmax(_heads(y @ Wk.T + bk), axis=-1)
        v = _heads(y @ Wv.T + bv)
        k_cumsum = jnp.sum(k, axis=-2, keepdims=True)
        D_inv = 1.0 / jnp.sum(q * k_cumsum, axis=-1, keepdims=True)
        kv = jnp.einsum('bhnd,bhne->bhde', k, v)
        out = q + jnp.einsum('bhnd,bhde->bhne', q, kv) * D_inv
        out = out.transpose(0, 2, 1, 3).reshape(x.shape[0], x.shape[1], C)
        return out @ Wp.T + bp

    def _L1_ffn_ref(x, router_w, router_b, W, V, W_out):
        import jax, jax.numpy as jnp
        import numpy as np
        B, T = (2, 256)
        D_MODEL, D_HIDDEN = (128, 256)
        N_EXPERTS, TOP_K = (8, 2)
        N_TOKENS = B * T
        CAPACITY = 2 * N_TOKENS * TOP_K // N_EXPERTS
        Bq, Tq, D = x.shape
        N = Bq * Tq
        x_flat = x.reshape(N, D)
        router_logits = x_flat @ router_w.T + router_b
        top_vals, top_ids = jax.lax.top_k(router_logits, TOP_K)
        top_probs = jax.nn.softmax(top_vals, axis=-1)
        x_pad = jnp.concatenate([x_flat, jnp.zeros((1, D), x_flat.dtype)], axis=0)
        probs_pad = jnp.concatenate([top_probs, jnp.zeros((1, TOP_K), top_probs.dtype)], axis=0)
        out = jnp.zeros((N + 1, D), x_flat.dtype)
        for e in range(N_EXPERTS):
            tok, slot = jnp.nonzero(top_ids == e, size=CAPACITY, fill_value=(N, 0))
            w = probs_pad[tok, slot][:, None]
            xin = x_pad[tok]
            a = xin @ W[e]
            b = xin @ V[e]
            y = a * (b * jax.nn.sigmoid(b)) @ W_out[e]
            out = out.at[tok].add(y * w)
        return out[:N].reshape(Bq, Tq, D)

    def _L2_xattn_ref(x, latents, ln1_w, ln1_b, ln2_w, ln2_b, Wq, Wkv, Wo):
        import jax, jax.numpy as jnp
        import numpy as np
        DIM = 128
        HEADS = 16
        DIM_HEAD = 64
        INNER = HEADS * DIM_HEAD
        EPS = 1e-05

        def _layernorm(t, w, b):
            mu = jnp.mean(t, axis=-1, keepdims=True)
            var = jnp.mean(jnp.square(t - mu), axis=-1, keepdims=True)
            return (t - mu) * jax.lax.rsqrt(var + EPS) * w + b
        xn = _layernorm(x, ln1_w, ln1_b)
        latn = _layernorm(latents, ln2_w, ln2_b)
        b, l, _ = latn.shape
        q = latn @ Wq
        kv_input = jnp.concatenate([xn, latn], axis=1)
        kv = kv_input @ Wkv
        k, v = jnp.split(kv, 2, axis=-1)

        def heads(t):
            return t.reshape(t.shape[0], t.shape[1], HEADS, DIM_HEAD).transpose(0, 2, 1, 3)
        q, k, v = (heads(q), heads(k), heads(v))
        scale = 1.0 / np.sqrt(np.sqrt(DIM_HEAD))
        weight = jnp.einsum('bhld,bhnd->bhln', q * scale, k * scale)
        weight = jax.nn.softmax(weight.astype(jnp.float32), axis=-1).astype(weight.dtype)
        out = jnp.einsum('bhln,bhnd->bhld', weight, v)
        out = out.transpose(0, 2, 1, 3).reshape(b, l, INNER)
        return out @ Wo

    def _L2_ffn_ref(x, gate_w, gate_up_w, down_w):
        import jax, jax.numpy as jnp
        import numpy as np
        FF_DIM = 256
        TOP_K = 2
        B, S, D = x.shape
        E = gate_up_w.shape[0]
        F = down_w.shape[1]
        x_flat = x.reshape(B * S, D)
        router_logits = x_flat @ gate_w
        router_probs = jax.nn.softmax(router_logits, axis=-1)
        top_k_probs, top_k_idx = jax.lax.top_k(router_probs, TOP_K)
        top_k_probs = top_k_probs / jnp.sum(top_k_probs, axis=-1, keepdims=True)
        gate_up = jnp.einsum('nd,edh->enh', x_flat, gate_up_w)
        gate_out = gate_up[..., :F]
        up_out = gate_up[..., F:]
        hidden = jax.nn.silu(gate_out) * up_out
        expert_out = jnp.einsum('enf,efd->end', hidden, down_w)
        out_t = jnp.transpose(expert_out, (1, 0, 2))
        sel = jnp.take_along_axis(out_t, top_k_idx[:, :, None], axis=1)
        output = jnp.sum(sel * top_k_probs[:, :, None], axis=1)
        return output.reshape(B, S, D)

    def _L3_xattn_ref(query, key, value, mask, Wq_w, Wq_b, Wk_w, Wk_b):
        import jax, jax.numpy as jnp
        import numpy as np
        D = 128
        B, LQ, LK = (8, 256, 256)
        NEG = -1000000000.0
        q = jnp.einsum('bld,ed->ble', query, Wq_w) + Wq_b
        k = jnp.einsum('bld,ed->ble', key, Wk_w) + Wk_b
        scale = 1.0 / jnp.sqrt(jnp.asarray(D, dtype=q.dtype))
        aw = jnp.einsum('bqd,bkd->bqk', q, k) * scale
        m = mask.astype(aw.dtype)[:, None, :]
        aw = aw * m
        aw = jnp.where(m == 0, jnp.asarray(NEG, dtype=aw.dtype), aw)
        attn = jax.nn.softmax(aw, axis=-1)
        return jnp.einsum('bqk,bkd->bqd', attn, value)

    def _L3_ffn_ref(x, gate_w, w1, b1, w2, b2):
        import jax, jax.numpy as jnp
        import numpy as np
        NUM_EXPERTS = 8
        N_EMBD = 128
        D_FF = 4 * N_EMBD
        B, S = (4, 256)
        Bb, Ss, D = x.shape
        x_flat = x.reshape(-1, D)
        router_logits = x_flat @ gate_w
        router_probs = jax.nn.softmax(router_logits, axis=-1)
        expert_idx = jnp.argmax(router_probs, axis=-1)
        expert_w = jnp.take_along_axis(router_probs, expert_idx[:, None], axis=1)[:, 0]
        out = jnp.zeros_like(x_flat)
        for e in range(NUM_EXPERTS):
            h = jax.nn.gelu(x_flat @ w1[e] + b1[e], approximate=False)
            y = h @ w2[e] + b2[e]
            sel = expert_idx == e
            out = out + jnp.where(sel, expert_w, 0.0)[:, None] * y
        return out.reshape(Bb, Ss, D)
    x = x + _L0_xattn_ref(ctx_1024, _layernorm(x, axis=-1), L0_xattn_W0, L0_xattn_W1, mask_BxS2_if1)
    x = x + _L0_ffn_ref(_layernorm(x, axis=-1), L0_ffn_router_w, L0_ffn_w1, L0_ffn_b1, L0_ffn_w2, L0_ffn_b2)
    x = x + _L1_xattn_ref(_layernorm(x, axis=-1), ctx_1024, L1_xattn_Wq, L1_xattn_bq, L1_xattn_Wk, L1_xattn_bk, L1_xattn_Wv, L1_xattn_bv, L1_xattn_Wp, L1_xattn_bp)
    x = x + _L1_ffn_ref(_layernorm(x, axis=-1), L1_ffn_router_w, L1_ffn_router_b, L1_ffn_W, L1_ffn_V, L1_ffn_W_out)
    x = x + _L2_xattn_ref(ctx_1024, _layernorm(x, axis=-1), L2_xattn_ln1_w, L2_xattn_ln1_b, L2_xattn_ln2_w, L2_xattn_ln2_b, L2_xattn_Wq, L2_xattn_Wkv, L2_xattn_Wo)
    x = x + _L2_ffn_ref(_layernorm(x, axis=-1), L2_ffn_gate_w, L2_ffn_gate_up_w, L2_ffn_down_w)
    x = x + _L3_xattn_ref(_layernorm(x, axis=-1), ctx_1024, ctx_1024, mask_BxS2_ik1, L3_xattn_Wq_w, L3_xattn_Wq_b, L3_xattn_Wk_w, L3_xattn_Wk_b)
    x = x + _L3_ffn_ref(_layernorm(x, axis=-1), L3_ffn_gate_w, L3_ffn_w1, L3_ffn_b1, L3_ffn_w2, L3_ffn_b2)
    return x

_drawn_inputs = setup_inputs


def setup_inputs(seed=0):
    import zlib

    import numpy as np

    out = dict(_drawn_inputs(seed))
    spreads = {'L1_xattn_bq': (0.0, 0.677),
     'L1_xattn_bk': (0.0, 0.8),
     'L1_xattn_bv': (0.0, 0.1),
     'L1_xattn_bp': (0.0, 0.1),
     'L1_ffn_router_b': (0.0, 0.1),
     'L2_xattn_ln1_w': (1.0, 0.6),
     'L2_xattn_ln1_b': (0.0, 0.412),
     'L2_xattn_ln2_w': (1.0, 0.6),
     'L2_xattn_ln2_b': (0.0, 0.443),
     'L3_xattn_Wq_b': (0.0, 0.8),
     'L3_xattn_Wk_b': (0.0, 0.8),
     'L3_ffn_b1': (0.0, 0.8),
     'L3_ffn_b2': (0.0, 0.8)}
    factors = {'L0_ffn_router_w': 3.609,
     'L0_ffn_w1': 3.58,
     'L0_ffn_b1': 8.0,
     'L0_ffn_w2': 3.493,
     'L0_ffn_b2': 6.761,
     'L2_ffn_gate_w': 8.0,
     'L2_ffn_gate_up_w': 8.0,
     'L2_ffn_down_w': 8.0,
     'L3_ffn_gate_w': 8.0,
     'L3_ffn_w1': 8.0,
     'L3_ffn_w2': 8.0}
    for name, (base, spread) in spreads.items():
        noise = np.random.default_rng([zlib.crc32(name.encode()), seed]).standard_normal(out[name].shape)
        drawn = base * np.exp(spread * noise) if base else spread * noise
        out[name] = jnp.asarray(drawn.astype(out[name].dtype))
    for name, factor in factors.items():
        out[name] = (out[name] * factor).astype(out[name].dtype)
    return out
```

```python
from contextlib import ExitStack

import concourse.bass as bass
from concourse import mybir
import numpy as np

ALU = mybir.AluOpType
ACT = mybir.ActivationFunctionType
AX = mybir.AxisListType
F32 = mybir.dt.float32
BF16 = mybir.dt.bfloat16
I32 = mybir.dt.int32
U32 = mybir.dt.uint32

P = 128
B = 32
G = 4
NG = B // G
E = 8
H1 = 512
EPS = 1e-5
MASKED = -1e30
FAR = 1.0e6
CAPACITY = 256
RSQRT_SEED = 1597463007.0

TILES_TOP2 = (2 * B * P + E * (P - 1)) // P + 1
TILES_TOP1 = (B * P + E * (P - 1)) // P + 1
TILES_CAP = E * CAPACITY // P

BIAS_PARTS = [("L0_ffn_b1", E * H1), ("L3_ffn_b1", E * H1), ("L0_ffn_b2", E * P), ("L3_ffn_b2", E * P),
              ("L1_xattn_bq", P), ("L1_xattn_bk", P), ("L1_xattn_bv", P), ("L1_xattn_bp", P)]
BIAS_AT = {}
_at = 0
for _n, _w in BIAS_PARTS:
    BIAS_AT[_n] = (_at, _w)
    _at += _w
BIAS_WIDTH = _at
ROUTER_B_AT = BIAS_WIDTH
BIAS_TOTAL = BIAS_WIDTH + P


class Steps:

    def __init__(self, counter, names):
        self.base, self.names = counter.value, names
        self.counter, self.seen = counter, 0

    def tick(self, name):
        assert self.names[self.seen % len(self.names)] == name, (name, self.names[self.seen % len(self.names)])
        self.seen += 1
        return 1

    def at(self, turn, name):
        return turn * len(self.names) + (self.base + self.names.index(name) + 1)

    def close(self, turns, written=1):
        assert self.seen == len(self.names) * written, (self.seen, len(self.names))
        self.counter.value = self.base + turns * len(self.names)


class Chain:

    def __init__(self, eng):
        self.eng = eng

    def link(self, ins=None):
        self.eng.drain()


class Counter:
    def __init__(self, sem):
        self.sem, self.value = sem, 0


def build(nc, A, out):
    with ExitStack() as top:
        names = set()

        def sb_in(ctx, name, shape, dt=F32):
            while name in names:
                name += "_"
            names.add(name)
            return ctx.enter_context(nc.sbuf_tensor(name, shape, dt))

        def sb(name, shape, dt=F32):
            return sb_in(top, name, shape, dt)

        def counter(name):
            return Counter(top.enter_context(nc.semaphore(name)))

        ps = top.enter_context(nc.psum_tensor("psum_banks", [P, 8, 512], F32))
        bank = [ps[:, i, :] for i in range(8)]

        X = sb("x_rows", [P, B, P])
        XN = sb("normed_rows", [P, B, P])
        Y1 = sb("gathered_rows", [P, B, P])
        CT = sb("ctx_rows", [P, B, P])
        CTT = sb("ctx_turned", [P, B, P])
        SETA1 = sb("expert_w1_a", [P, E * H1])
        SETA2 = sb("expert_w2_a", [P, E * H1])
        SETB1 = sb("expert_w1_b", [P, E * H1])
        SETB2 = sb("expert_w2_b", [P, E * H1])
        ident = sb("ident", [P, P])
        tri = sb("tri", [P, P], BF16)
        ones = sb("ones", [P, P], BF16)
        iota8 = sb("iota8", [P, E])
        blocks = sb("head_blocks", [P, P + 16])
        wsmall = sb("wsmall", [P, 8, P])
        router = sb("router", [P, 4, E])
        rows3 = sb("bias_rows", [3, 2 * E * P + 4 * P + P], BF16)
        cols = sb("bias_cols", [P, 6])
        MX = sb("top_logits", [P, B, E])
        IX = sb("top_experts", [P, B, E])
        LG = sb("logits", [P, B, E])
        POS = sb("slots", [P, 2, B], U32)
        SCT = sb("scatter_slots", [P, 2, B], U32)
        WT = sb("mix_weights", [P, 2, B])
        tile_expert = sb("tile_expert", [1, TILES_TOP2], I32)
        iota_tile = sb("iota_tile", [1, TILES_TOP2])

        xs = nc.dram_tensor("sorted_rows", [TILES_TOP2 * P, P], F32).ap()
        ys = nc.dram_tensor("expert_rows", [TILES_TOP2 * P, P], F32).ap()
        bias_dram = nc.dram_tensor("bias_split", [3, BIAS_TOTAL], BF16).ap()
        mask_dram = nc.dram_tensor("mask_rows", [2, B * P], BF16).ap()

        loaded = counter("loaded")
        pe_done = counter("pe_done")
        act_done = counter("act_done")
        dve_done = counter("dve_done")
        pool_done = counter("pool_done")
        bias_stored = counter("bias_stored")
        rows_loaded = counter("rows_loaded")
        zeroed = counter("zeroed")
        scattered = counter("scattered")
        gathered = [counter("gathered_even"), counter("gathered_odd")]
        rows_here = counter("rows_here")
        sorted_in = [counter(f"sorted_in{i}") for i in range(4)]
        expert_out = [counter(f"expert_out{i}") for i in range(4)]
        rows_turned = counter("rows_turned")
        hidden_made = counter("hidden_made")
        hidden_turned = counter("hidden_turned")
        expert_made = counter("expert_made")
        rows_turned_kept = counter("rows_turned_kept")
        gates_kept = counter("gates_kept")
        hidden_kept = counter("hidden_kept")
        hidden_turned_kept = counter("hidden_turned_kept")
        expert_kept = counter("expert_kept")
        stored = counter("stored")
        weights_a = counter("weights_a")
        weights_b = counter("weights_b")
        weights_x = counter("weights_x")

        def group(t, g):
            return t[:, bass.ds(g * G, G), :]

        def flat(ap):
            return ap.rearrange("p a d -> p (a d)")

        with ExitStack() as ph:
            wraw = sb_in(ph, "small_raw", [P, 6, P])
            rraw = sb_in(ph, "router_raw", [E, 2, P])
            NBC = BIAS_TOTAL // P
            braw = sb_in(ph, "bias_raw", [P, NBC])
            bres = sb_in(ph, "bias_rest", [P, 2, NBC])
            bsp = sb_in(ph, "bias_split_sb", [P, 3, NBC], BF16)
            mraw = sb_in(ph, "mask_raw", [P, 2, B], I32)
            mbf = sb_in(ph, "mask_bf", [P, 2, B], BF16)
            zero = sb_in(ph, "zero_rows", [P, 1024])
            block = ph.enter_context(nc.Block())
            n_loads = 0

            @block.sync
            def _(sp):
                nonlocal n_loads

                def load(dst, src):
                    nonlocal n_loads
                    sp.dma_start(dst, src).then_inc(loaded.sem, 16)
                    n_loads += 1
                sp.wait_ge(dve_done.sem, 1)
                for name, width in BIAS_PARTS:
                    at = BIAS_AT[name][0] // P
                    src = A[name] if len(A[name].shape) == 1 else A[name].rearrange("e f -> (e f)")
                    load(braw[:, at:at + width // P], src.rearrange("(p c) -> p c", p=P))
                load(braw[0:E, NBC - 1:NBC], A["L1_ffn_router_b"].rearrange("(e a) -> e a", a=1))
                for m, name in enumerate(("mask_BxS2_if1", "mask_BxS2_ik1")):
                    load(mraw[:, m, :], A[name].rearrange("b (q c) -> (b q) c", c=B))
                for i, name in enumerate(("L1_xattn_Wq", "L1_xattn_Wk", "L1_xattn_Wv", "L1_xattn_Wp",
                                          "L3_xattn_Wq_w", "L3_xattn_Wk_w")):
                    load(wraw[:, i, :], A[name])
                load(wsmall[:, 0, :], A["L0_xattn_W0"])
                load(wsmall[:, 1, :], A["L0_xattn_W1"])
                load(rraw[:, 0, :], A["L0_ffn_router_w"])
                load(rraw[:, 1, :], A["L1_ffn_router_w"])
                load(router[:, 2, :], A["L2_ffn_gate_w"])
                load(router[:, 3, :], A["L3_ffn_gate_w"])
                for i, name in enumerate(("L3_xattn_Wq_b", "L3_xattn_Wk_b", "L2_xattn_ln1_w", "L2_xattn_ln1_b",
                                          "L2_xattn_ln2_w", "L2_xattn_ln2_b")):
                    load(cols[:, i:i + 1], A[name].rearrange("(p a) -> p a", a=1))
                load(X[:, :, :], A["x"].rearrange("t p d -> p t d"))
                load(CT[:, :, :], A["ctx_1024"].rearrange("t p d -> p t d"))
                load(SETB1[:, :].rearrange("p (c h) -> p c h", h=P), A["L0_ffn_w1"].rearrange("e (c p) h -> p (e c) h", p=P))
                load(SETB2[:, :].rearrange("p (e f) -> p e f", e=E), A["L0_ffn_w2"].rearrange("e h f -> h e f"))
                sp.wait_ge(dve_done.sem, 4)
                for k in range(3):
                    for name, width in BIAS_PARTS + [("router_b", P)]:
                        at = BIAS_AT.get(name, (ROUTER_B_AT,))[0]
                        sp.dma_start(bias_dram[k, at:at + width].rearrange("(p c) -> p c", p=P),
                                     bsp[:, k, at // P:(at + width) // P]).then_inc(bias_stored.sem, 16)
                for m in range(2):
                    sp.dma_start(mask_dram[m, :].rearrange("(p c) -> p c", p=P), mbf[:, m, :]).then_inc(bias_stored.sem, 16)
                sp.wait_ge(bias_stored.sem, 16 * (3 * (len(BIAS_PARTS) + 1) + 2))
                at = BIAS_AT["L0_ffn_b2"][0]
                sp.dma_start(rows3[:, :], bias_dram[:, at:at + 2 * E * P + 5 * P]).then_inc(rows_loaded.sem, 16)
                for i in range(TILES_TOP2 // 8):
                    sp.dma_start(xs.rearrange("(i p r) d -> i p (r d)", p=P, r=8)[i], zero[:, :]).then_inc(zeroed.sem, 16)
                sp.wait_ge(rows_loaded.sem, 16)
                sp.wait_ge(zeroed.sem, 16 * (TILES_TOP2 // 8))
                sp.wait_ge(loaded.sem, 16 * n_loads)

            @block.gpsimd
            def _(pool):
                pool.memset(blocks[:, :], 1.0).then_inc(pool_done.sem, 1)
                pool.wait_ge(pool_done.sem, 1)
                for base, sign in ((0, 1), (7, -1)):
                    pool.affine_select(out=blocks[:, 0:P].rearrange("p (h c) -> p h c", c=8), in_=blocks[:, 0:P].rearrange("p (h c) -> p h c", c=8),
                                       compare_op=ALU.is_ge, fill=0.0, base=base, pattern=[[-8 * sign, 16], [0, 8]], channel_multiplier=sign)
                    pool.affine_select(out=blocks[:, P:P + 16], in_=blocks[:, P:P + 16], compare_op=ALU.is_ge, fill=0.0, base=base,
                                       pattern=[[-8 * sign, 16]], channel_multiplier=sign).then_inc(pool_done.sem, 1)
                    pool.wait_ge(pool_done.sem, 2 if sign == 1 else 3)
                pool.memset(ident[:, :], 0.0).then_inc(pool_done.sem, 1)
                pool.memset(tri[:, :], 1.0).then_inc(pool_done.sem, 1)
                pool.iota(iota8[:, :], [[1, E]], base=0, channel_multiplier=0,
                          allow_small_or_imprecise_dtypes=True).then_inc(pool_done.sem, 1)
                pool.iota(iota_tile[:, :], [[1, TILES_TOP2]], base=0, channel_multiplier=0,
                          allow_small_or_imprecise_dtypes=True).then_inc(pool_done.sem, 1)
                pool.wait_ge(pool_done.sem, 7)
                pool.affine_select(out=ident[:, :], in_=ident[:, :], compare_op=ALU.not_equal, fill=1.0, base=0,
                                   pattern=[[-1, P]], channel_multiplier=1).then_inc(pool_done.sem, 1)
                pool.affine_select(out=tri[:, :], in_=tri[:, :], compare_op=ALU.is_gt, fill=0.0, base=0,
                                   pattern=[[1, P]], channel_multiplier=-1).then_inc(pool_done.sem, 1)

            @block.vector
            def _(dve):
                dve.memset(braw[:, :], 0.0).then_inc(dve_done.sem, 1)
                dve.memset(ones[:, :], 1.0)
                dve.memset(zero[:, :], 0.0).then_inc(dve_done.sem, 1)
                ch = Chain(dve)
                dve.wait_ge(loaded.sem, 16 * n_loads)
                for m in range(2):
                    ins = dve.tensor_scalar(mbf[:, m, :], mraw[:, m, :], 0.0, MASKED, ALU.is_equal, ALU.mult)
                ins.then_inc(dve_done.sem, 1)
                ch.link(dve.tensor_copy(bsp[:, 0, :], braw[:, :]))
                ch.link(dve.tensor_tensor(bres[:, 0, :], braw[:, :], bsp[:, 0, :], ALU.subtract))
                ch.link(dve.tensor_copy(bsp[:, 1, :], bres[:, 0, :]))
                ch.link(dve.tensor_tensor(bres[:, 1, :], bres[:, 0, :], bsp[:, 1, :], ALU.subtract))
                dve.tensor_copy(bsp[:, 2, :], bres[:, 1, :]).then_inc(dve_done.sem, 1)

            @block.tensor
            def _(pe):
                pe.wait_ge(pool_done.sem, 9)
                pe.wait_ge(loaded.sem, 16 * n_loads)
                for i in range(6):
                    ins = pe.transpose(bank[i // 4][:, (i % 4) * P:(i % 4 + 1) * P], wraw[:, i, :], ident[:, :])
                for i in range(2):
                    ins = pe.transpose(bank[2][:, i * E:(i + 1) * E], rraw[:, i, :], ident[0:E, 0:E])
                ins.then_inc(pe_done.sem, 1)

            @block.scalar
            def _(act):
                act.wait_ge(pe_done.sem, 1)
                act.copy(flat(wsmall[:, 2:6, :]), bank[0][:, :])
                act.copy(flat(wsmall[:, 6:8, :]), bank[1][:, 0:2 * P])
                act.copy(flat(router[:, 0:2, :]), bank[2][:, 0:2 * E]).then_inc(act_done.sem, 1)
        loaded.value = 16 * n_loads
        pe_done.value, act_done.value, dve_done.value, pool_done.value = 1, 1, 4, 9
        bias_stored.value = 16 * (3 * (len(BIAS_PARTS) + 1) + 2)
        rows_loaded.value = 16

        R_B2 = {"L0": 0, "L3": E * P}
        R_SMALL = 2 * E * P
        R_ROUTER = R_SMALL + 4 * P

        def norm_scales(ch, dve, var, rstd, work):
            half, sq = work[:, 0, :], work[:, 1, :]
            bits = work[:, 2, :].bitcast(I32)
            ch.link(dve.tensor_scalar(sq, var, EPS, None, ALU.add))
            dve.tensor_scalar(half, sq, -0.5, None, ALU.mult)
            ch.link(dve.tensor_scalar(bits, sq.bitcast(I32), 1, None, ALU.logical_shift_right))
            ch.link(dve.tensor_scalar(rstd.bitcast(I32), bits, -1.0, RSQRT_SEED, ALU.mult, ALU.add))
            for _ in range(3):
                ch.link(dve.tensor_tensor(sq, rstd, rstd, ALU.mult))
                ch.link(dve.tensor_tensor(sq, sq, half, ALU.mult))
                ch.link(dve.scalar_tensor_tensor(rstd, sq, 1.5, rstd, ALU.add, ALU.mult))

        def layer_norm(ch, dve, src, dst, st, dst_free=None):
            for j in range(G):
                ins = dve.bn_stats(st["stats"][:, j, :], src(j))
            ch.link(ins)
            for j in range(G):
                ins = dve.bn_aggr(st["mv"][:, j, :], st["stats"][:, j, :])
            ch.link(ins)
            norm_scales(ch, dve, st["mv"][:, :, 1], st["rstd"][:, :], st["work"])
            if dst_free:
                dst_free()
            for j in range(G):
                ins = dve.tensor_scalar(dst(j), src(j), st["mv"][:, j, 0:1], st["rstd"][:, j:j + 1],
                                        ALU.subtract, ALU.mult)
            return ins


        def norm_tiles(ph, tag):
            return {"stats": sb_in(ph, f"stats_{tag}", [P, G, 6]), "mv": sb_in(ph, f"mean_var_{tag}", [P, G, 2]),
                    "rstd": sb_in(ph, f"rstd_{tag}", [P, G]), "work": sb_in(ph, f"newton_{tag}", [P, 3, G])}

        def combine(dve, ch, g, slots, j_src):
            for k in range(slots):
                for j in range(G):
                    t = g * G + j
                    xt = flat(X[:, bass.ds(t, 1), :])
                    ins = dve.scalar_tensor_tensor(xt, flat(j_src[k][:, bass.ds(t, 1), :]), WT[:, k, bass.ds(t, 1)], xt,
                                                   ALU.mult, ALU.add)
                ch.link(ins)

        TAIL_PE = ["turn_tail", "logits"]
        TAIL_ACT = ["tail_turned"]
        TAIL_DVE = ["tail_normed", "logits_kept"]

        def tail_tiles(ph):
            return {"turned": sb_in(ph, "tail_turned_sb", [P, G, P]), "rows": sb_in(ph, "tail_rows", [P, G, P]),
                    "mx": sb_in(ph, "tail_max", [P, G, E]), "ix": sb_in(ph, "tail_index", [P, G, E], U32),
                    "lg": sb_in(ph, "tail_logits", [P, G, E])}

        def tail_dve(dve, ch, g, D, PEs, st, tl):
            ins = layer_norm(ch, dve, lambda j: flat(X[:, bass.ds(g * G + j, 1), :]), lambda j: tl["rows"][:, j, :], st)
            ch.link(ins)
            dve.tensor_copy(flat(group(XN, g)), flat(tl["rows"][:, :, :])).then_inc(dve_done.sem, D.tick("tail_normed"))
            dve.wait_ge(pe_done.sem, PEs.at(g, "logits"))
            ch.link(dve.tensor_copy(flat(tl["lg"][:, :, :]), bank[7][:, 0:G * E]))
            for j in range(G):
                ins = dve.max(tl["mx"][:, j, :], tl["lg"][:, j, :])
            ch.link(ins)
            for j in range(G):
                ins = dve.max_index(tl["ix"][:, j, :], tl["mx"][:, j, :], tl["lg"][:, j, :])
            dve.tensor_copy(flat(group(MX, g)), flat(tl["mx"][:, :, :]))
            dve.tensor_copy(flat(group(LG, g)), flat(tl["lg"][:, :, :]))
            ch.link()
            dve.tensor_copy(flat(group(IX, g)), flat(tl["ix"][:, :, :])).then_inc(dve_done.sem, D.tick("logits_kept"))


        def tail_pe(pe, g, D, PEs, ACs, tl, layer):
            pe.wait_ge(dve_done.sem, D.at(g, "tail_normed"))
            for j in range(G):
                ins = pe.transpose(bank[6][:, j * P:(j + 1) * P], tl["rows"][:, j, :], ident[:, :])
            ins.then_inc(pe_done.sem, PEs.tick("turn_tail"))
            pe.wait_ge(act_done.sem, ACs.at(g, "tail_turned"))
            if layer == 1:
                for j in range(G):
                    pe.matmul(bank[7][:, j * E:(j + 1) * E], ones[0:3, :], rows3[:, R_ROUTER:R_ROUTER + E],
                              start=(j == 0), stop=False, skip_group_check=True)
            for j in range(G):
                ins = pe.matmul(bank[7][:, j * E:(j + 1) * E], tl["turned"][:, j, :], router[:, layer, :],
                                start=(layer != 1 and j == 0), stop=True, skip_group_check=True)
            ins.then_inc(pe_done.sem, PEs.tick("logits"))

        def tail_act(act, g, PEs, ACs, tl):
            act.wait_ge(pe_done.sem, PEs.at(g, "turn_tail"))
            act.copy(flat(tl["turned"][:, :, :]), bank[6][:, :]).then_inc(act_done.sem, ACs.tick("tail_turned"))

        def attention_0():
            with ExitStack() as ph:
                u = sb_in(ph, "u_rows", [P, G, P])
                uT = sb_in(ph, "u_turned", [P, G, P])
                keys = sb_in(ph, "keys", [P, 2, G * P])
                probs = sb_in(ph, "probs", [P, G, P])
                probsT = sb_in(ph, "probs_turned", [P, G, P])
                cg = sb_in(ph, "ctx_group", [P, G, P])
                mask = sb_in(ph, "mask_row", [1, B * P], BF16)
                sums = sb_in(ph, "sums", [P, 2, G])
                nmax = sb_in(ph, "neg_max", [P, 2, G])
                rinv = sb_in(ph, "rinv", [P, 2, G])
                st = norm_tiles(ph, "a0")
                tl = tail_tiles(ph)
                PEs = Steps(pe_done, ["turn_ctx", "keys"] + [f"{s}{h}" for h in range(2) for s in ("turn_u", "scores", "turn_p", "mixed")] + TAIL_PE)
                ACs = Steps(act_done, ["ctx_turned", "keys_kept"] + [f"{s}{h}" for h in range(2) for s in ("u_turned", "exp", "p_turned")] + TAIL_ACT)
                D = Steps(dve_done, ["u_normed", "max0", "u_new0", "max1"] + TAIL_DVE)
                PO = Steps(pool_done, ["ctx_copied"])
                mask_loaded = loaded.value + 16
                block = ph.enter_context(nc.Block())

                @block.sync
                def _(sp):
                    sp.dma_start(mask[:, :], mask_dram[0:1, :]).then_inc(loaded.sem, 16)

                @block.gpsimd
                def _(pool):
                    with pool.Fori(0, NG) as g:
                        pool.wait_ge(pe_done.sem, g * len(PEs.names) + PEs.base)
                        pool.tensor_copy(flat(cg[:, :, :]), flat(group(CT, g))).then_inc(pool_done.sem, PO.tick("ctx_copied"))

                @block.tensor
                def _(pe):
                    pe.wait_ge(loaded.sem, mask_loaded)
                    with pe.Fori(0, NG) as g:
                        pe.wait_ge(pool_done.sem, PO.at(g, "ctx_copied"))
                        for j in range(G):
                            ins = pe.transpose(bank[0][:, j * P:(j + 1) * P], cg[:, j, :], ident[:, :])
                        ins.then_inc(pe_done.sem, PEs.tick("turn_ctx"))
                        pe.wait_ge(act_done.sem, ACs.at(g, "ctx_turned"))
                        for h in range(2):
                            ins = pe.matmul(bank[1 + h][:, :], wsmall[:, h, :], flat(group(CTT, g)), start=True, stop=True)
                        ins.then_inc(pe_done.sem, PEs.tick("keys"))
                        for h in range(2):
                            pe.wait_ge(dve_done.sem, D.at(g, "u_normed" if h == 0 else "u_new0"))
                            for j in range(G):
                                ins = pe.transpose(bank[3][:, j * P:(j + 1) * P], u[:, j, :], ident[:, :])
                            ins.then_inc(pe_done.sem, PEs.tick(f"turn_u{h}"))
                            pe.matmul(bank[4][:, :], ones[0:1, :], mask[:, bass.ds(g * (G * P), G * P)], start=True, stop=False, skip_group_check=True)
                            pe.wait_ge(act_done.sem, ACs.at(g, "keys_kept"))
                            pe.wait_ge(act_done.sem, ACs.at(g, f"u_turned{h}"))
                            for j in range(G):
                                ins = pe.matmul(bank[4][:, j * P:(j + 1) * P], uT[:, j, :], keys[:, h, j * P:(j + 1) * P], start=False, stop=True, skip_group_check=True)
                            ins.then_inc(pe_done.sem, PEs.tick(f"scores{h}"))
                            pe.wait_ge(act_done.sem, ACs.at(g, f"exp{h}"))
                            for j in range(G):
                                ins = pe.transpose(bank[5][:, j * P:(j + 1) * P], probs[:, j, :], ident[:, :])
                            ins.then_inc(pe_done.sem, PEs.tick(f"turn_p{h}"))
                            pe.wait_ge(act_done.sem, ACs.at(g, f"p_turned{h}"))
                            for j in range(G):
                                ins = pe.matmul(bank[0][:, j * P:(j + 1) * P], probsT[:, j, :], flat(CT[:, bass.ds(g * G + j, 1), :]), start=True, stop=True)
                            ins.then_inc(pe_done.sem, PEs.tick(f"mixed{h}"))
                        tail_pe(pe, g, D, PEs, ACs, tl, 0)

                @block.scalar
                def _(act):
                    with act.Fori(0, NG) as g:
                        act.wait_ge(pe_done.sem, PEs.at(g, "turn_ctx"))
                        act.copy(flat(group(CTT, g)), bank[0][:, :]).then_inc(act_done.sem, ACs.tick("ctx_turned"))
                        act.wait_ge(pe_done.sem, PEs.at(g, "keys"))
                        act.copy(keys[:, 0, :], bank[1][:, :])
                        act.copy(keys[:, 1, :], bank[2][:, :]).then_inc(act_done.sem, ACs.tick("keys_kept"))
                        for h in range(2):
                            act.wait_ge(pe_done.sem, PEs.at(g, f"turn_u{h}"))
                            act.copy(flat(uT[:, :, :]), bank[3][:, :]).then_inc(act_done.sem, ACs.tick(f"u_turned{h}"))
                            act.wait_ge(dve_done.sem, D.at(g, f"max{h}"))
                            for j in range(G):
                                ins = act.activation(probs[:, j, :], bank[4][:, j * P:(j + 1) * P], ACT.Exp, bias=nmax[:, h, j:j + 1], accum_out=sums[:, h, j:j + 1])
                            ins.then_inc(act_done.sem, ACs.tick(f"exp{h}"))
                            act.wait_ge(pe_done.sem, PEs.at(g, f"turn_p{h}"))
                            act.copy(flat(probsT[:, :, :]), bank[5][:, :]).then_inc(act_done.sem, ACs.tick(f"p_turned{h}"))
                        tail_act(act, g, PEs, ACs, tl)

                @block.vector
                def _(dve):
                    with dve.Fori(0, NG) as g:
                        ch = Chain(dve)
                        layer_norm(ch, dve, lambda j: flat(X[:, bass.ds(g * G + j, 1), :]), lambda j: u[:, j, :], st).then_inc(dve_done.sem, D.tick("u_normed"))
                        for h in range(2):
                            dve.wait_ge(pe_done.sem, PEs.at(g, f"scores{h}"))
                            dve.tensor_reduce(nmax[:, h, :], bank[4][:, :].rearrange("p (j l) -> p j l", j=G), AX.X, ALU.max, negate=True).then_inc(dve_done.sem, D.tick(f"max{h}"))
                            dve.wait_ge(act_done.sem, ACs.at(g, f"exp{h}"))
                            ch.link(dve.reciprocal(rinv[:, h, :], sums[:, h, :]))
                            dve.wait_ge(pe_done.sem, PEs.at(g, f"mixed{h}"))
                            for j in range(G):
                                ins = dve.scalar_tensor_tensor(u[:, j, :], bank[0][:, j * P:(j + 1) * P], rinv[:, h, j:j + 1], u[:, j, :], ALU.mult, ALU.add)
                            if h == 0:
                                ins.then_inc(dve_done.sem, D.tick("u_new0"))
                            else:
                                ch.link(ins)
                        ins = dve.tensor_tensor(flat(group(X, g)), flat(group(X, g)), flat(u[:, :, :]), ALU.add)
                        ch.link(ins)
                        tail_dve(dve, ch, g, D, PEs, st, tl)
                for s in (PEs, ACs, D, PO):
                    s.close(NG)
                loaded.value += 16

        attention_0()

        def route(layer, top, capacity):
            n_tiles = {0: TILES_TOP2, 1: TILES_CAP, 2: TILES_TOP2, 3: TILES_TOP1}[layer]
            with ExitStack() as ph:
                oh = sb_in(ph, "one_hot", [P, 2, B, E])
                ohb = sb_in(ph, "one_hot_bf", [P, B, E], BF16)
                tot = sb_in(ph, "totals", [P, B, E])
                run = sb_in(ph, "running", [P, B, E])
                pos = sb_in(ph, "positions", [P, B, E])
                tmp = sb_in(ph, "picked", [P, B, E])
                zeros = sb_in(ph, "zeros", [P, B])
                posf = sb_in(ph, "slot_f", [P, 2, B])
                keep = sb_in(ph, "kept", [P, 2, B])
                small = sb_in(ph, "tile_counts", [P, 4, E])
                cnt_i = sb_in(ph, "count_bits", [P, E], I32)
                expo = sb_in(ph, "exp_logits", [P, B, E])
                tcmp = sb_in(ph, "tile_compare", [1, TILES_TOP2, E])
                tsum = sb_in(ph, "tile_sum", [1, TILES_TOP2])
                block = ph.enter_context(nc.Block())
                dv, pv, av = dve_done.value, pe_done.value, act_done.value

                @block.vector
                def _(dve):
                    ch = Chain(dve)
                    dve.memset(zeros[:, :], 0.0)
                    for k in range(top):
                        dve.tensor_tensor(oh[:, k, :, :], IX[:, :, k:k + 1].to_broadcast([P, B, E]),
                                          iota8[:, :].unsqueeze(1).to_broadcast([P, B, E]), ALU.is_equal)
                    ch.link()
                    if top == 2:
                        dve.tensor_tensor(ohb[:, :, :], oh[:, 0, :, :], oh[:, 1, :, :], ALU.add).then_inc(dve_done.sem, 1)
                        dve.tensor_tensor(expo[:, :, 0], MX[:, :, 1], MX[:, :, 0], ALU.subtract).then_inc(dve_done.sem, 1)
                    else:
                        dve.tensor_copy(ohb[:, :, :], oh[:, 0, :, :]).then_inc(dve_done.sem, 1)
                        dve.tensor_tensor(expo[:, :, :], LG[:, :, :], MX[:, :, 0:1].to_broadcast([P, B, E]), ALU.subtract).then_inc(dve_done.sem, 1)
                    dve.wait_ge(pe_done.sem, pv + 1)
                    ch.link(dve.tensor_copy(tot[:, :, :].rearrange("p b e -> p (b e)"), bank[1][:, 0:B * E]))
                    for e in range(E):
                        dve.tensor_tensor_scan(run[:, :, e], tot[:, :, e], zeros[:, :], 0.0, ALU.add, ALU.add)
                    ch.link()
                    ch.link(dve.tensor_tensor(pos[:, :, :], run[:, :, :], tot[:, :, :], ALU.subtract))
                    ch.link(dve.tensor_tensor(pos[:, :, :], pos[:, :, :], bank[0][:, 0:B * E].rearrange("p (b e) -> p b e", e=E), ALU.add))
                    if capacity:
                        for k in range(top):
                            ch.link(dve.scalar_tensor_tensor(tmp[:, :, :], pos[:, :, :], float(capacity), oh[:, k, :, :], ALU.is_lt, ALU.mult))
                            ch.link(dve.tensor_reduce(keep[:, k, :], tmp[:, :, :], AX.X, ALU.add))
                        ch.link(dve.tensor_scalar(small[:, 3, :], iota8[:, :], float(capacity), None, ALU.mult))
                    else:
                        ch.link(dve.tensor_scalar(cnt_i[:, :], run[:, B - 1, :], float(P - 1), None, ALU.add))
                        ch.link(dve.tensor_scalar(cnt_i[:, :], cnt_i[:, :], 7, None, ALU.arith_shift_right))
                        ch.link(dve.tensor_copy(small[:, 0, :], cnt_i[:, :]))
                        ch.link(dve.tensor_tensor_scan(small[:, 1, :], small[:, 0, :], zeros[:, 0:E], 0.0, ALU.add, ALU.add))
                        ch.link(dve.tensor_tensor(small[:, 2, :], small[:, 1, :], small[:, 0, :], ALU.subtract))
                        ch.link(dve.tensor_scalar(small[:, 3, :], small[:, 2, :], float(P), None, ALU.mult))
                    ch.link(dve.tensor_tensor(pos[:, :, :], pos[:, :, :], small[:, 3, :].unsqueeze(1).to_broadcast([P, B, E]), ALU.add))
                    for k in range(top):
                        ch.link(dve.tensor_tensor(tmp[:, :, :], oh[:, k, :, :], pos[:, :, :], ALU.mult))
                        ch.link(dve.tensor_reduce(posf[:, k, :], tmp[:, :, :], AX.X, ALU.add))
                    if capacity:
                        ch.link(dve.tensor_tensor(posf[:, :, :], posf[:, :, :], keep[:, :, :], ALU.mult))
                        dve.tensor_copy(POS[:, :, :], posf[:, :, :])
                        ch.link(dve.tensor_scalar(tmp[:, 0:2 * B // E, :].rearrange("p a e -> p (a e)"), keep[:, :, :].rearrange("p a b -> p (a b)"), -FAR, FAR, ALU.mult, ALU.add))
                        dve.tensor_tensor(SCT[:, :, :].rearrange("p a b -> p (a b)"), posf[:, :, :].rearrange("p a b -> p (a b)"), tmp[:, 0:2 * B // E, :].rearrange("p a e -> p (a e)"), ALU.add).then_inc(dve_done.sem, 1)
                    else:
                        dve.tensor_copy(POS[:, 0:top, :], posf[:, 0:top, :]).then_inc(dve_done.sem, 1)
                        ch.link(dve.tensor_tensor(tcmp[:, 0:n_tiles, :], iota_tile[:, 0:n_tiles].unsqueeze(2).to_broadcast([1, n_tiles, E]),
                                                  small[0:1, 1, :].unsqueeze(1).to_broadcast([1, n_tiles, E]), ALU.is_ge))
                        ch.link(dve.tensor_reduce(tsum[:, 0:n_tiles], tcmp[:, 0:n_tiles, :], AX.X, ALU.add))
                        dve.tensor_scalar(tile_expert[:, 0:n_tiles], tsum[:, 0:n_tiles], float(E - 1), None, ALU.min)
                    dve.wait_ge(act_done.sem, av + 1)
                    ch.link()
                    if top == 2:
                        ch.link(dve.tensor_scalar(tmp[:, :, 0], expo[:, :, 1], 1.0, None, ALU.add))
                        ch.link(dve.reciprocal(WT[:, 0, :], tmp[:, :, 0]))
                        ch.link(dve.tensor_tensor(WT[:, 1, :], WT[:, 0, :], expo[:, :, 1], ALU.mult))
                        if capacity:
                            dve.tensor_tensor(WT[:, :, :], WT[:, :, :], keep[:, :, :], ALU.mult)
                    else:
                        ch.link(dve.tensor_reduce(tmp[:, :, 0], expo[:, :, :], AX.X, ALU.add))
                        dve.reciprocal(WT[:, 0, :], tmp[:, :, 0])

                @block.scalar
                def _(act):
                    act.wait_ge(dve_done.sem, dv + 2)
                    if top == 2:
                        act.activation(expo[:, :, 1], expo[:, :, 0], ACT.Exp).then_inc(act_done.sem, 1)
                    else:
                        act.activation(expo[:, :, :], expo[:, :, :], ACT.Exp).then_inc(act_done.sem, 1)
                    if layer == 0:
                        for i in range(16):
                            act.wait_ge(pe_done.sem, pv + 2 + i)
                            dst = SETA1 if i < 8 else SETA2
                            act.copy(dst[:, (i % 8) * 512:(i % 8 + 1) * 512], bank[2 + i % 6][:, :]).then_inc(act_done.sem, 1)

                @block.tensor
                def _(pe):
                    pe.wait_ge(dve_done.sem, dv + 1)
                    pe.matmul(bank[0][:, 0:B * E], tri[:, :], ohb[:, :, :].rearrange("p b e -> p (b e)"), start=True, stop=True)
                    pe.matmul(bank[1][:, 0:B * E], ones[:, :], ohb[:, :, :].rearrange("p b e -> p (b e)"), start=True, stop=True).then_inc(pe_done.sem, 1)
                    if layer == 0:
                        for i in range(16):
                            if i >= 6:
                                pe.wait_ge(act_done.sem, av + 2 + i - 6)
                            raw = SETB1 if i < 8 else SETB2
                            for j in range(4):
                                c = (i % 8) * 4 + j
                                ins = pe.transpose(bank[2 + i % 6][:, j * P:(j + 1) * P], raw[:, c * P:(c + 1) * P], ident[:, :])
                            ins.then_inc(pe_done.sem, 1)

                @block.gpsimd
                def _(pool):
                    pool.wait_ge(dve_done.sem, dv + 3)
                    idx = SCT if capacity else POS
                    bound = dict(bounds_check=TILES_CAP * P - 1, oob_is_err=False) if capacity else {}
                    for t in range(B):
                        for k in range(top):
                            pool.indirect_dma_start(xs, bass.IndirectOffsetOnAxis(ap=idx[:, k, t:t + 1], axis=0), XN[:, t, :], None,
                                                    **bound).then_inc(scattered.sem, 16)
                    pool.wait_ge(scattered.sem, scattered.value + 16 * B * top)
            dve_done.value += 3
            pe_done.value += 1 + (16 if layer == 0 else 0)
            act_done.value += 1 + (16 if layer == 0 else 0)
            scattered.value += 16 * B * top

        def experts(layer):
            n_tiles = {0: TILES_TOP2, 1: TILES_CAP, 2: TILES_TOP2, 3: TILES_TOP1}[layer]
            W1, W2 = (SETA1, SETA2) if layer in (0, 2) else (SETB1, SETB2)
            gated = layer in (1, 2)
            NC = 2 if gated else 4
            UNROLL = 4
            with ExitStack() as ph:
                xr = sb_in(ph, "tile_rows", [P, 4, P])
                xt = sb_in(ph, "tile_turned", [P, 2, P])
                hid = sb_in(ph, "hidden", [P, 2, NC * P])
                gat = sb_in(ph, "gate", [P, 2, 256])
                hidT = sb_in(ph, "hidden_turned_sb", [P, 2, NC * P])
                yo = sb_in(ph, "expert_rows_sb", [P, 4, P])
                b1 = sb_in(ph, "expert_b1", [3, E * H1], BF16)
                b1_here = rows_loaded.value + 16
                block = ph.enter_context(nc.Block())

                def tile_of(rows, j):
                    return rows.rearrange("(t p) d -> t p d", p=P)[bass.ds(j, 1), :, :].rearrange("a p d -> (a p) d")

                def run(eng, step):
                    for k in range(-2, 2):
                        step(k, k % UNROLL)
                    with eng.Fori(0, (n_tiles - 4) // UNROLL) as q:
                        for u in range(UNROLL):
                            step(q * UNROLL + (2 + u), (2 + u) % UNROLL)
                    for k in range(n_tiles - 2, n_tiles + 1):
                        step(k, k % UNROLL)

                def exists(j):
                    return not isinstance(j, int) or 0 <= j < n_tiles

                def beyond(j, n):
                    return not isinstance(j, int) or j >= n

                @block.sync
                def _(sp):
                    if not gated:
                        at, width = BIAS_AT[f"L{layer}_ffn_b1"]
                        sp.dma_start(b1[:, :], bias_dram[:, at:at + width]).then_inc(rows_loaded.sem, 16)

                    if layer in (0, 2):
                        load_expert_weights(sp, layer + 1)

                    def load(j, s):
                        sp.dma_start(xr[:, s, :], tile_of(xs, j)).then_inc(sorted_in[s].sem, 16)
                    for j in range(4):
                        load(j, j)
                    with sp.Fori(1, n_tiles // 4) as q:
                        for s in range(4):
                            sp.wait_ge(rows_turned.sem, q * 4 + (s + rows_turned.value - 3))
                            load(q * 4 + s, s)

                @block.tensor
                def _(pe):
                    if not gated:
                        pe.wait_ge(rows_loaded.sem, b1_here)
                    if layer:
                        done = weights_a if layer == 2 else weights_b
                        pe.wait_ge(done.sem, done.value)

                    def turn_rows(j, u):
                        if exists(j):
                            if isinstance(j, int):
                                pe.wait_ge(sorted_in[u].sem, sorted_in[u].value + 16 * (j // 4 + 1))
                            else:
                                pe.wait_ge(sorted_in[u].sem, (j - u) * 4 + (sorted_in[u].value + 16))
                            if beyond(j, 2):
                                pe.wait_ge(rows_turned_kept.sem, j + (rows_turned_kept.value - 1))
                            pe.transpose(bank[u % 2][:, 0:P], xr[:, u, :], ident[:, :]).then_inc(rows_turned.sem, 1)

                    def expert_of(j):
                        if layer == 1:
                            return None
                        return pe.value_load(tile_expert[0:1, bass.ds(j, 1)], min_val=0, max_val=E - 1)

                    def hidden(j, u):
                        if exists(j):
                            e = expert_of(j)
                            if layer == 1:
                                off = (j // 2) * H1 if isinstance(j, int) else (j - u % 2) * (H1 // 2)
                            else:
                                off = e * H1
                            pe.wait_ge(rows_turned_kept.sem, j + (rows_turned_kept.value + 1))
                            if beyond(j, 2):
                                pe.wait_ge(hidden_kept.sem, j + (hidden_kept.value - 1))
                            out_ = bank[2 + u % 2]
                            ins = pe.matmul(out_[:, :], xt[:, u % 2, :], W1[:, bass.ds(off, H1)], start=True, stop=gated)
                            if not gated:
                                ins = pe.matmul(out_[:, :], ones[0:3, :], b1[:, bass.ds(off, H1)], start=False, stop=True)
                            ins.then_inc(hidden_made.sem, 1)

                    def turn_hidden(j, u):
                        if exists(j):
                            pe.wait_ge(hidden_kept.sem, j + (hidden_kept.value + 1))
                            if beyond(j, 2):
                                pe.wait_ge(hidden_turned_kept.sem, j + (hidden_turned_kept.value - 1))
                            for c in range(NC):
                                ins = pe.transpose(bank[4 + u % 2][:, c * P:(c + 1) * P], hid[:, u % 2, c * P:(c + 1) * P], ident[:, :])
                            ins.then_inc(hidden_turned.sem, 1)

                    def rows_out(j, u):
                        if exists(j):
                            e = expert_of(j)
                            if layer == 1:
                                off = (j // 2) * NC * P if isinstance(j, int) else (j - u % 2) * (NC * P // 2)
                            else:
                                off = e * (NC * P)
                            pe.wait_ge(hidden_turned_kept.sem, j + (hidden_turned_kept.value + 1))
                            if beyond(j, 2):
                                pe.wait_ge(expert_kept.sem, j + (expert_kept.value - 1))
                            out_ = bank[6 + u % 2]
                            for c in range(NC):
                                ins = pe.matmul(out_[:, 0:P], hidT[:, u % 2, c * P:(c + 1) * P], W2[:, bass.ds(off + c * P, P)],
                                                start=(c == 0), stop=(gated and c == NC - 1))
                            if not gated:
                                ins = pe.matmul(out_[:, 0:P], ones[0:3, :], rows3[:, bass.ds(e * P + R_B2[f"L{layer}"], P)], start=False, stop=True)
                            ins.then_inc(expert_made.sem, 1)

                    def step(k, u):
                        turn_rows(k + 2, (u + 2) % 4)
                        hidden(k + 1, (u + 1) % 4)
                        turn_hidden(k, u)
                        rows_out(k - 1, (u + 3) % 4)
                    run(pe, step)

                @block.scalar
                def _(act):
                    def store(j, s):
                        if exists(j):
                            act.wait_ge(expert_kept.sem, j + (expert_kept.value + 1))
                            act.dma_start(tile_of(ys, j), yo[:, s, :]).then_inc(expert_out[s].sem, 16)

                    def step(k, u):
                        store(k - 2, (u + 2) % 4)
                        j, s = k + 1, (u + 1) % 2
                        if exists(j):
                            act.wait_ge(hidden_made.sem, j + (hidden_made.value + 1))
                            if beyond(j, 2):
                                if gated:
                                    act.wait_ge(hidden_kept.sem, j + (hidden_kept.value - 1))
                                else:
                                    act.wait_ge(hidden_turned.sem, j + (hidden_turned.value - 1))
                            if gated:
                                half = 256 if layer == 1 else 0
                                act.activation(gat[:, s, :], bank[2 + s][:, half:half + 256], ACT.Silu).then_inc(gates_kept.sem, 1)
                            else:
                                act.activation(hid[:, s, :], bank[2 + s][:, :], ACT.Gelu).then_inc(hidden_kept.sem, 1)
                    run(act, step)
                    store(n_tiles - 1, 3)
                    for s in range(4):
                        act.wait_ge(expert_out[s].sem, expert_out[s].value + 16 * (n_tiles // 4))

                @block.vector
                def _(dve):
                    def step(k, u):
                        j, s = k + 2, u % 2
                        if exists(j):
                            dve.wait_ge(rows_turned.sem, j + (rows_turned.value + 1))
                            if beyond(j, 2):
                                dve.wait_ge(hidden_made.sem, j + (hidden_made.value - 1))
                            dve.tensor_copy(xt[:, s, :], bank[s][:, 0:P]).then_inc(rows_turned_kept.sem, 1)
                        j, s = k + 1, (u + 1) % 2
                        if gated and exists(j):
                            dve.wait_ge(gates_kept.sem, j + (gates_kept.value + 1))
                            if beyond(j, 2):
                                dve.wait_ge(hidden_turned.sem, j + (hidden_turned.value - 1))
                            half = 0 if layer == 1 else 256
                            dve.tensor_tensor(hid[:, s, :], bank[2 + s][:, half:half + 256], gat[:, s, :], ALU.mult).then_inc(hidden_kept.sem, 1)
                        j, s = k, u % 2
                        if exists(j):
                            dve.wait_ge(hidden_turned.sem, j + (hidden_turned.value + 1))
                            if beyond(j, 2):
                                dve.wait_ge(expert_made.sem, j + (expert_made.value - 1))
                            dve.tensor_copy(hidT[:, s, :], bank[4 + s][:, 0:NC * P]).then_inc(hidden_turned_kept.sem, 1)
                        j, s = k - 1, (u + 3) % 4
                        if exists(j):
                            dve.wait_ge(expert_made.sem, j + (expert_made.value + 1))
                            if isinstance(j, int):
                                if j >= 4:
                                    dve.wait_ge(expert_out[s].sem, expert_out[s].value + 16 * (j // 4))
                            else:
                                dve.wait_ge(expert_out[s].sem, (j - s) * 4 + expert_out[s].value)
                            dve.tensor_copy(yo[:, s, :], bank[6 + s % 2][:, 0:P]).then_inc(expert_kept.sem, 1)
                    run(dve, step)

            for c in (rows_turned, hidden_made, hidden_turned, expert_made, rows_turned_kept, hidden_kept, hidden_turned_kept, expert_kept):
                c.value += n_tiles
            if gated:
                gates_kept.value += n_tiles
            else:
                rows_loaded.value += 16
            for s in range(4):
                sorted_in[s].value += 16 * (n_tiles // 4)
                expert_out[s].value += 16 * (n_tiles // 4)

        def gather_group(pool, g, top):
            for t in range(g * G, (g + 1) * G):
                for k in range(top):
                    dst = (XN, Y1)[k]
                    pool.indirect_dma_start(dst[:, t, :], None, ys, bass.IndirectOffsetOnAxis(ap=POS[:, k, t:t + 1], axis=0)).then_inc(gathered[g % 2].sem, 16)

        def group_is_here(pool, g, top):
            pool.wait_ge(gathered[g % 2].sem, gathered[g % 2].value + 16 * G * top * (g // 2 + 1))
            pool.sem_inc(rows_here.sem, 1)

        def close_gathers(top):
            for c in gathered:
                c.value += 16 * G * top * NG // 2
            rows_here.value += NG

        def load_expert_weights(sp, layer):
            W1, W2 = (SETA1, SETA2) if layer in (0, 2) else (SETB1, SETB2)
            done = weights_a if layer in (0, 2) else weights_b
            w1v = W1[:, :].rearrange("p (e f) -> p e f", e=E)
            if layer == 1:
                srcs = [(w1v[:, :, 0:256], A["L1_ffn_W"].rearrange("e d f -> d e f")),
                        (w1v[:, :, 256:512], A["L1_ffn_V"].rearrange("e d f -> d e f")),
                        (W2[:, 0:E * 256].rearrange("p (c d) -> p c d", d=P), A["L1_ffn_W_out"].rearrange("e (c p) d -> p (e c) d", p=P))]
            elif layer == 2:
                srcs = [(w1v, A["L2_ffn_gate_up_w"].rearrange("e d f -> d e f")),
                        (W2[:, 0:E * 256].rearrange("p (c d) -> p c d", d=P), A["L2_ffn_down_w"].rearrange("e (c p) d -> p (e c) d", p=P))]
            else:
                srcs = [(w1v, A["L3_ffn_w1"].rearrange("e d f -> d e f")),
                        (W2[:, :].rearrange("p (c d) -> p c d", d=P), A["L3_ffn_w2"].rearrange("e (c p) d -> p (e c) d", p=P))]
            for dst, src in srcs:
                sp.dma_start(dst, src).then_inc(done.sem, 16)
            done.value += 16 * len(srcs)

        def combine_only(top):
            with nc.Block() as block:
                @block.gpsimd
                def _(pool):
                    for g in range(NG + 1):
                        if g < NG:
                            gather_group(pool, g, top)
                        if g >= 1:
                            group_is_here(pool, g - 1, top)

                @block.vector
                def _(dve):
                    ch = Chain(dve)
                    with dve.Fori(0, NG) as g:
                        dve.wait_ge(rows_here.sem, g + (rows_here.value + 1))
                        combine(dve, ch, g, top, (XN, Y1))
            close_gathers(top)

        route(0, 2, 0)
        experts(0)

        def attention_1(top_before):
            with ExitStack() as ph:
                VX = P + 16
                u = sb_in(ph, "u_rows1", [P, G, P])
                uT = sb_in(ph, "u_turned1", [P, G, P])
                cT = sb_in(ph, "ctx_turned_group", [P, G, P])
                q = sb_in(ph, "q_soft", [P, G * P])
                k = sb_in(ph, "k_soft", [P, G * P])
                vx = sb_in(ph, "values_ones", [P, G, VX])
                kvm = sb_in(ph, "kv_masked", [P, G, VX])
                qT = sb_in(ph, "q_turned", [P, G * P])
                o = sb_in(ph, "attended", [P, G, P])
                oT = sb_in(ph, "attended_turned", [P, G * P])
                red = sb_in(ph, "head_sums", [P, 4, G * 16])
                dinv = sb_in(ph, "d_inv", [P, G, 16])
                st = norm_tiles(ph, "a1")
                tl = tail_tiles(ph)
                PEs = Steps(pe_done, ["k", "v", "turn_u", "q", "turn_q", "kv", "out", "turn_o", "proj"] + TAIL_PE)
                ACs = Steps(act_done, ["k_exp", "v_kept", "u_turned", "q_exp", "q_turned", "o_turned"] + TAIL_ACT)
                D = Steps(dve_done, ["k_less", "k_soft", "u_normed", "q_less", "q_soft", "kv_masked", "o"] + TAIL_DVE)
                PO = Steps(pool_done, ["ctx_copied"])
                block = ph.enter_context(nc.Block())

                @block.sync
                def _(sp):
                    load_expert_weights(sp, 2)

                @block.gpsimd
                def _(pool):
                    for g in range(NG + 1):
                        if g < NG:
                            gather_group(pool, g, top_before)
                            if g:
                                pool.wait_ge(pe_done.sem, PEs.at(g - 1, "v"))
                            pool.tensor_copy(flat(cT[:, :, :]), flat(CTT[:, g * G:(g + 1) * G, :])).then_inc(pool_done.sem, 1)
                        if g >= 1:
                            group_is_here(pool, g - 1, top_before)
                    PO.seen += 1

                def soft_heads(dve, ch, src, dst, w, less, soft, act_step, g):
                    heads = lambda ap: ap.rearrange("p (h c) -> p h c", c=8)
                    wide = lambda ap: ap.unsqueeze(2).to_broadcast([P, G * 16, 8])
                    ch.link(dve.tensor_reduce(red[:, w, :], heads(src), AX.X, ALU.max))
                    dve.tensor_tensor(heads(dst), heads(src), wide(red[:, w, :]), ALU.subtract).then_inc(dve_done.sem, D.tick(less))
                    dve.wait_ge(act_done.sem, ACs.at(g, act_step))
                    ch.link(dve.tensor_reduce(red[:, w + 1, :], heads(dst), AX.X, ALU.add))
                    ch.link(dve.reciprocal(red[:, w + 1, :], red[:, w + 1, :]))
                    dve.tensor_tensor(heads(dst), heads(dst), wide(red[:, w + 1, :]), ALU.mult).then_inc(dve_done.sem, D.tick(soft))

                @block.vector
                def _(dve):
                    ch = Chain(dve)
                    dve.memset(vx[:, :, P:VX], 1.0)
                    with dve.Fori(0, NG) as g:
                        dve.wait_ge(pe_done.sem, PEs.at(g, "k"))
                        soft_heads(dve, ch, bank[0][:, :], k[:, :], 0, "k_less", "k_soft", "k_exp", g)
                        dve.wait_ge(rows_here.sem, g + (rows_here.value + 1))
                        combine(dve, ch, g, top_before, (XN, Y1))
                        layer_norm(ch, dve, lambda j: flat(X[:, bass.ds(g * G + j, 1), :]), lambda j: u[:, j, :], st).then_inc(dve_done.sem, D.tick("u_normed"))
                        dve.wait_ge(pe_done.sem, PEs.at(g, "q"))
                        soft_heads(dve, ch, bank[3][:, :], q[:, :], 2, "q_less", "q_soft", "q_exp", g)
                        dve.wait_ge(pe_done.sem, PEs.at(g, "kv"))
                        for half in range(2):
                            ins = dve.tensor_tensor(kvm[:, 2 * half:2 * half + 2, :], bank[4 + half][:, 0:2 * VX].rearrange("p (j c) -> p j c", c=VX),
                                                    blocks[:, :].unsqueeze(1).to_broadcast([P, 2, VX]), ALU.mult)
                        ins.then_inc(dve_done.sem, D.tick("kv_masked"))
                        dve.wait_ge(pe_done.sem, PEs.at(g, "out"))
                        for half in range(2):
                            dve.reciprocal(dinv[:, 2 * half:2 * half + 2, :], bank[4 + half][:, 0:2 * VX].rearrange("p (j c) -> p j c", c=VX)[:, :, P:VX])
                        ch.link()
                        for j in range(G):
                            at = (j % 2) * VX
                            dve.tensor_tensor(o[:, j, :].rearrange("p (h c) -> p h c", c=8), bank[4 + j // 2][:, at:at + P].rearrange("p (h c) -> p h c", c=8),
                                              dinv[:, j, :].unsqueeze(2).to_broadcast([P, 16, 8]), ALU.mult)
                        ch.link()
                        dve.tensor_tensor(flat(o[:, :, :]), flat(o[:, :, :]), q[:, :], ALU.add).then_inc(dve_done.sem, D.tick("o"))
                        dve.wait_ge(pe_done.sem, PEs.at(g, "proj"))
                        ch.link(dve.tensor_tensor(flat(group(X, g)), flat(group(X, g)), bank[7][:, :], ALU.add))
                        tail_dve(dve, ch, g, D, PEs, st, tl)

                @block.scalar
                def _(act):
                    with act.Fori(0, NG) as g:
                        act.wait_ge(dve_done.sem, D.at(g, "k_less"))
                        act.activation(k[:, :], k[:, :], ACT.Exp).then_inc(act_done.sem, ACs.tick("k_exp"))
                        act.wait_ge(pe_done.sem, PEs.at(g, "v"))
                        act.copy(vx[:, :, 0:P], bank[1][:, :].rearrange("p (j c) -> p j c", c=P)).then_inc(act_done.sem, ACs.tick("v_kept"))
                        act.wait_ge(pe_done.sem, PEs.at(g, "turn_u"))
                        act.copy(flat(uT[:, :, :]), bank[2][:, :]).then_inc(act_done.sem, ACs.tick("u_turned"))
                        act.wait_ge(dve_done.sem, D.at(g, "q_less"))
                        act.activation(q[:, :], q[:, :], ACT.Exp).then_inc(act_done.sem, ACs.tick("q_exp"))
                        act.wait_ge(pe_done.sem, PEs.at(g, "turn_q"))
                        act.copy(qT[:, :], bank[2][:, :]).then_inc(act_done.sem, ACs.tick("q_turned"))
                        act.wait_ge(pe_done.sem, PEs.at(g, "turn_o"))
                        act.copy(oT[:, :], bank[2][:, :]).then_inc(act_done.sem, ACs.tick("o_turned"))
                        tail_act(act, g, PEs, ACs, tl)

                @block.tensor
                def _(pe):
                    def biased(out_, which, lhs, w):
                        for j in range(G):
                            pe.matmul(out_[:, j * P:(j + 1) * P], ones[0:3, :], rows3[:, R_SMALL + which * P:R_SMALL + (which + 1) * P],
                                      start=(j == 0), stop=False, skip_group_check=True)
                        for j in range(G):
                            ins = pe.matmul(out_[:, j * P:(j + 1) * P], lhs(j), w, start=False, stop=True, skip_group_check=True)
                        return ins

                    def turn(src):
                        for j in range(G):
                            ins = pe.transpose(bank[2][:, j * P:(j + 1) * P], src(j), ident[:, :])
                        return ins
                    with pe.Fori(0, NG) as g:
                        pe.wait_ge(pool_done.sem, PO.at(g, "ctx_copied"))
                        biased(bank[0], 1, lambda j: cT[:, j, :], wsmall[:, 3, :]).then_inc(pe_done.sem, PEs.tick("k"))
                        biased(bank[1], 2, lambda j: cT[:, j, :], wsmall[:, 4, :]).then_inc(pe_done.sem, PEs.tick("v"))
                        pe.wait_ge(dve_done.sem, D.at(g, "u_normed"))
                        turn(lambda j: u[:, j, :]).then_inc(pe_done.sem, PEs.tick("turn_u"))
                        pe.wait_ge(act_done.sem, ACs.at(g, "u_turned"))
                        biased(bank[3], 0, lambda j: uT[:, j, :], wsmall[:, 2, :]).then_inc(pe_done.sem, PEs.tick("q"))
                        pe.wait_ge(dve_done.sem, D.at(g, "q_soft"))
                        turn(lambda j: q[:, j * P:(j + 1) * P]).then_inc(pe_done.sem, PEs.tick("turn_q"))
                        pe.wait_ge(act_done.sem, ACs.at(g, "v_kept"))
                        for j in range(G):
                            at = (j % 2) * VX
                            ins = pe.matmul(bank[4 + j // 2][:, at:at + VX], k[:, j * P:(j + 1) * P], vx[:, j, :], start=True, stop=True)
                        ins.then_inc(pe_done.sem, PEs.tick("kv"))
                        pe.wait_ge(dve_done.sem, D.at(g, "kv_masked"))
                        pe.wait_ge(act_done.sem, ACs.at(g, "q_turned"))
                        for j in range(G):
                            at = (j % 2) * VX
                            ins = pe.matmul(bank[4 + j // 2][:, at:at + VX], qT[:, j * P:(j + 1) * P], kvm[:, j, :], start=True, stop=True)
                        ins.then_inc(pe_done.sem, PEs.tick("out"))
                        pe.wait_ge(dve_done.sem, D.at(g, "o"))
                        turn(lambda j: o[:, j, :]).then_inc(pe_done.sem, PEs.tick("turn_o"))
                        pe.wait_ge(act_done.sem, ACs.at(g, "o_turned"))
                        biased(bank[7], 3, lambda j: oT[:, j * P:(j + 1) * P], wsmall[:, 5, :]).then_inc(pe_done.sem, PEs.tick("proj"))
                        tail_pe(pe, g, D, PEs, ACs, tl, 1)
                for c in (PEs, ACs, D, PO):
                    c.close(NG)
                close_gathers(top_before)


        HEADS, HD = 16, 64
        INNER = HEADS * HD
        LT = SETB1[:, :].rearrange("p (b d) -> p b d", d=P)
        CNT = SETB2[:, :].rearrange("p (b d) -> p b d", d=P)

        def attention_2_norms(top_before):
            with ExitStack() as ph:
                u = sb_in(ph, "u_rows2", [P, G, P])
                l = sb_in(ph, "latent_rows", [P, G, P])
                c = sb_in(ph, "ctx_normed", [P, G, P])
                st = norm_tiles(ph, "a2")
                PEs = Steps(pe_done, ["turn_c", "turn_l"])
                ACs = Steps(act_done, ["c_kept", "l_kept"])
                D = Steps(dve_done, ["c", "l"])
                block = ph.enter_context(nc.Block())

                @block.gpsimd
                def _(pool):
                    for g in range(NG + 1):
                        if g < NG:
                            gather_group(pool, g, top_before)
                        if g >= 1:
                            group_is_here(pool, g - 1, top_before)

                @block.vector
                def _(dve):
                    ch = Chain(dve)
                    with dve.Fori(0, NG) as g:
                        layer_norm(ch, dve, lambda j: flat(CT[:, bass.ds(g * G + j, 1), :]), lambda j: c[:, j, :], st,
                                   lambda: dve.wait_ge(pe_done.sem, g * 2 + PEs.base)).then_inc(dve_done.sem, D.tick("c"))
                        dve.wait_ge(rows_here.sem, g + (rows_here.value + 1))
                        combine(dve, ch, g, top_before, (XN, Y1))
                        ch.link(layer_norm(ch, dve, lambda j: flat(X[:, bass.ds(g * G + j, 1), :]), lambda j: u[:, j, :], st))
                        layer_norm(ch, dve, lambda j: u[:, j, :], lambda j: l[:, j, :], st).then_inc(dve_done.sem, D.tick("l"))
                        ch.link()

                @block.tensor
                def _(pe):
                    with pe.Fori(0, NG) as g:
                        for src, b_, step, made, kept in ((c, 0, "turn_c", "c", "c_kept"), (l, 1, "turn_l", "l", "l_kept")):
                            pe.wait_ge(dve_done.sem, D.at(g, made))
                            pe.wait_ge(act_done.sem, g * 2 + ACs.base)
                            for j in range(G):
                                ins = pe.transpose(bank[b_][:, j * P:(j + 1) * P], src[:, j, :], ident[:, :])
                            ins.then_inc(pe_done.sem, PEs.tick(step))

                @block.scalar
                def _(act):
                    with act.Fori(0, NG) as g:
                        for b_, dst, step, kept, at in ((0, CNT, "turn_c", "c_kept", 2), (1, LT, "turn_l", "l_kept", 4)):
                            act.wait_ge(pe_done.sem, PEs.at(g, step))
                            act.activation(flat(group(dst, g)), bank[b_][:, :], ACT.Identity, scale=cols[:, at:at + 1],
                                           bias=cols[:, at + 1:at + 2]).then_inc(act_done.sem, ACs.tick(kept))
                for s_ in (PEs, ACs, D):
                    s_.close(NG)
                close_gathers(top_before)

        def attention_2():
            with ExitStack() as ph:
                wq = sb_in(ph, "wq", [P, INNER])
                wkv = sb_in(ph, "wkv", [P, 2 * INNER])
                wo = sb_in(ph, "wo", [P, INNER])
                kv_in = sb_in(ph, "kv_in", [P, 2, 2 * P])
                qT = SETA2[:, 2048:4096].rearrange("p (s c q) -> p s c q", s=2, c=8)
                kT = Y1[:, :, :].rearrange("p a d -> p (a d)").rearrange("p (s c k) -> p s c k", s=2, c=8)
                v = XN[:, :, :].rearrange("p a d -> p (a d)").rearrange("p (s t f) -> p s t f", s=2, t=2)
                probs = sb_in(ph, "probs2", [P, 2, 4, 256])
                pT = sb_in(ph, "probs_turned2", [P, 2, 2, 512])
                orow = sb_in(ph, "head_rows", [P, INNER])
                oT = sb_in(ph, "head_rows_turned", [P, INNER])
                nmax = sb_in(ph, "neg_max2", [P, 4, 4])
                sums = sb_in(ph, "sums2", [P, HEADS])
                rinv = sb_in(ph, "rinv2", [P, HEADS])
                PEs = Steps(pe_done, ["S1", "OT1p", "T00", "Q0", "T01", "Q1", "PV0", "K0",
                                      "S2", "Yp", "T10", "K1", "T11", "K2", "PV1", "K3",
                                      "S3", "V0", "T20", "OT0", "T21", "V1", "PV2", "V2",
                                      "S0n", "V3", "T30", "T31", "PV3"])
                ACs = Steps(act_done, ["OT1p", "exp1", "T01", "Q1", "exp2", "T11", "K2", "V0", "exp3", "T21", "V1", "V3", "exp0n", "T31"])
                D = Steps(dve_done, ["max1", "T00", "Q0", "K0", "Yp", "max2", "T10", "K1", "O0", "K3",
                                     "max3", "T20", "OT0", "V2", "max0n", "T30", "O1"])
                FIRST = ["Q0", "Q1", "K0", "K1", "K2", "K3", "V0", "V1", "V2", "V3"]
                PE0, AC0, D0 = PEs.base, ACs.base, D.base
                PEs.base += len(FIRST) + 1
                ACs.base += 6
                D.base += 6
                PO = Steps(pool_done, ["kv_in"])
                block = ph.enter_context(nc.Block())
                PJ, BO, BT, BS = 0, 1, (2, 3), (4, 6)

                def cols_of_k(c):
                    return wkv[:, c * P:(c + 1) * P]

                @block.sync
                def _(sp):
                    sp.dma_start(wq[:, :], A["L2_xattn_Wq"]).then_inc(weights_x.sem, 16)
                    sp.dma_start(wkv[:, :], A["L2_xattn_Wkv"]).then_inc(weights_x.sem, 16)
                    sp.dma_start(wo[:, :].rearrange("p (c d) -> p c d", d=P), A["L2_xattn_Wo"].rearrange("(c p) d -> p c d", p=P)).then_inc(weights_x.sem, 16)

                @block.gpsimd
                def _(pool):
                    def copy(b, s):
                        pool.tensor_copy(kv_in[:, s, 0:P], flat(CNT[:, bass.ds(b, 1), :]))
                        pool.tensor_copy(kv_in[:, s, P:2 * P], flat(LT[:, bass.ds(b, 1), :])).then_inc(pool_done.sem, 1)
                    copy(0, 0)
                    copy(1, 1)
                    PO.seen = 1
                    with pool.Fori(1, B // 2) as i:
                        for s in range(2):
                            pool.wait_ge(pe_done.sem, (i * 2 + s - 3) * len(PEs.names) + (PEs.base + PEs.names.index("V3") + 1) if s == 1
                                         else (i * 2 - 2) * len(PEs.names) + PEs.base)
                            copy(i * 2 + s, s)

                def idle(eng, sem, S, name):
                    eng.drain().then_inc(sem, S.tick(name))

                PJ_ORDER = ["OT1p", "Q0", "Q1", "K0", "Yp", "K1", "K2", "K3", "V0", "OT0", "V1", "V2", "V3"]

                def pe_batch(pe, b, s, prev, nxt, mark):
                    def bank_free(name):
                        i = PJ_ORDER.index(name)
                        before = PJ_ORDER[i - 1]
                        t = b if i else b - 1
                        if i == 0 and isinstance(b, int) and b == 0:
                            return
                        if before in ACs.names:
                            pe.wait_ge(act_done.sem, ACs.at(t, before))
                        else:
                            pe.wait_ge(dve_done.sem, D.at(t, before))

                    def q_chunks(n, slot, name):
                        for c in range(4):
                            ins = pe.matmul(bank[PJ][:, c * P:(c + 1) * P], wq[:, (4 * n + c) * P:(4 * n + c + 1) * P], kv_in[:, slot, P:2 * P], start=True, stop=True)
                        return ins

                    def k_chunks(n, slot):
                        for c in range(2):
                            ins = pe.matmul(bank[PJ][:, c * 256:(c + 1) * 256], cols_of_k(2 * n + c), kv_in[:, slot, :], start=True, stop=True)
                        return ins

                    def v_rows(n, slot):
                        t, half = n // 2, n % 2
                        return pe.matmul(bank[PJ][:, :], kv_in[:, slot, t * P:(t + 1) * P], wkv[:, INNER + half * 512:INNER + (half + 1) * 512], start=True, stop=True)

                    def project(name):
                        make = {"Q": lambda n: q_chunks(n, 1 - s, name), "K": lambda n: k_chunks(n, 1 - s), "V": lambda n: v_rows(n, 1 - s)}
                        bank_free(name)
                        if nxt:
                            make[name[0]](int(name[1])).then_inc(pe_done.sem, PEs.tick(name))
                        else:
                            idle(pe, pe_done.sem, PEs, name)

                    def scores(u, slot, name):
                        for pp in range(2):
                            for par in range(2):
                                c = 2 * u + pp
                                ins = pe.matmul(bank[BS[u % 2] + par][:, pp * 256:(pp + 1) * 256], qT[par * HD:(par + 1) * HD, slot, c, :],
                                                kT[par * HD:(par + 1) * HD, slot, c, :], start=True, stop=True)
                        return ins

                    def turn_probs(u, pp, name):
                        for par in range(2):
                            for c in range(2):
                                ins = pe.transpose(bank[BT[pp]][:, (2 * par + c) * P:(2 * par + c + 1) * P], probs[:, u % 2, 2 * par + pp, c * P:(c + 1) * P], ident[:, :])
                        ins.then_inc(pe_done.sem, PEs.tick(name))

                    def mix(u):
                        if u % 2 == 0:
                            if u == 2:
                                pe.wait_ge(dve_done.sem, D.at(b, "O0"))
                            elif prev:
                                pe.wait_ge(dve_done.sem, D.at(b - 1, "O1"))
                        pe.wait_ge(dve_done.sem, D.at(b, f"T{u}0"))
                        pe.wait_ge(act_done.sem, ACs.at(b, f"T{u}1"))
                        for pp in range(2):
                            for par in range(2):
                                h = 4 * u + 2 * pp + par
                                for c in range(2):
                                    ins = pe.matmul(bank[BO][:, (h % 8) * HD:(h % 8 + 1) * HD], pT[:, u % 2, pp, (2 * par + c) * P:(2 * par + c + 1) * P],
                                                    v[:, s, c, h * HD:(h + 1) * HD], start=(c == 0), stop=(c == 1))
                        ins.then_inc(pe_done.sem, PEs.tick(f"PV{u}"))

                    def turn_out(half, name):
                        bank_free(name)
                        for c in range(4):
                            cc = 4 * half + c
                            ins = pe.transpose(bank[PJ][:, c * P:(c + 1) * P], orow[:, cc * P:(cc + 1) * P], ident[:, :])
                        ins.then_inc(pe_done.sem, PEs.tick(name))

                    def out_rows(name):
                        bank_free(name)
                        for c in range(8):
                            ins = pe.matmul(bank[PJ][:, 0:P], oT[:, c * P:(c + 1) * P], wo[:, c * P:(c + 1) * P], start=(c == 0), stop=(c == 7))
                        ins.then_inc(pe_done.sem, PEs.tick(name))

                    if mark == "first":
                        for i, name in enumerate(FIRST):
                            if i:
                                if (i - 1) % 2 == 0:
                                    pe.wait_ge(act_done.sem, AC0 + (i - 1) // 2 + 1)
                                else:
                                    pe.wait_ge(dve_done.sem, D0 + (i - 1) // 2 + 1)
                            n = int(name[1])
                            {"Q": lambda: q_chunks(n, 0, name), "K": lambda: k_chunks(n, 0), "V": lambda: v_rows(n, 0)}[name[0]]().then_inc(pe_done.sem, 1)
                        pe.wait_ge(dve_done.sem, D0 + 5)
                        scores(0, 0, "S0").then_inc(pe_done.sem, 1)
                        return
                    for u in range(4):
                        if u < 3:
                            scores(u + 1, s, None).then_inc(pe_done.sem, PEs.tick(f"S{u + 1}"))
                        elif nxt:
                            pe.wait_ge(dve_done.sem, D.at(b, "K3"))
                            pe.wait_ge(act_done.sem, ACs.at(b, "K2"))
                            scores(0, 1 - s, None).then_inc(pe_done.sem, PEs.tick("S0n"))
                        else:
                            idle(pe, pe_done.sem, PEs, "S0n")
                        if u == 0:
                            if prev:
                                pe.wait_ge(dve_done.sem, D.at(b - 1, "O1"))
                                turn_out(1, "OT1p")
                            else:
                                idle(pe, pe_done.sem, PEs, "OT1p")
                        elif u == 1:
                            if prev:
                                out_rows("Yp")
                            else:
                                idle(pe, pe_done.sem, PEs, "Yp")
                        elif u == 2:
                            project("V0")
                        else:
                            project("V3")
                        if u == 0:
                            if isinstance(b, int) and b == 0:
                                pe.wait_ge(act_done.sem, ACs.base)
                            else:
                                pe.wait_ge(act_done.sem, ACs.at(b - 1, "exp0n"))
                        else:
                            pe.wait_ge(act_done.sem, ACs.at(b, f"exp{u}"))
                        if u:
                            pe.wait_ge(dve_done.sem, D.at(b, f"T{u - 1}0"))
                        turn_probs(u, 0, f"T{u}0")
                        if u == 0:
                            project("Q0")
                        elif u == 1:
                            project("K1")
                        elif u == 2:
                            pe.wait_ge(dve_done.sem, D.at(b, "O0"))
                            turn_out(0, "OT0")
                        if u:
                            pe.wait_ge(act_done.sem, ACs.at(b, f"T{u - 1}1"))
                        turn_probs(u, 1, f"T{u}1")
                        if u < 3:
                            project(("Q1", "K2", "V1")[u])
                        mix(u)
                        if u < 3:
                            project(("K0", "K3", "V2")[u])
                    if mark == "last":
                        pe.wait_ge(dve_done.sem, D.at(b, "O1"))
                        for c in range(4):
                            ins = pe.transpose(bank[PJ][:, c * P:(c + 1) * P], orow[:, (4 + c) * P:(5 + c) * P], ident[:, :])
                        ins.then_inc(pe_done.sem, 1)
                        pe.wait_ge(act_done.sem, ACs.base + B * len(ACs.names) + 1)
                        for c in range(8):
                            ins = pe.matmul(bank[PJ][:, 0:P], oT[:, c * P:(c + 1) * P], wo[:, c * P:(c + 1) * P], start=(c == 0), stop=(c == 7))
                        ins.then_inc(pe_done.sem, 1)

                def kept(name, slot):
                    n = int(name[1])
                    if name[0] == "Q":
                        return qT[:, slot, 4 * n:4 * n + 4, :].rearrange("p c q -> p (c q)"), 0.125
                    if name[0] == "K":
                        return kT[:, slot, 2 * n:2 * n + 2, :].rearrange("p c k -> p (c k)"), None
                    return v[:, slot, n // 2, (n % 2) * 512:(n % 2 + 1) * 512], None

                def act_batch(act, b, s, prev, nxt, mark):
                    def keep(name):
                        if nxt:
                            act.wait_ge(pe_done.sem, PEs.at(b, name))
                            dst, scale = kept(name, 1 - s)
                            (act.mul(dst, bank[PJ][:, :], scale) if scale else act.copy(dst, bank[PJ][:, :])).then_inc(act_done.sem, ACs.tick(name))
                        else:
                            idle(act, act_done.sem, ACs, name)

                    def exps(u, tick):
                        for par in range(2):
                            for pp in range(2):
                                h = 4 * u + 2 * pp + par
                                ins = act.activation(probs[:, u % 2, 2 * par + pp, :], bank[BS[u % 2] + par][:, pp * 256:(pp + 1) * 256], ACT.Exp,
                                                     bias=nmax[:, u, 2 * par + pp:2 * par + pp + 1], accum_out=sums[:, h:h + 1])
                        ins.then_inc(act_done.sem, tick)

                    if mark == "first":
                        for i in range(0, 10, 2):
                            act.wait_ge(pe_done.sem, PE0 + i + 1)
                            dst, scale = kept(FIRST[i], 0)
                            (act.mul(dst, bank[PJ][:, :], scale) if scale else act.copy(dst, bank[PJ][:, :])).then_inc(act_done.sem, 1)
                        act.wait_ge(dve_done.sem, D0 + 6)
                        exps(0, 1)
                        return
                    for u in range(4):
                        if u == 0:
                            if prev:
                                act.wait_ge(pe_done.sem, PEs.at(b, "OT1p"))
                                act.copy(oT[:, 512:1024], bank[PJ][:, :]).then_inc(act_done.sem, ACs.tick("OT1p"))
                            else:
                                idle(act, act_done.sem, ACs, "OT1p")
                        elif u == 2:
                            keep("V0")
                        elif u == 3:
                            keep("V3")
                        if u < 3:
                            act.wait_ge(dve_done.sem, D.at(b, f"max{u + 1}"))
                            exps(u + 1, ACs.tick(f"exp{u + 1}"))
                        elif nxt:
                            act.wait_ge(dve_done.sem, D.at(b, "max0n"))
                            exps(0, ACs.tick("exp0n"))
                        else:
                            idle(act, act_done.sem, ACs, "exp0n")
                        act.wait_ge(pe_done.sem, PEs.at(b, f"T{u}1"))
                        act.copy(pT[:, u % 2, 1, :], bank[BT[1]][:, :]).then_inc(act_done.sem, ACs.tick(f"T{u}1"))
                        if u < 3:
                            keep(("Q1", "K2", "V1")[u])
                    if mark == "last":
                        act.wait_ge(pe_done.sem, PEs.base + B * len(PEs.names) + 1)
                        act.copy(oT[:, 512:1024], bank[PJ][:, :]).then_inc(act_done.sem, 1)

                def dve_batch(dve, ch, b, s, prev, nxt, mark):
                    def keep(name):
                        if nxt:
                            dve.wait_ge(pe_done.sem, PEs.at(b, name))
                            dst, scale = kept(name, 1 - s)
                            dve.tensor_scalar(dst, bank[PJ][:, :], scale or 1.0, None, ALU.mult).then_inc(dve_done.sem, D.tick(name))
                        else:
                            idle(dve, dve_done.sem, D, name)

                    def maxima(u, tick):
                        dve.tensor_reduce(nmax[:, u, :], ps[:, BS[u % 2]:BS[u % 2] + 2, :].rearrange("p r (h k) -> p (r h) k", k=256), AX.X, ALU.max,
                                          negate=True).then_inc(dve_done.sem, tick)

                    def heads_out(half, tick):
                        ch.link(dve.reciprocal(rinv[:, half * 8:half * 8 + 8], sums[:, half * 8:half * 8 + 8]))
                        dve.tensor_tensor(orow[:, half * 512:(half + 1) * 512].rearrange("p (h d) -> p h d", d=HD), bank[BO][:, :].rearrange("p (h d) -> p h d", d=HD),
                                          rinv[:, half * 8:half * 8 + 8].unsqueeze(2).to_broadcast([P, 8, HD]), ALU.mult).then_inc(dve_done.sem, tick)

                    def add_rows(bb, tick):
                        xt = flat(X[:, bass.ds(bb, 1), :])
                        dve.tensor_tensor(xt, xt, bank[PJ][:, 0:P], ALU.add).then_inc(dve_done.sem, tick)

                    if mark == "first":
                        for i in range(1, 10, 2):
                            dve.wait_ge(pe_done.sem, PE0 + i + 1)
                            dst, scale = kept(FIRST[i], 0)
                            dve.tensor_scalar(dst, bank[PJ][:, :], scale or 1.0, None, ALU.mult).then_inc(dve_done.sem, 1)
                        dve.wait_ge(pe_done.sem, PE0 + 11)
                        maxima(0, 1)
                        return
                    for u in range(4):
                        if u == 1:
                            if prev:
                                dve.wait_ge(pe_done.sem, PEs.at(b, "Yp"))
                                add_rows(b - 1, D.tick("Yp"))
                            else:
                                idle(dve, dve_done.sem, D, "Yp")
                        if u < 3:
                            dve.wait_ge(pe_done.sem, PEs.at(b, f"S{u + 1}"))
                            maxima(u + 1, D.tick(f"max{u + 1}"))
                        elif nxt:
                            dve.wait_ge(pe_done.sem, PEs.at(b, "S0n"))
                            maxima(0, D.tick("max0n"))
                        else:
                            idle(dve, dve_done.sem, D, "max0n")
                        dve.wait_ge(pe_done.sem, PEs.at(b, f"T{u}0"))
                        dve.tensor_copy(pT[:, u % 2, 0, :], bank[BT[0]][:, :]).then_inc(dve_done.sem, D.tick(f"T{u}0"))
                        if u < 2:
                            keep(("Q0", "K1")[u])
                        elif u == 2:
                            dve.wait_ge(pe_done.sem, PEs.at(b, "OT0"))
                            dve.tensor_copy(oT[:, 0:512], bank[PJ][:, :]).then_inc(dve_done.sem, D.tick("OT0"))
                        if u % 2 == 1:
                            dve.wait_ge(pe_done.sem, PEs.at(b, f"PV{u}"))
                            heads_out(u // 2, D.tick(f"O{u // 2}"))
                        if u < 3:
                            keep(("K0", "K3", "V2")[u])
                    if mark == "last":
                        dve.wait_ge(pe_done.sem, PEs.base + B * len(PEs.names) + 2)
                        add_rows(b, 1)

                def all_batches(eng, batch):
                    batch(0, 0, False, True, "first")
                    batch(0, 0, False, True, None)
                    with eng.Fori(0, B // 2 - 1) as i:
                        batch(i * 2 + 1, 1, True, True, None)
                        batch(i * 2 + 2, 0, True, True, None)
                    batch(B - 1, 1, True, False, "last")

                @block.tensor
                def _(pe):
                    pe.wait_ge(weights_x.sem, weights_x.value + 48)
                    pe.wait_ge(pool_done.sem, PO.base + 1)

                    def batch(b, s, prev, nxt, mark):
                        if nxt and mark != "first":
                            pe.wait_ge(pool_done.sem, PO.at(b + 1, "kv_in"))
                        pe_batch(pe, b, s, prev, nxt, mark)
                    all_batches(pe, batch)

                @block.scalar
                def _(act):
                    all_batches(act, lambda *a: act_batch(act, *a))

                @block.vector
                def _(dve):
                    ch = Chain(dve)
                    all_batches(dve, lambda *a: dve_batch(dve, ch, *a))
                for c in (PEs, ACs, D):
                    c.close(B, 4)
                PO.close(B)
                pe_done.value += 2
                act_done.value += 1
                dve_done.value += 1
                weights_x.value += 48

        def tail_only(layer):
            with ExitStack() as ph:
                st = norm_tiles(ph, "t2")
                tl = tail_tiles(ph)
                PEs, ACs, D = Steps(pe_done, TAIL_PE), Steps(act_done, TAIL_ACT), Steps(dve_done, TAIL_DVE)
                block = ph.enter_context(nc.Block())

                @block.vector
                def _(dve):
                    ch = Chain(dve)
                    with dve.Fori(0, NG) as g:
                        tail_dve(dve, ch, g, D, PEs, st, tl)

                @block.tensor
                def _(pe):
                    with pe.Fori(0, NG) as g:
                        tail_pe(pe, g, D, PEs, ACs, tl, layer)

                @block.scalar
                def _(act):
                    with act.Fori(0, NG) as g:
                        tail_act(act, g, PEs, ACs, tl)
                for c in (PEs, ACs, D):
                    c.close(NG)

        def attention_3(top_before):
            SCALE = float(P) ** -0.5
            with ExitStack() as ph:
                u = sb_in(ph, "u_rows3", [P, G, P])
                uT = sb_in(ph, "u_turned3", [P, G * P])
                qT = sb_in(ph, "q_turned3", [P, G * P])
                kT = sb_in(ph, "k_turned3", [P, G * P])
                probs = sb_in(ph, "probs3", [P, G, P])
                probsT = sb_in(ph, "probs_turned3", [P, G, P])
                mask = sb_in(ph, "mask_row3", [1, B * P], BF16)
                sums = sb_in(ph, "sums3", [P, G])
                nmax = sb_in(ph, "neg_max3", [P, G])
                rinv = sb_in(ph, "rinv3", [P, G])
                st = norm_tiles(ph, "a3")
                tl = tail_tiles(ph)
                PEs = Steps(pe_done, ["k", "turn_u", "q", "scores", "turn_p", "mixed"] + TAIL_PE)
                ACs = Steps(act_done, ["k_kept", "u_turned", "q_kept", "exp", "p_turned"] + TAIL_ACT)
                D = Steps(dve_done, ["u_normed", "max"] + TAIL_DVE)
                mask_loaded = loaded.value + 16
                block = ph.enter_context(nc.Block())

                @block.sync
                def _(sp):
                    sp.dma_start(mask[:, :], mask_dram[1:2, :]).then_inc(loaded.sem, 16)

                @block.gpsimd
                def _(pool):
                    for g in range(NG + 1):
                        if g < NG:
                            gather_group(pool, g, top_before)
                        if g >= 1:
                            group_is_here(pool, g - 1, top_before)

                @block.tensor
                def _(pe):
                    pe.wait_ge(loaded.sem, mask_loaded)
                    with pe.Fori(0, NG) as g:
                        pe.matmul(bank[0][:, :], wsmall[:, 7, :], flat(group(CTT, g)), start=True, stop=True).then_inc(pe_done.sem, PEs.tick("k"))
                        pe.wait_ge(dve_done.sem, D.at(g, "u_normed"))
                        for j in range(G):
                            ins = pe.transpose(bank[1][:, j * P:(j + 1) * P], u[:, j, :], ident[:, :])
                        ins.then_inc(pe_done.sem, PEs.tick("turn_u"))
                        pe.wait_ge(act_done.sem, ACs.at(g, "u_turned"))
                        pe.matmul(bank[2][:, :], wsmall[:, 6, :], uT[:, :], start=True, stop=True).then_inc(pe_done.sem, PEs.tick("q"))
                        pe.matmul(bank[3][:, :], ones[0:1, :], mask[:, bass.ds(g * (G * P), G * P)], start=True, stop=False, skip_group_check=True)
                        pe.wait_ge(act_done.sem, ACs.at(g, "q_kept"))
                        for j in range(G):
                            ins = pe.matmul(bank[3][:, j * P:(j + 1) * P], qT[:, j * P:(j + 1) * P], kT[:, j * P:(j + 1) * P], start=False, stop=True, skip_group_check=True)
                        ins.then_inc(pe_done.sem, PEs.tick("scores"))
                        pe.wait_ge(act_done.sem, ACs.at(g, "exp"))
                        for j in range(G):
                            ins = pe.transpose(bank[4][:, j * P:(j + 1) * P], probs[:, j, :], ident[:, :])
                        ins.then_inc(pe_done.sem, PEs.tick("turn_p"))
                        pe.wait_ge(act_done.sem, ACs.at(g, "p_turned"))
                        for j in range(G):
                            ins = pe.matmul(bank[5][:, j * P:(j + 1) * P], probsT[:, j, :], flat(CT[:, bass.ds(g * G + j, 1), :]), start=True, stop=True)
                        ins.then_inc(pe_done.sem, PEs.tick("mixed"))
                        tail_pe(pe, g, D, PEs, ACs, tl, 3)

                @block.scalar
                def _(act):
                    with act.Fori(0, NG) as g:
                        act.wait_ge(pe_done.sem, PEs.at(g, "k"))
                        act.activation(kT[:, :], bank[0][:, :], ACT.Identity, bias=cols[:, 1:2]).then_inc(act_done.sem, ACs.tick("k_kept"))
                        act.wait_ge(pe_done.sem, PEs.at(g, "turn_u"))
                        act.copy(uT[:, :], bank[1][:, :]).then_inc(act_done.sem, ACs.tick("u_turned"))
                        act.wait_ge(pe_done.sem, PEs.at(g, "q"))
                        act.activation(qT[:, :], bank[2][:, :], ACT.Identity, bias=cols[:, 0:1]).then_inc(act_done.sem, ACs.tick("q_kept"))
                        act.wait_ge(dve_done.sem, D.at(g, "max"))
                        for j in range(G):
                            ins = act.activation(probs[:, j, :], bank[3][:, j * P:(j + 1) * P], ACT.Exp, bias=nmax[:, j:j + 1], scale=SCALE, accum_out=sums[:, j:j + 1])
                        ins.then_inc(act_done.sem, ACs.tick("exp"))
                        act.wait_ge(pe_done.sem, PEs.at(g, "turn_p"))
                        act.copy(flat(probsT[:, :, :]), bank[4][:, :]).then_inc(act_done.sem, ACs.tick("p_turned"))
                        tail_act(act, g, PEs, ACs, tl)

                @block.vector
                def _(dve):
                    ch = Chain(dve)
                    with dve.Fori(0, NG) as g:
                        dve.wait_ge(rows_here.sem, g + (rows_here.value + 1))
                        combine(dve, ch, g, top_before, (XN, Y1))
                        layer_norm(ch, dve, lambda j: flat(X[:, bass.ds(g * G + j, 1), :]), lambda j: u[:, j, :], st).then_inc(dve_done.sem, D.tick("u_normed"))
                        dve.wait_ge(pe_done.sem, PEs.at(g, "scores"))
                        ch.link(dve.tensor_reduce(nmax[:, :], bank[3][:, :].rearrange("p (j l) -> p j l", j=G), AX.X, ALU.max, negate=True))
                        dve.tensor_scalar(nmax[:, :], nmax[:, :], SCALE, None, ALU.mult).then_inc(dve_done.sem, D.tick("max"))
                        dve.wait_ge(act_done.sem, ACs.at(g, "exp"))
                        ch.link(dve.reciprocal(rinv[:, :], sums[:, :]))
                        dve.wait_ge(pe_done.sem, PEs.at(g, "mixed"))
                        for j in range(G):
                            xt = flat(X[:, bass.ds(g * G + j, 1), :])
                            ins = dve.scalar_tensor_tensor(xt, bank[5][:, j * P:(j + 1) * P], rinv[:, j:j + 1], xt, ALU.mult, ALU.add)
                        ch.link(ins)
                        tail_dve(dve, ch, g, D, PEs, st, tl)
                for c in (PEs, ACs, D):
                    c.close(NG)
                close_gathers(top_before)
                loaded.value += 16

        attention_1(2)
        route(1, 2, CAPACITY)
        experts(1)
        attention_2_norms(2)
        attention_2()
        tail_only(2)
        route(2, 2, 0)
        experts(2)
        attention_3(2)
        route(3, 1, 0)
        experts(3)
        combine_only(1)

        with nc.Block() as block:
            @block.sync
            def _(sp):
                sp.dma_start(out.rearrange("t p d -> p t d"), X[:, :, :]).then_inc(stored.sem, 16)
                sp.wait_ge(stored.sem, 16)


_INS = ['x', 'ctx_1024', 'mask_BxS2_if1', 'mask_BxS2_ik1', 'L0_xattn_W0', 'L0_xattn_W1', 'L0_ffn_router_w', 'L0_ffn_w1', 'L0_ffn_b1', 'L0_ffn_w2', 'L0_ffn_b2', 'L1_xattn_Wq', 'L1_xattn_bq', 'L1_xattn_Wk', 'L1_xattn_bk', 'L1_xattn_Wv', 'L1_xattn_bv', 'L1_xattn_Wp', 'L1_xattn_bp', 'L1_ffn_router_w', 'L1_ffn_router_b', 'L1_ffn_W', 'L1_ffn_V', 'L1_ffn_W_out', 'L2_xattn_ln1_w', 'L2_xattn_ln1_b', 'L2_xattn_ln2_w', 'L2_xattn_ln2_b', 'L2_xattn_Wq', 'L2_xattn_Wkv', 'L2_xattn_Wo', 'L2_ffn_gate_w', 'L2_ffn_gate_up_w', 'L2_ffn_down_w', 'L3_xattn_Wq_w', 'L3_xattn_Wq_b', 'L3_xattn_Wk_w', 'L3_xattn_Wk_b', 'L3_ffn_gate_w', 'L3_ffn_w1', 'L3_ffn_b1', 'L3_ffn_w2', 'L3_ffn_b2']


def kernel(**inputs):
    import numpy as _np
    import concourse.bacc as _bacc
    from concourse import mybir as _mybir
    from concourse.bass_utils import run_bass_kernel_spmd as _run

    nc = _bacc.Bacc("TRN2", target_bir_lowering=False, num_devices=1)
    arrays, handles = {}, {}
    for name in _INS:
        a = _np.ascontiguousarray(inputs[name])
        arrays[f"in_{name}_dram"] = a
        handles[name] = nc.dram_tensor(f"in_{name}_dram", a.shape, _mybir.dt.from_np(a.dtype), kind="ExternalInput").ap()
    out = nc.dram_tensor("out_0_dram", (B, P, P), _mybir.dt.float32, kind="ExternalOutput").ap()
    build(nc, handles, out)
    r = _run(nc, [arrays], core_ids=[0])
    return r.results[0]["out_0_dram"]
```

```python
from contextlib import ExitStack

import concourse.bass as bass
from concourse import mybir
import numpy as np

ALU = mybir.AluOpType
ACT = mybir.ActivationFunctionType
AX = mybir.AxisListType
F32 = mybir.dt.float32
BF16 = mybir.dt.bfloat16
I32 = mybir.dt.int32
U32 = mybir.dt.uint32

P = 128
B = 32
G = 4
NG = B // G
E = 8
H1 = 512
EPS = 1e-5
MASKED = -1e30
FAR = 1.0e6
CAPACITY = 256
RSQRT_SEED = 1597463007.0

TILES_TOP2 = (2 * B * P + E * (P - 1)) // P + 1
TILES_TOP1 = (B * P + E * (P - 1)) // P + 1
TILES_CAP = E * CAPACITY // P

BIAS_PARTS = [("L0_ffn_b1", E * H1), ("L3_ffn_b1", E * H1), ("L0_ffn_b2", E * P), ("L3_ffn_b2", E * P),
              ("L1_xattn_bq", P), ("L1_xattn_bk", P), ("L1_xattn_bv", P), ("L1_xattn_bp", P)]
BIAS_AT = {}
_at = 0
for _n, _w in BIAS_PARTS:
    BIAS_AT[_n] = (_at, _w)
    _at += _w
BIAS_WIDTH = _at
ROUTER_B_AT = BIAS_WIDTH
BIAS_TOTAL = BIAS_WIDTH + P


class Steps:

    def __init__(self, counter, names):
        self.base, self.names = counter.value, names
        self.counter, self.seen = counter, 0

    def tick(self, name):
        assert self.names[self.seen % len(self.names)] == name, (name, self.names[self.seen % len(self.names)])
        self.seen += 1
        return 1

    def at(self, turn, name):
        return turn * len(self.names) + (self.base + self.names.index(name) + 1)

    def close(self, turns):
        assert self.names == [] or (self.seen and self.seen % len(self.names) == 0), (self.seen, len(self.names))
        self.counter.value = self.base + turns * len(self.names)


class Chain:

    def __init__(self, eng):
        self.eng = eng

    def link(self, ins=None):
        self.eng.drain()


class Counter:
    def __init__(self, sem):
        self.sem, self.value = sem, 0


def weave(bodies):
    bodies = list(bodies)
    while bodies:
        bodies = [b for b in bodies if next(b, "end") != "end"]


class Stream:

    def __init__(self, counters, pe=(), act=(), dve=(), pool=()):
        self.pe, self.act, self.dve, self.pool = counters
        self.PE, self.ACT, self.DVE, self.POOL = (Steps(c, n) for c, n in zip(counters, (pe, act, dve, pool)))

    def close(self, turns):
        for steps in (self.PE, self.ACT, self.DVE, self.POOL):
            steps.close(turns)


def build(nc, A, out):
    with ExitStack() as top:
        names = set()

        def sb_in(ctx, name, shape, dt=F32):
            while name in names:
                name += "_"
            names.add(name)
            return ctx.enter_context(nc.sbuf_tensor(name, shape, dt))

        def sb(name, shape, dt=F32):
            return sb_in(top, name, shape, dt)

        def counter(name):
            return Counter(top.enter_context(nc.semaphore(name)))

        ps = top.enter_context(nc.psum_tensor("psum_banks", [P, 8, 512], F32))
        bank = [ps[:, i, :] for i in range(8)]

        X = sb("x_rows", [P, B, P])
        XN = sb("normed_rows", [P, B, P])
        Y1 = sb("gathered_rows", [P, B, P])
        CT = sb("ctx_rows", [P, B, P])
        CTT = sb("ctx_turned", [P, B, P])
        SETA1 = sb("expert_w1_a", [P, E * H1])
        SETA2 = sb("expert_w2_a", [P, E * H1])
        SETB1 = sb("expert_w1_b", [P, E * H1])
        SETB2 = sb("expert_w2_b", [P, E * H1])
        ident = sb("ident", [P, P])
        tri = sb("tri", [P, P], BF16)
        ones = sb("ones", [P, P], BF16)
        iota8 = sb("iota8", [P, E])
        blocks = sb("head_blocks", [P, P + 16])
        wsmall = sb("wsmall", [P, 8, P])
        router = sb("router", [P, 4, E])
        rows3 = sb("bias_rows", [3, 2 * E * P + 4 * P + P], BF16)
        cols = sb("bias_cols", [P, 6])
        MX = sb("top_logits", [P, B, E])
        IX = sb("top_experts", [P, B, E])
        LG = sb("logits", [P, B, E])
        POS = sb("slots", [P, 2, B], U32)
        SCT = sb("scatter_slots", [P, 2, B], U32)
        WT = sb("mix_weights", [P, 2, B])
        tile_expert = sb("tile_expert", [1, TILES_TOP2], I32)
        iota_tile = sb("iota_tile", [1, TILES_TOP2])

        spare = sb("mask_or_head_rows", [P, B * P // 2])
        mask = spare[0:1, :].bitcast(BF16)
        zero = Y1[:, 0:8, :].rearrange("p a d -> p (a d)")
        xs = nc.dram_tensor("sorted_rows", [TILES_TOP2 * P, P], F32).ap()
        ys = nc.dram_tensor("expert_rows", [TILES_TOP2 * P, P], F32).ap()
        bias_dram = nc.dram_tensor("bias_split", [3, BIAS_TOTAL], BF16).ap()
        mask_dram = nc.dram_tensor("mask_rows", [2, B * P], BF16).ap()

        loaded = counter("loaded")
        x_loaded = counter("x_loaded")
        ctx_loaded = counter("ctx_loaded")
        masks_loaded = counter("masks_loaded")
        W = 4
        stream_counters = [[counter(f"{n}{w}") for n in ("pe_step", "act_step", "dve_step", "pool_step")] for w in range(W)]
        ctx_copied = [counter(f"ctx_copied{w}") for w in range(W)]
        pe_done = counter("pe_done")
        act_done = counter("act_done")
        dve_done = counter("dve_done")
        pool_done = counter("pool_done")
        bias_stored = counter("bias_stored")
        rows_loaded = counter("rows_loaded")
        zeroed = counter("zeroed")
        scattered = counter("scattered")
        gathered = [counter("gathered_even"), counter("gathered_odd")]
        rows_here = counter("rows_here")
        sorted_in = [counter(f"sorted_in{i}") for i in range(4)]
        expert_out = [counter(f"expert_out{i}") for i in range(4)]
        rows_turned = counter("rows_turned")
        hidden_made = counter("hidden_made")
        hidden_turned = counter("hidden_turned")
        expert_made = counter("expert_made")
        rows_turned_kept = counter("rows_turned_kept")
        gates_kept = counter("gates_kept")
        hidden_kept = counter("hidden_kept")
        hidden_turned_kept = counter("hidden_turned_kept")
        expert_kept = counter("expert_kept")
        stored = counter("stored")
        weights_a = counter("weights_a")
        weights_b = counter("weights_b")
        weights_x = counter("weights_x")

        def group(t, g):
            return t[:, bass.ds(g * G, G), :]

        def flat(ap):
            return ap.rearrange("p a d -> p (a d)")

        with ExitStack() as ph:
            wraw = sb_in(ph, "small_raw", [P, 6, P])
            rraw = sb_in(ph, "router_raw", [E, 2, P])
            NBC = BIAS_TOTAL // P
            braw = sb_in(ph, "bias_raw", [P, NBC])
            bres = sb_in(ph, "bias_rest", [P, 2, NBC])
            bsp = sb_in(ph, "bias_split_sb", [P, 3, NBC], BF16)
            mraw = sb_in(ph, "mask_raw", [P, 2, B], I32)
            mbf = sb_in(ph, "mask_bf", [P, 2, B], BF16)
            block = ph.enter_context(nc.Block())
            n_loads = 0

            @block.sync
            def _(sp):
                nonlocal n_loads

                def load(dst, src):
                    nonlocal n_loads
                    sp.dma_start(dst, src).then_inc(loaded.sem, 16)
                    n_loads += 1
                sp.wait_ge(dve_done.sem, 1)
                for name, width in BIAS_PARTS:
                    at = BIAS_AT[name][0] // P
                    src = A[name] if len(A[name].shape) == 1 else A[name].rearrange("e f -> (e f)")
                    load(braw[:, at:at + width // P], src.rearrange("(p c) -> p c", p=P))
                load(braw[0:E, NBC - 1:NBC], A["L1_ffn_router_b"].rearrange("(e a) -> e a", a=1))
                for m, name in enumerate(("mask_BxS2_if1", "mask_BxS2_ik1")):
                    load(mraw[:, m, :], A[name].rearrange("b (q c) -> (b q) c", c=B))
                for i, name in enumerate(("L1_xattn_Wq", "L1_xattn_Wk", "L1_xattn_Wv", "L1_xattn_Wp",
                                          "L3_xattn_Wq_w", "L3_xattn_Wk_w")):
                    load(wraw[:, i, :], A[name])
                load(wsmall[:, 0, :], A["L0_xattn_W0"])
                load(wsmall[:, 1, :], A["L0_xattn_W1"])
                load(rraw[:, 0, :], A["L0_ffn_router_w"])
                load(rraw[:, 1, :], A["L1_ffn_router_w"])
                load(router[:, 2, :], A["L2_ffn_gate_w"])
                load(router[:, 3, :], A["L3_ffn_gate_w"])
                for i, name in enumerate(("L3_xattn_Wq_b", "L3_xattn_Wk_b", "L2_xattn_ln1_w", "L2_xattn_ln1_b",
                                          "L2_xattn_ln2_w", "L2_xattn_ln2_b")):
                    load(cols[:, i:i + 1], A[name].rearrange("(p a) -> p a", a=1))
                sp.dma_start(CT[:, :, :], A["ctx_1024"].rearrange("t p d -> p t d")).then_inc(ctx_loaded.sem, 16)
                sp.dma_start(X[:, :, :], A["x"].rearrange("t p d -> p t d")).then_inc(x_loaded.sem, 16)
                sp.wait_ge(dve_done.sem, 4)
                for k in range(3):
                    for name, width in BIAS_PARTS + [("router_b", P)]:
                        at = BIAS_AT.get(name, (ROUTER_B_AT,))[0]
                        sp.dma_start(bias_dram[k, at:at + width].rearrange("(p c) -> p c", p=P),
                                     bsp[:, k, at // P:(at + width) // P]).then_inc(bias_stored.sem, 16)
                for m in range(2):
                    sp.dma_start(mask_dram[m, :].rearrange("(p c) -> p c", p=P), mbf[:, m, :]).then_inc(bias_stored.sem, 16)
                sp.wait_ge(bias_stored.sem, 16 * (3 * (len(BIAS_PARTS) + 1) + 2))
                sp.dma_start(mask[:, :], mask_dram[0:1, :]).then_inc(masks_loaded.sem, 16)
                at = BIAS_AT["L0_ffn_b2"][0]
                sp.dma_start(rows3[:, :], bias_dram[:, at:at + 2 * E * P + 5 * P]).then_inc(rows_loaded.sem, 16)
                sp.dma_start(SETB1[:, :].rearrange("p (c h) -> p c h", h=P), A["L0_ffn_w1"].rearrange("e (c p) h -> p (e c) h", p=P)).then_inc(weights_b.sem, 16)
                sp.dma_start(SETB2[:, :].rearrange("p (e f) -> p e f", e=E), A["L0_ffn_w2"].rearrange("e h f -> h e f")).then_inc(weights_b.sem, 16)
                for i in range(TILES_TOP2 // 8):
                    sp.dma_start(xs.rearrange("(i p r) d -> i p (r d)", p=P, r=8)[i], zero).then_inc(zeroed.sem, 16)

            @block.gpsimd
            def _(pool):
                for c in stream_counters:
                    pool.drain().then_inc(c[3].sem, 1)
                pool.memset(blocks[:, :], 1.0).then_inc(pool_done.sem, 1)
                pool.wait_ge(pool_done.sem, 1)
                for base, sign in ((0, 1), (7, -1)):
                    pool.affine_select(out=blocks[:, 0:P].rearrange("p (h c) -> p h c", c=8), in_=blocks[:, 0:P].rearrange("p (h c) -> p h c", c=8),
                                       compare_op=ALU.is_ge, fill=0.0, base=base, pattern=[[-8 * sign, 16], [0, 8]], channel_multiplier=sign)
                    pool.affine_select(out=blocks[:, P:P + 16], in_=blocks[:, P:P + 16], compare_op=ALU.is_ge, fill=0.0, base=base,
                                       pattern=[[-8 * sign, 16]], channel_multiplier=sign).then_inc(pool_done.sem, 1)
                    pool.wait_ge(pool_done.sem, 2 if sign == 1 else 3)
                pool.memset(ident[:, :], 0.0).then_inc(pool_done.sem, 1)
                pool.memset(tri[:, :], 1.0).then_inc(pool_done.sem, 1)
                pool.iota(iota8[:, :], [[1, E]], base=0, channel_multiplier=0,
                          allow_small_or_imprecise_dtypes=True).then_inc(pool_done.sem, 1)
                pool.iota(iota_tile[:, :], [[1, TILES_TOP2]], base=0, channel_multiplier=0,
                          allow_small_or_imprecise_dtypes=True).then_inc(pool_done.sem, 1)
                pool.wait_ge(pool_done.sem, 7)
                pool.affine_select(out=ident[:, :], in_=ident[:, :], compare_op=ALU.not_equal, fill=1.0, base=0,
                                   pattern=[[-1, P]], channel_multiplier=1).then_inc(pool_done.sem, 1)
                pool.affine_select(out=tri[:, :], in_=tri[:, :], compare_op=ALU.is_gt, fill=0.0, base=0,
                                   pattern=[[1, P]], channel_multiplier=-1).then_inc(pool_done.sem, 1)

            @block.vector
            def _(dve):
                for c in stream_counters:
                    dve.drain().then_inc(c[2].sem, 1)
                dve.memset(braw[:, :], 0.0).then_inc(dve_done.sem, 1)
                dve.memset(ones[:, :], 1.0)
                dve.memset(zero, 0.0).then_inc(dve_done.sem, 1)
                ch = Chain(dve)
                dve.wait_ge(loaded.sem, 16 * n_loads)
                for m in range(2):
                    ins = dve.tensor_scalar(mbf[:, m, :], mraw[:, m, :], 0.0, MASKED, ALU.is_equal, ALU.mult)
                ins.then_inc(dve_done.sem, 1)
                ch.link(dve.tensor_copy(bsp[:, 0, :], braw[:, :]))
                ch.link(dve.tensor_tensor(bres[:, 0, :], braw[:, :], bsp[:, 0, :], ALU.subtract))
                ch.link(dve.tensor_copy(bsp[:, 1, :], bres[:, 0, :]))
                ch.link(dve.tensor_tensor(bres[:, 1, :], bres[:, 0, :], bsp[:, 1, :], ALU.subtract))
                dve.tensor_copy(bsp[:, 2, :], bres[:, 1, :]).then_inc(dve_done.sem, 1)

            @block.tensor
            def _(pe):
                for c in stream_counters:
                    pe.drain().then_inc(c[0].sem, 1)
                pe.wait_ge(pool_done.sem, 9)
                pe.wait_ge(loaded.sem, 16 * n_loads)
                for i in range(6):
                    ins = pe.transpose(bank[i // 4][:, (i % 4) * P:(i % 4 + 1) * P], wraw[:, i, :], ident[:, :])
                for i in range(2):
                    ins = pe.transpose(bank[2][:, i * E:(i + 1) * E], rraw[:, i, :], ident[0:E, 0:E])
                ins.then_inc(pe_done.sem, 1)

            @block.scalar
            def _(act):
                for c in stream_counters:
                    act.drain().then_inc(c[1].sem, 1)
                act.wait_ge(pe_done.sem, 1)
                act.copy(flat(wsmall[:, 2:6, :]), bank[0][:, :])
                act.copy(flat(wsmall[:, 6:8, :]), bank[1][:, 0:2 * P])
                act.copy(flat(router[:, 0:2, :]), bank[2][:, 0:2 * E]).then_inc(act_done.sem, 1)
        loaded.value = 16 * n_loads
        pe_done.value, act_done.value, dve_done.value, pool_done.value = 1, 1, 4, 9
        bias_stored.value = 16 * (3 * (len(BIAS_PARTS) + 1) + 2)
        rows_loaded.value, masks_loaded.value = 16, 16
        for cs in stream_counters:
            for c in cs:
                c.value = 1
        weights_b.value = 32

        R_B2 = {"L0": 0, "L3": E * P}
        R_SMALL = 2 * E * P
        R_ROUTER = R_SMALL + 4 * P

        def norm_scales(ch, dve, var, rstd, work):
            half, sq = work[:, 0, :], work[:, 1, :]
            bits = work[:, 2, :].bitcast(I32)
            ch.link(dve.tensor_scalar(sq, var, EPS, None, ALU.add))
            dve.tensor_scalar(half, sq, -0.5, None, ALU.mult)
            ch.link(dve.tensor_scalar(bits, sq.bitcast(I32), 1, None, ALU.logical_shift_right))
            ch.link(dve.tensor_scalar(rstd.bitcast(I32), bits, -1.0, RSQRT_SEED, ALU.mult, ALU.add))
            for _ in range(3):
                ch.link(dve.tensor_tensor(sq, rstd, rstd, ALU.mult))
                ch.link(dve.tensor_tensor(sq, sq, half, ALU.mult))
                ch.link(dve.scalar_tensor_tensor(rstd, sq, 1.5, rstd, ALU.add, ALU.mult))

        def norm_all(dve, ch, st, src, dst, signal, free=None):
            for w in range(W):
                for j in range(G):
                    dve.bn_stats(st["stats"][:, w * G + j, :], src(w)(j))
            ch.link()
            for j in range(W * G):
                dve.bn_aggr(st["mv"][:, j, :], st["stats"][:, j, :])
            ch.link()
            norm_scales(ch, dve, st["mv"][:, :, 1], st["rstd"][:, :], st["work"])
            for w in range(W):
                if free:
                    free(w)
                for j in range(G):
                    n = w * G + j
                    ins = dve.tensor_scalar(dst(w)(j), src(w)(j), st["mv"][:, n, 0:1], st["rstd"][:, n:n + 1],
                                            ALU.subtract, ALU.mult)
                signal(w, ins)

        def combine_turn(dve, ch, i, slots):
            for w in range(W):
                dve.wait_ge(rows_here.sem, i * W + (w + rows_here.value + 1))
                combine(dve, ch, i * W + w, slots)

        def close_streams(SS, ctx=False):
            for w, S in enumerate(SS):
                S.close(TURNS)
                if ctx:
                    ctx_copied[w].value += TURNS

        def combine(dve, ch, g, slots):
            for k in range(slots):
                for j in range(G):
                    t = g * G + j
                    xt = flat(X[:, bass.ds(t, 1), :])
                    ins = dve.scalar_tensor_tensor(xt, flat((XN, Y1)[k][:, bass.ds(t, 1), :]), WT[:, k, bass.ds(t, 1)], xt,
                                                   ALU.mult, ALU.add)
                ch.link(ins)

        def x_tile(g):
            return lambda j: flat(X[:, bass.ds(g * G + j, 1), :])

        def tile_in(t):
            return lambda j: t[:, j, :]

        TAIL = dict(pe=["turn_tail", "logits"], act=["tail_turned", "tail_kept"], dve=["tail_normed", "logits_kept"])

        def norm_tiles(ph):
            return {"stats": sb_in(ph, "norm_stats", [P, W * G, 6]), "mv": sb_in(ph, "mean_var", [P, W * G, 2]),
                    "rstd": sb_in(ph, "rstd", [P, W * G]), "work": sb_in(ph, "newton", [P, 3, W * G])}

        def tail_tiles(ph, rows, turned):
            return {"rows": rows, "turned": turned, "mx": sb_in(ph, "tail_max", [P, G, E]),
                    "ix": sb_in(ph, "tail_index", [P, G, E], U32), "lg": sb_in(ph, "tail_logits", [P, G, E])}

        def tail_norms(dve, ch, i, SS, st, T, free=None):
            norm_all(dve, ch, st, lambda w: x_tile(i * W + w), lambda w: tile_in(T[w]["tl"]["rows"]),
                     lambda w, ins: ins.then_inc(SS[w].dve.sem, SS[w].DVE.tick("tail_normed")), free)

        def tail_dve(dve, ch, g, i, S, tl, logits_bank):
            dve.wait_ge(S.pe.sem, S.PE.at(i, "logits"))
            ch.link(dve.tensor_copy(flat(tl["lg"][:, :, :]), logits_bank[:, 0:G * E]))
            for j in range(G):
                ins = dve.max(tl["mx"][:, j, :], tl["lg"][:, j, :])
            ch.link(ins)
            for j in range(G):
                ins = dve.max_index(tl["ix"][:, j, :], tl["mx"][:, j, :], tl["lg"][:, j, :])
            dve.tensor_copy(flat(group(MX, g)), flat(tl["mx"][:, :, :]))
            dve.tensor_copy(flat(group(LG, g)), flat(tl["lg"][:, :, :]))
            ch.link()
            dve.tensor_copy(flat(group(IX, g)), flat(tl["ix"][:, :, :])).then_inc(S.dve.sem, S.DVE.tick("logits_kept"))
            yield

        def tail_pe(pe, i, S, tl, layer, turn_bank, logits_bank):
            pe.wait_ge(S.dve.sem, S.DVE.at(i, "tail_normed"))
            for j in range(G):
                ins = pe.transpose(turn_bank[:, j * P:(j + 1) * P], tl["rows"][:, j, :], ident[:, :])
            ins.then_inc(S.pe.sem, S.PE.tick("turn_tail"))
            yield
            pe.wait_ge(S.act.sem, S.ACT.at(i, "tail_turned"))
            if layer == 1:
                for j in range(G):
                    pe.matmul(logits_bank[:, j * E:(j + 1) * E], ones[0:3, :], rows3[:, R_ROUTER:R_ROUTER + E],
                              start=(j == 0), stop=False, skip_group_check=True)
            for j in range(G):
                ins = pe.matmul(logits_bank[:, j * E:(j + 1) * E], tl["turned"][:, j, :], router[:, layer, :],
                                start=(layer != 1 and j == 0), stop=True, skip_group_check=True)
            ins.then_inc(S.pe.sem, S.PE.tick("logits"))
            yield

        def tail_act(act, g, i, S, tl, turn_bank):
            act.wait_ge(S.pe.sem, S.PE.at(i, "turn_tail"))
            act.copy(flat(tl["turned"][:, :, :]), turn_bank[:, :]).then_inc(S.act.sem, S.ACT.tick("tail_turned"))
            yield
            act.copy(flat(group(XN, g)), flat(tl["rows"][:, :, :])).then_inc(S.act.sem, S.ACT.tick("tail_kept"))
            yield

        def turn_before(steps, i):
            return i * len(steps.names) + steps.base

        def streams(pe=(), act=(), dve=(), pool=(), tail=True):
            t = TAIL if tail else {}
            return [Stream(c, list(pe) + t.get("pe", []), list(act) + t.get("act", []), list(dve) + t.get("dve", []),
                           list(pool) + t.get("pool", [])) for c in stream_counters]

        def carve(big, at, shape):
            n = int(np.prod(shape[1:]))
            v = big[:, at:at + n]
            return v.rearrange("p (a b) -> p a b", b=shape[2]) if len(shape) == 3 else v

        def turn_group(pe, bank_, src):
            for j in range(G):
                ins = pe.transpose(bank_[:, j * P:(j + 1) * P], src(j), ident[:, :])
            return ins

        TURNS = NG // W

        def attention_0():
            with ExitStack() as ph:
                SS = streams(pe=["turn_ctx", "keys"] + [f"{n}{h}" for h in range(2) for n in ("turn_u", "scores", "turn_p", "mixed")],
                             act=["ctx_turned", "keys_kept"] + [f"{n}{h}" for h in range(2) for n in ("u_turned", "exp", "p_turned")],
                             dve=["u_normed", "max0", "u_new", "max1"], pool=["x_and_u"])
                T = []
                for w in range(W):
                    t = {"keys": carve(SETA1, w * 2 * G * P, [P, 2, G * P]), "cg": carve(SETA2, w * 2 * G * P, [P, G, P]),
                         "probsT": carve(SETA2, (2 * w + 1) * G * P, [P, G, P]), "u": sb_in(ph, "u_rows", [P, G, P]),
                         "uT": sb_in(ph, "u_turned", [P, G, P]), "probs": sb_in(ph, "probs", [P, G, P]),
                         "xu": sb_in(ph, "x_plus_u", [P, G, P]),
                         "sums": sb_in(ph, "sums", [P, 2, G]), "nmax": sb_in(ph, "neg_max", [P, 2, G]), "rinv": sb_in(ph, "rinv", [P, 2, G]),
                         "A": bank[2 * w], "B": bank[2 * w + 1]}
                    t["tl"] = tail_tiles(ph, t["u"], t["uT"])
                    T.append(t)
                st = norm_tiles(ph)
                block = ph.enter_context(nc.Block())

                @block.gpsimd
                def _(pool):
                    def copy_ctx(w, i, S, t):
                        pool.tensor_copy(flat(t["cg"]), flat(group(CT, i * W + w))).then_inc(ctx_copied[w].sem, 1)

                    def body(w, i, S, t, more):
                        g = i * W + w
                        if more:
                            pool.wait_ge(S.pe.sem, S.PE.at(i, "turn_ctx"))
                            copy_ctx(w, i + 1, S, t)
                        yield
                        pool.wait_ge(S.dve.sem, S.DVE.at(i, "u_new"))
                        pool.tensor_tensor(flat(t["xu"][:, :, :]), flat(t["u"][:, :, :]), flat(group(X, g)), ALU.add).then_inc(S.pool.sem, S.POOL.tick("x_and_u"))
                        yield
                    pool.wait_ge(ctx_loaded.sem, 16)
                    for w in range(W):
                        copy_ctx(w, 0, SS[w], T[w])
                    with pool.Fori(0, TURNS - 1) as i:
                        weave(body(w, i, SS[w], T[w], True) for w in range(W))
                    weave(body(w, TURNS - 1, SS[w], T[w], False) for w in range(W))

                @block.tensor
                def _(pe):
                    def body(w, i, S, t):
                        g, A_, B_ = i * W + w, t["A"], t["B"]
                        pe.wait_ge(S.dve.sem, turn_before(S.DVE, i))
                        pe.wait_ge(ctx_copied[w].sem, i + (ctx_copied[w].value + 1))
                        turn_group(pe, A_, tile_in(t["cg"])).then_inc(S.pe.sem, S.PE.tick("turn_ctx"))
                        yield
                        pe.wait_ge(S.act.sem, S.ACT.at(i, "ctx_turned"))
                        for h, b_ in ((0, B_), (1, A_)):
                            ins = pe.matmul(b_[:, :], wsmall[:, h, :], flat(group(CTT, g)), start=True, stop=True)
                        ins.then_inc(S.pe.sem, S.PE.tick("keys"))
                        yield
                        pe.wait_ge(S.act.sem, S.ACT.at(i, "keys_kept"))
                        for h in range(2):
                            pe.wait_ge(S.dve.sem, S.DVE.at(i, ("u_normed", "u_new")[h]))
                            turn_group(pe, B_, tile_in(t["u"])).then_inc(S.pe.sem, S.PE.tick(f"turn_u{h}"))
                            pe.matmul(A_[:, :], ones[0:1, :], mask[:, bass.ds(g * (G * P), G * P)], start=True, stop=False, skip_group_check=True)
                            yield
                            pe.wait_ge(S.act.sem, S.ACT.at(i, f"u_turned{h}"))
                            for j in range(G):
                                ins = pe.matmul(A_[:, j * P:(j + 1) * P], t["uT"][:, j, :], t["keys"][:, h, j * P:(j + 1) * P], start=False, stop=True, skip_group_check=True)
                            ins.then_inc(S.pe.sem, S.PE.tick(f"scores{h}"))
                            yield
                            pe.wait_ge(S.act.sem, S.ACT.at(i, f"exp{h}"))
                            turn_group(pe, B_, tile_in(t["probs"])).then_inc(S.pe.sem, S.PE.tick(f"turn_p{h}"))
                            yield
                            pe.wait_ge(S.act.sem, S.ACT.at(i, f"p_turned{h}"))
                            for j in range(G):
                                ins = pe.matmul(A_[:, j * P:(j + 1) * P], t["probsT"][:, j, :], flat(CT[:, bass.ds(g * G + j, 1), :]), start=True, stop=True)
                            ins.then_inc(S.pe.sem, S.PE.tick(f"mixed{h}"))
                            yield
                        yield from tail_pe(pe, i, S, t["tl"], 0, B_, A_)
                    pe.wait_ge(masks_loaded.sem, 16)
                    with pe.Fori(0, TURNS) as i:
                        weave(body(w, i, SS[w], T[w]) for w in range(W))

                @block.scalar
                def _(act):
                    def body(w, i, S, t):
                        g, A_, B_ = i * W + w, t["A"], t["B"]
                        act.wait_ge(S.pe.sem, S.PE.at(i, "turn_ctx"))
                        act.copy(flat(group(CTT, g)), A_[:, :]).then_inc(S.act.sem, S.ACT.tick("ctx_turned"))
                        yield
                        act.wait_ge(S.pe.sem, S.PE.at(i, "keys"))
                        act.copy(t["keys"][:, 0, :], B_[:, :])
                        act.copy(t["keys"][:, 1, :], A_[:, :]).then_inc(S.act.sem, S.ACT.tick("keys_kept"))
                        yield
                        for h in range(2):
                            act.wait_ge(S.pe.sem, S.PE.at(i, f"turn_u{h}"))
                            act.copy(flat(t["uT"][:, :, :]), B_[:, :]).then_inc(S.act.sem, S.ACT.tick(f"u_turned{h}"))
                            yield
                            act.wait_ge(S.dve.sem, S.DVE.at(i, f"max{h}"))
                            for j in range(G):
                                ins = act.activation(t["probs"][:, j, :], A_[:, j * P:(j + 1) * P], ACT.Exp, bias=t["nmax"][:, h, j:j + 1], accum_out=t["sums"][:, h, j:j + 1])
                            ins.then_inc(S.act.sem, S.ACT.tick(f"exp{h}"))
                            yield
                            act.wait_ge(S.pe.sem, S.PE.at(i, f"turn_p{h}"))
                            act.copy(flat(t["probsT"]), B_[:, :]).then_inc(S.act.sem, S.ACT.tick(f"p_turned{h}"))
                            yield
                        yield from tail_act(act, g, i, S, t["tl"], B_)
                    with act.Fori(0, TURNS) as i:
                        weave(body(w, i, SS[w], T[w]) for w in range(W))

                @block.vector
                def _(dve):
                    ch = Chain(dve)

                    def body(w, i, S, t):
                        g, A_ = i * W + w, t["A"]
                        for h in range(2):
                            dve.wait_ge(S.pe.sem, S.PE.at(i, f"scores{h}"))
                            dve.tensor_reduce(t["nmax"][:, h, :], A_[:, :].rearrange("p (j l) -> p j l", j=G), AX.X, ALU.max, negate=True).then_inc(S.dve.sem, S.DVE.tick(f"max{h}"))
                            yield
                            dve.wait_ge(S.act.sem, S.ACT.at(i, f"exp{h}"))
                            ch.link(dve.reciprocal(t["rinv"][:, h, :], t["sums"][:, h, :]))
                            yield
                            dve.wait_ge(S.pe.sem, S.PE.at(i, f"mixed{h}"))
                            if h == 1:
                                dve.wait_ge(S.pool.sem, S.POOL.at(i, "x_and_u"))
                            for j in range(G):
                                dst, add = (t["u"][:, j, :], t["u"][:, j, :]) if h == 0 else (x_tile(g)(j), t["xu"][:, j, :])
                                ins = dve.scalar_tensor_tensor(dst, A_[:, j * P:(j + 1) * P], t["rinv"][:, h, j:j + 1], add, ALU.mult, ALU.add)
                            if h == 0:
                                ins.then_inc(S.dve.sem, S.DVE.tick("u_new"))
                            yield
                        ch.link()
                    dve.wait_ge(x_loaded.sem, 16)
                    with dve.Fori(0, TURNS) as i:
                        norm_all(dve, ch, st, lambda w: x_tile(i * W + w), lambda w: tile_in(T[w]["u"]),
                                 lambda w, ins: ins.then_inc(SS[w].dve.sem, SS[w].DVE.tick("u_normed")),
                                 lambda w: dve.wait_ge(SS[w].act.sem, turn_before(SS[w].ACT, i)))
                        weave(body(w, i, SS[w], T[w]) for w in range(W))
                        tail_norms(dve, ch, i, SS, st, T)
                        weave(tail_dve(dve, ch, i * W + w, i, SS[w], T[w]["tl"], T[w]["A"]) for w in range(W))
                close_streams(SS, ctx=True)

        attention_0()

        def route(layer, top, capacity):
            n_tiles = {0: TILES_TOP2, 1: TILES_CAP, 2: TILES_TOP2, 3: TILES_TOP1}[layer]
            with ExitStack() as ph:
                oh = sb_in(ph, "one_hot", [P, 2, B, E])
                ohb = sb_in(ph, "one_hot_bf", [P, B, E], BF16)
                tot = sb_in(ph, "totals", [P, B, E])
                run = sb_in(ph, "running", [P, B, E])
                pos = sb_in(ph, "positions", [P, B, E])
                tmp = sb_in(ph, "picked", [P, B, E])
                zeros = sb_in(ph, "zeros", [P, B])
                posf = sb_in(ph, "slot_f", [P, 2, B])
                keep = sb_in(ph, "kept", [P, 2, B])
                small = sb_in(ph, "tile_counts", [P, 4, E])
                cnt_i = sb_in(ph, "count_bits", [P, E], I32)
                expo = sb_in(ph, "exp_logits", [P, B, E])
                tcmp = sb_in(ph, "tile_compare", [1, TILES_TOP2, E])
                tsum = sb_in(ph, "tile_sum", [1, TILES_TOP2])
                block = ph.enter_context(nc.Block())
                dv, pv, av = dve_done.value, pe_done.value, act_done.value

                @block.vector
                def _(dve):
                    ch = Chain(dve)
                    dve.memset(zeros[:, :], 0.0)
                    for k in range(top):
                        dve.tensor_tensor(oh[:, k, :, :], IX[:, :, k:k + 1].to_broadcast([P, B, E]),
                                          iota8[:, :].unsqueeze(1).to_broadcast([P, B, E]), ALU.is_equal)
                    ch.link()
                    if top == 2:
                        dve.tensor_tensor(ohb[:, :, :], oh[:, 0, :, :], oh[:, 1, :, :], ALU.add).then_inc(dve_done.sem, 1)
                        dve.tensor_tensor(expo[:, :, 0], MX[:, :, 1], MX[:, :, 0], ALU.subtract).then_inc(dve_done.sem, 1)
                    else:
                        dve.tensor_copy(ohb[:, :, :], oh[:, 0, :, :]).then_inc(dve_done.sem, 1)
                        dve.tensor_tensor(expo[:, :, :], LG[:, :, :], MX[:, :, 0:1].to_broadcast([P, B, E]), ALU.subtract).then_inc(dve_done.sem, 1)
                    dve.wait_ge(pe_done.sem, pv + 1)
                    ch.link(dve.tensor_copy(tot[:, :, :].rearrange("p b e -> p (b e)"), bank[1][:, 0:B * E]))
                    for e in range(E):
                        dve.tensor_tensor_scan(run[:, :, e], tot[:, :, e], zeros[:, :], 0.0, ALU.add, ALU.add)
                    ch.link()
                    ch.link(dve.tensor_tensor(pos[:, :, :], run[:, :, :], tot[:, :, :], ALU.subtract))
                    ch.link(dve.tensor_tensor(pos[:, :, :], pos[:, :, :], bank[0][:, 0:B * E].rearrange("p (b e) -> p b e", e=E), ALU.add))
                    if capacity:
                        for k in range(top):
                            ch.link(dve.scalar_tensor_tensor(tmp[:, :, :], pos[:, :, :], float(capacity), oh[:, k, :, :], ALU.is_lt, ALU.mult))
                            ch.link(dve.tensor_reduce(keep[:, k, :], tmp[:, :, :], AX.X, ALU.add))
                        ch.link(dve.tensor_scalar(small[:, 3, :], iota8[:, :], float(capacity), None, ALU.mult))
                    else:
                        ch.link(dve.tensor_scalar(cnt_i[:, :], run[:, B - 1, :], float(P - 1), None, ALU.add))
                        ch.link(dve.tensor_scalar(cnt_i[:, :], cnt_i[:, :], 7, None, ALU.arith_shift_right))
                        ch.link(dve.tensor_copy(small[:, 0, :], cnt_i[:, :]))
                        ch.link(dve.tensor_tensor_scan(small[:, 1, :], small[:, 0, :], zeros[:, 0:E], 0.0, ALU.add, ALU.add))
                        ch.link(dve.tensor_tensor(small[:, 2, :], small[:, 1, :], small[:, 0, :], ALU.subtract))
                        ch.link(dve.tensor_scalar(small[:, 3, :], small[:, 2, :], float(P), None, ALU.mult))
                    ch.link(dve.tensor_tensor(pos[:, :, :], pos[:, :, :], small[:, 3, :].unsqueeze(1).to_broadcast([P, B, E]), ALU.add))
                    for k in range(top):
                        ch.link(dve.tensor_tensor(tmp[:, :, :], oh[:, k, :, :], pos[:, :, :], ALU.mult))
                        ch.link(dve.tensor_reduce(posf[:, k, :], tmp[:, :, :], AX.X, ALU.add))
                    if capacity:
                        ch.link(dve.tensor_tensor(posf[:, :, :], posf[:, :, :], keep[:, :, :], ALU.mult))
                        dve.tensor_copy(POS[:, :, :], posf[:, :, :])
                        ch.link(dve.tensor_scalar(tmp[:, 0:2 * B // E, :].rearrange("p a e -> p (a e)"), keep[:, :, :].rearrange("p a b -> p (a b)"), -FAR, FAR, ALU.mult, ALU.add))
                        dve.tensor_tensor(SCT[:, :, :].rearrange("p a b -> p (a b)"), posf[:, :, :].rearrange("p a b -> p (a b)"), tmp[:, 0:2 * B // E, :].rearrange("p a e -> p (a e)"), ALU.add).then_inc(dve_done.sem, 1)
                    else:
                        dve.tensor_copy(POS[:, 0:top, :], posf[:, 0:top, :]).then_inc(dve_done.sem, 1)
                        ch.link(dve.tensor_tensor(tcmp[:, 0:n_tiles, :], iota_tile[:, 0:n_tiles].unsqueeze(2).to_broadcast([1, n_tiles, E]),
                                                  small[0:1, 1, :].unsqueeze(1).to_broadcast([1, n_tiles, E]), ALU.is_ge))
                        ch.link(dve.tensor_reduce(tsum[:, 0:n_tiles], tcmp[:, 0:n_tiles, :], AX.X, ALU.add))
                        dve.tensor_scalar(tile_expert[:, 0:n_tiles], tsum[:, 0:n_tiles], float(E - 1), None, ALU.min)
                    dve.wait_ge(act_done.sem, av + 1)
                    ch.link()
                    if top == 2:
                        ch.link(dve.tensor_scalar(tmp[:, :, 0], expo[:, :, 1], 1.0, None, ALU.add))
                        ch.link(dve.reciprocal(WT[:, 0, :], tmp[:, :, 0]))
                        ch.link(dve.tensor_tensor(WT[:, 1, :], WT[:, 0, :], expo[:, :, 1], ALU.mult))
                        if capacity:
                            dve.tensor_tensor(WT[:, :, :], WT[:, :, :], keep[:, :, :], ALU.mult)
                    else:
                        ch.link(dve.tensor_reduce(tmp[:, :, 0], expo[:, :, :], AX.X, ALU.add))
                        dve.reciprocal(WT[:, 0, :], tmp[:, :, 0])

                @block.scalar
                def _(act):
                    act.wait_ge(dve_done.sem, dv + 2)
                    if top == 2:
                        act.activation(expo[:, :, 1], expo[:, :, 0], ACT.Exp).then_inc(act_done.sem, 1)
                    else:
                        act.activation(expo[:, :, :], expo[:, :, :], ACT.Exp).then_inc(act_done.sem, 1)
                    if layer == 0:
                        for i in range(16):
                            act.wait_ge(pe_done.sem, pv + 2 + i)
                            dst = SETA1 if i < 8 else SETA2
                            act.copy(dst[:, (i % 8) * 512:(i % 8 + 1) * 512], bank[2 + i % 6][:, :]).then_inc(act_done.sem, 1)

                @block.tensor
                def _(pe):
                    pe.wait_ge(dve_done.sem, dv + 1)
                    pe.matmul(bank[0][:, 0:B * E], tri[:, :], ohb[:, :, :].rearrange("p b e -> p (b e)"), start=True, stop=True)
                    pe.matmul(bank[1][:, 0:B * E], ones[:, :], ohb[:, :, :].rearrange("p b e -> p (b e)"), start=True, stop=True).then_inc(pe_done.sem, 1)
                    if layer == 0:
                        pe.wait_ge(weights_b.sem, weights_b.value)
                        for i in range(16):
                            if i >= 6:
                                pe.wait_ge(act_done.sem, av + 2 + i - 6)
                            raw = SETB1 if i < 8 else SETB2
                            for j in range(4):
                                c = (i % 8) * 4 + j
                                ins = pe.transpose(bank[2 + i % 6][:, j * P:(j + 1) * P], raw[:, c * P:(c + 1) * P], ident[:, :])
                            ins.then_inc(pe_done.sem, 1)

                @block.gpsimd
                def _(pool):
                    pool.wait_ge(dve_done.sem, dv + 3)
                    if layer == 0:
                        pool.wait_ge(zeroed.sem, 16 * (TILES_TOP2 // 8))
                    idx = SCT if capacity else POS
                    bound = dict(bounds_check=TILES_CAP * P - 1, oob_is_err=False) if capacity else {}
                    for t in range(B):
                        for k in range(top):
                            pool.indirect_dma_start(xs, bass.IndirectOffsetOnAxis(ap=idx[:, k, t:t + 1], axis=0), XN[:, t, :], None,
                                                    **bound).then_inc(scattered.sem, 16)
                    pool.wait_ge(scattered.sem, scattered.value + 16 * B * top)
            dve_done.value += 3
            pe_done.value += 1 + (16 if layer == 0 else 0)
            act_done.value += 1 + (16 if layer == 0 else 0)
            scattered.value += 16 * B * top

        def experts(layer):
            n_tiles = {0: TILES_TOP2, 1: TILES_CAP, 2: TILES_TOP2, 3: TILES_TOP1}[layer]
            W1, W2 = (SETA1, SETA2) if layer in (0, 2) else (SETB1, SETB2)
            gated = layer in (1, 2)
            NC = 2 if gated else 4
            UNROLL = 4
            with ExitStack() as ph:
                xr = sb_in(ph, "tile_rows", [P, 4, P])
                xt = sb_in(ph, "tile_turned", [P, 2, P])
                hid = sb_in(ph, "hidden", [P, 2, NC * P])
                gat = sb_in(ph, "gate", [P, 2, 256])
                hidT = sb_in(ph, "hidden_turned_sb", [P, 2, NC * P])
                yo = sb_in(ph, "expert_rows_sb", [P, 4, P])
                b1 = sb_in(ph, "expert_b1", [3, E * H1], BF16)
                b1_here = rows_loaded.value + 16
                block = ph.enter_context(nc.Block())

                def tile_of(rows, j):
                    return rows.rearrange("(t p) d -> t p d", p=P)[bass.ds(j, 1), :, :].rearrange("a p d -> (a p) d")

                def run(eng, step):
                    for k in range(-2, 2):
                        step(k, k % UNROLL)
                    with eng.Fori(0, (n_tiles - 4) // UNROLL) as q:
                        for u in range(UNROLL):
                            step(q * UNROLL + (2 + u), (2 + u) % UNROLL)
                    for k in range(n_tiles - 2, n_tiles + 1):
                        step(k, k % UNROLL)

                def exists(j):
                    return not isinstance(j, int) or 0 <= j < n_tiles

                def beyond(j, n):
                    return not isinstance(j, int) or j >= n

                @block.sync
                def _(sp):
                    if not gated:
                        at, width = BIAS_AT[f"L{layer}_ffn_b1"]
                        sp.dma_start(b1[:, :], bias_dram[:, at:at + width]).then_inc(rows_loaded.sem, 16)

                    if layer in (0, 2):
                        load_expert_weights(sp, layer + 1)

                    def load(j, s):
                        sp.dma_start(xr[:, s, :], tile_of(xs, j)).then_inc(sorted_in[s].sem, 16)
                    for j in range(4):
                        load(j, j)
                    with sp.Fori(1, n_tiles // 4) as q:
                        for s in range(4):
                            sp.wait_ge(rows_turned.sem, q * 4 + (s + rows_turned.value - 3))
                            load(q * 4 + s, s)

                @block.tensor
                def _(pe):
                    if not gated:
                        pe.wait_ge(rows_loaded.sem, b1_here)
                    if layer:
                        done = weights_a if layer == 2 else weights_b
                        pe.wait_ge(done.sem, done.value)

                    def turn_rows(j, u):
                        if exists(j):
                            if isinstance(j, int):
                                pe.wait_ge(sorted_in[u].sem, sorted_in[u].value + 16 * (j // 4 + 1))
                            else:
                                pe.wait_ge(sorted_in[u].sem, (j - u) * 4 + (sorted_in[u].value + 16))
                            if beyond(j, 2):
                                pe.wait_ge(rows_turned_kept.sem, j + (rows_turned_kept.value - 1))
                            pe.transpose(bank[u % 2][:, 0:P], xr[:, u, :], ident[:, :]).then_inc(rows_turned.sem, 1)

                    def expert_of(j):
                        if layer == 1:
                            return None
                        return pe.value_load(tile_expert[0:1, bass.ds(j, 1)], min_val=0, max_val=E - 1)

                    def hidden(j, u):
                        if exists(j):
                            e = expert_of(j)
                            if layer == 1:
                                off = (j // 2) * H1 if isinstance(j, int) else (j - u % 2) * (H1 // 2)
                            else:
                                off = e * H1
                            pe.wait_ge(rows_turned_kept.sem, j + (rows_turned_kept.value + 1))
                            if beyond(j, 2):
                                pe.wait_ge(hidden_kept.sem, j + (hidden_kept.value - 1))
                            out_ = bank[2 + u % 2]
                            ins = pe.matmul(out_[:, :], xt[:, u % 2, :], W1[:, bass.ds(off, H1)], start=True, stop=gated)
                            if not gated:
                                ins = pe.matmul(out_[:, :], ones[0:3, :], b1[:, bass.ds(off, H1)], start=False, stop=True)
                            ins.then_inc(hidden_made.sem, 1)

                    def turn_hidden(j, u):
                        if exists(j):
                            pe.wait_ge(hidden_kept.sem, j + (hidden_kept.value + 1))
                            if beyond(j, 2):
                                pe.wait_ge(hidden_turned_kept.sem, j + (hidden_turned_kept.value - 1))
                            for c in range(NC):
                                ins = pe.transpose(bank[4 + u % 2][:, c * P:(c + 1) * P], hid[:, u % 2, c * P:(c + 1) * P], ident[:, :])
                            ins.then_inc(hidden_turned.sem, 1)

                    def rows_out(j, u):
                        if exists(j):
                            e = expert_of(j)
                            if layer == 1:
                                off = (j // 2) * NC * P if isinstance(j, int) else (j - u % 2) * (NC * P // 2)
                            else:
                                off = e * (NC * P)
                            pe.wait_ge(hidden_turned_kept.sem, j + (hidden_turned_kept.value + 1))
                            if beyond(j, 2):
                                pe.wait_ge(expert_kept.sem, j + (expert_kept.value - 1))
                            out_ = bank[6 + u % 2]
                            for c in range(NC):
                                ins = pe.matmul(out_[:, 0:P], hidT[:, u % 2, c * P:(c + 1) * P], W2[:, bass.ds(off + c * P, P)],
                                                start=(c == 0), stop=(gated and c == NC - 1))
                            if not gated:
                                ins = pe.matmul(out_[:, 0:P], ones[0:3, :], rows3[:, bass.ds(e * P + R_B2[f"L{layer}"], P)], start=False, stop=True)
                            ins.then_inc(expert_made.sem, 1)

                    def step(k, u):
                        turn_rows(k + 2, (u + 2) % 4)
                        hidden(k + 1, (u + 1) % 4)
                        turn_hidden(k, u)
                        rows_out(k - 1, (u + 3) % 4)
                    run(pe, step)

                @block.scalar
                def _(act):
                    def store(j, s):
                        if exists(j):
                            act.wait_ge(expert_kept.sem, j + (expert_kept.value + 1))
                            act.dma_start(tile_of(ys, j), yo[:, s, :]).then_inc(expert_out[s].sem, 16)

                    def step(k, u):
                        store(k - 2, (u + 2) % 4)
                        j, s = k + 1, (u + 1) % 2
                        if exists(j):
                            act.wait_ge(hidden_made.sem, j + (hidden_made.value + 1))
                            if beyond(j, 2):
                                if gated:
                                    act.wait_ge(hidden_kept.sem, j + (hidden_kept.value - 1))
                                else:
                                    act.wait_ge(hidden_turned.sem, j + (hidden_turned.value - 1))
                            if gated:
                                half = 256 if layer == 1 else 0
                                act.activation(gat[:, s, :], bank[2 + s][:, half:half + 256], ACT.Silu).then_inc(gates_kept.sem, 1)
                            else:
                                act.activation(hid[:, s, :], bank[2 + s][:, :], ACT.Gelu).then_inc(hidden_kept.sem, 1)
                    run(act, step)
                    store(n_tiles - 1, 3)
                    for s in range(4):
                        act.wait_ge(expert_out[s].sem, expert_out[s].value + 16 * (n_tiles // 4))

                @block.vector
                def _(dve):
                    def step(k, u):
                        j, s = k + 2, u % 2
                        if exists(j):
                            dve.wait_ge(rows_turned.sem, j + (rows_turned.value + 1))
                            if beyond(j, 2):
                                dve.wait_ge(hidden_made.sem, j + (hidden_made.value - 1))
                            dve.tensor_copy(xt[:, s, :], bank[s][:, 0:P]).then_inc(rows_turned_kept.sem, 1)
                        j, s = k + 1, (u + 1) % 2
                        if gated and exists(j):
                            dve.wait_ge(gates_kept.sem, j + (gates_kept.value + 1))
                            if beyond(j, 2):
                                dve.wait_ge(hidden_turned.sem, j + (hidden_turned.value - 1))
                            half = 0 if layer == 1 else 256
                            dve.tensor_tensor(hid[:, s, :], bank[2 + s][:, half:half + 256], gat[:, s, :], ALU.mult).then_inc(hidden_kept.sem, 1)
                        j, s = k, u % 2
                        if exists(j):
                            dve.wait_ge(hidden_turned.sem, j + (hidden_turned.value + 1))
                            if beyond(j, 2):
                                dve.wait_ge(expert_made.sem, j + (expert_made.value - 1))
                            dve.tensor_copy(hidT[:, s, :], bank[4 + s][:, 0:NC * P]).then_inc(hidden_turned_kept.sem, 1)
                        j, s = k - 1, (u + 3) % 4
                        if exists(j):
                            dve.wait_ge(expert_made.sem, j + (expert_made.value + 1))
                            if isinstance(j, int):
                                if j >= 4:
                                    dve.wait_ge(expert_out[s].sem, expert_out[s].value + 16 * (j // 4))
                            else:
                                dve.wait_ge(expert_out[s].sem, (j - s) * 4 + expert_out[s].value)
                            dve.tensor_copy(yo[:, s, :], bank[6 + s % 2][:, 0:P]).then_inc(expert_kept.sem, 1)
                    run(dve, step)

            for c in (rows_turned, hidden_made, hidden_turned, expert_made, rows_turned_kept, hidden_kept, hidden_turned_kept, expert_kept):
                c.value += n_tiles
            if gated:
                gates_kept.value += n_tiles
            else:
                rows_loaded.value += 16
            for s in range(4):
                sorted_in[s].value += 16 * (n_tiles // 4)
                expert_out[s].value += 16 * (n_tiles // 4)

        def gather_group(pool, g, top):
            for t in range(g * G, (g + 1) * G):
                for k in range(top):
                    dst = (XN, Y1)[k]
                    pool.indirect_dma_start(dst[:, t, :], None, ys, bass.IndirectOffsetOnAxis(ap=POS[:, k, t:t + 1], axis=0)).then_inc(gathered[g % 2].sem, 16)

        def group_is_here(pool, g, top):
            pool.wait_ge(gathered[g % 2].sem, gathered[g % 2].value + 16 * G * top * (g // 2 + 1))
            pool.sem_inc(rows_here.sem, 1)

        def close_gathers(top):
            for c in gathered:
                c.value += 16 * G * top * NG // 2
            rows_here.value += NG

        def load_expert_weights(sp, layer):
            W1, W2 = (SETA1, SETA2) if layer in (0, 2) else (SETB1, SETB2)
            done = weights_a if layer in (0, 2) else weights_b
            w1v = W1[:, :].rearrange("p (e f) -> p e f", e=E)
            if layer == 1:
                srcs = [(w1v[:, :, 0:256], A["L1_ffn_W"].rearrange("e d f -> d e f")),
                        (w1v[:, :, 256:512], A["L1_ffn_V"].rearrange("e d f -> d e f")),
                        (W2[:, 0:E * 256].rearrange("p (c d) -> p c d", d=P), A["L1_ffn_W_out"].rearrange("e (c p) d -> p (e c) d", p=P))]
            elif layer == 2:
                srcs = [(w1v, A["L2_ffn_gate_up_w"].rearrange("e d f -> d e f")),
                        (W2[:, 0:E * 256].rearrange("p (c d) -> p c d", d=P), A["L2_ffn_down_w"].rearrange("e (c p) d -> p (e c) d", p=P))]
            else:
                srcs = [(w1v, A["L3_ffn_w1"].rearrange("e d f -> d e f")),
                        (W2[:, :].rearrange("p (c d) -> p c d", d=P), A["L3_ffn_w2"].rearrange("e (c p) d -> p (e c) d", p=P))]
            for dst, src in srcs:
                sp.dma_start(dst, src).then_inc(done.sem, 16)
            done.value += 16 * len(srcs)

        def combine_only(top):
            with nc.Block() as block:
                @block.gpsimd
                def _(pool):
                    for g in range(NG + 1):
                        if g < NG:
                            gather_group(pool, g, top)
                        if g >= 1:
                            group_is_here(pool, g - 1, top)

                @block.vector
                def _(dve):
                    ch = Chain(dve)
                    with dve.Fori(0, NG) as g:
                        dve.wait_ge(rows_here.sem, g + (rows_here.value + 1))
                        combine(dve, ch, g, top)
            close_gathers(top)

        def gather_turns(pool, top, before_turn=None):
            for g in range(NG + 1):
                if g < NG:
                    if before_turn and g % W == 0:
                        before_turn(g // W)
                    gather_group(pool, g, top)
                if g >= 1:
                    group_is_here(pool, g - 1, top)

        def attention_1(top_before):
            with ExitStack() as ph:
                VX = P + 16
                SS = streams(pe=["k", "v", "turn_u", "q", "turn_q", "kv", "out", "turn_o", "proj"],
                             act=["v_kept", "k_exp", "u_turned", "q_exp", "q_turned", "o_turned"],
                             dve=["k_less", "k_soft", "u_normed", "q_less", "q_soft", "kv_masked", "o"])
                one = sb_in(ph, "one_column", [P, 1])
                T = []
                for w in range(W):
                    t = {"ctx": carve(SETA1, 2 * w * G * P, [P, G, P]), "v": carve(SETA1, (2 * w + 1) * G * P, [P, G, P]),
                         "k": carve(SETA2, 2 * w * G * P, [P, G * P]), "q": carve(SETA2, (2 * w + 1) * G * P, [P, G * P]),
                         "u": sb_in(ph, "u_rows1", [P, G, P]), "uT": sb_in(ph, "u_turned1", [P, G, P]),
                         "qT": sb_in(ph, "q_turned", [P, G, P]), "kvm": sb_in(ph, "kv_masked", [P, G, VX]),
                         "red": sb_in(ph, "head_sums", [P, 4, G * 16]), "dinv": sb_in(ph, "d_inv", [P, G * 16]),
                         "A": bank[2 * w], "B": bank[2 * w + 1]}
                    t["tl"] = tail_tiles(ph, t["u"], t["uT"])
                    T.append(t)
                st = norm_tiles(ph)
                block = ph.enter_context(nc.Block())

                @block.gpsimd
                def _(pool):
                    def copy_ctx(i):
                        for w in range(W):
                            if i:
                                pool.wait_ge(SS[w].pe.sem, SS[w].PE.at(i - 1, "v"))
                            pool.tensor_copy(flat(T[w]["ctx"]), flat(group(CTT, i * W + w))).then_inc(ctx_copied[w].sem, 1)
                    gather_turns(pool, top_before, copy_ctx)

                @block.vector
                def _(dve):
                    ch = Chain(dve)

                    def heads(ap):
                        return ap.rearrange("p (h c) -> p h c", c=8)

                    def wide(ap):
                        return ap.unsqueeze(2).to_broadcast([P, G * 16, 8])

                    def soft_heads(i, S, t, src, name, at):
                        dst, red = t[name], t["red"]
                        dve.wait_ge(S.pe.sem, S.PE.at(i, name))
                        ch.link(dve.tensor_reduce(red[:, at, :], heads(src), AX.X, ALU.max))
                        dve.tensor_tensor(heads(dst), heads(src), wide(red[:, at, :]), ALU.subtract).then_inc(S.dve.sem, S.DVE.tick(f"{name}_less"))
                        yield
                        dve.wait_ge(S.act.sem, S.ACT.at(i, f"{name}_exp"))
                        ch.link(dve.tensor_reduce(red[:, at + 1, :], heads(dst), AX.X, ALU.add))
                        ch.link(dve.reciprocal(red[:, at + 1, :], red[:, at + 1, :]))
                        dve.tensor_tensor(heads(dst), heads(dst), wide(red[:, at + 1, :]), ALU.mult).then_inc(S.dve.sem, S.DVE.tick(f"{name}_soft"))
                        yield

                    def body(w, i, S, t):
                        g, A_, B_ = i * W + w, t["A"], t["B"]
                        yield from soft_heads(i, S, t, A_[:, :], "q", 2)
                        dve.wait_ge(S.pe.sem, S.PE.at(i, "kv"))
                        dve.tensor_tensor(t["kvm"][:, :, 0:P], A_[:, :].rearrange("p (j c) -> p j c", c=P), blocks[:, 0:P].unsqueeze(1).to_broadcast([P, G, P]), ALU.mult)
                        dve.tensor_tensor(t["kvm"][:, :, P:VX], B_[:, 0:G].unsqueeze(2).to_broadcast([P, G, 16]),
                                          blocks[:, P:VX].unsqueeze(1).to_broadcast([P, G, 16]), ALU.mult).then_inc(S.dve.sem, S.DVE.tick("kv_masked"))
                        yield
                        dve.wait_ge(S.pe.sem, S.PE.at(i, "out"))
                        ch.link(dve.reciprocal(t["dinv"][:, :], B_[:, 0:G * 16]))
                        o = flat(t["u"][:, :, :])
                        ch.link(dve.tensor_tensor(heads(o), heads(A_[:, :]), wide(t["dinv"][:, :]), ALU.mult))
                        dve.tensor_tensor(o, o, t["q"], ALU.add).then_inc(S.dve.sem, S.DVE.tick("o"))
                        yield
                        dve.wait_ge(S.pe.sem, S.PE.at(i, "proj"))
                        dve.tensor_tensor(flat(group(X, g)), flat(group(X, g)), A_[:, :], ALU.add)
                        yield
                    dve.memset(one[:, :], 1.0)
                    with dve.Fori(0, TURNS) as i:
                        weave(soft_heads(i, SS[w], T[w], T[w]["A"][:, :], "k", 0) for w in range(W))
                        combine_turn(dve, ch, i, top_before)
                        norm_all(dve, ch, st, lambda w: x_tile(i * W + w), lambda w: tile_in(T[w]["u"]),
                                 lambda w, ins: ins.then_inc(SS[w].dve.sem, SS[w].DVE.tick("u_normed")),
                                 lambda w: dve.wait_ge(SS[w].act.sem, turn_before(SS[w].ACT, i)))
                        weave(body(w, i, SS[w], T[w]) for w in range(W))
                        ch.link()
                        tail_norms(dve, ch, i, SS, st, T)
                        weave(tail_dve(dve, ch, i * W + w, i, SS[w], T[w]["tl"], T[w]["A"]) for w in range(W))

                @block.scalar
                def _(act):
                    def body(w, i, S, t):
                        g, A_, B_ = i * W + w, t["A"], t["B"]

                        def keep(step, name, dst):
                            act.wait_ge(S.pe.sem, S.PE.at(i, step))
                            act.copy(flat(t[dst][:, :, :]), B_[:, :]).then_inc(S.act.sem, S.ACT.tick(name))

                        def exp(name):
                            act.wait_ge(S.dve.sem, S.DVE.at(i, f"{name}_less"))
                            act.activation(t[name], t[name], ACT.Exp).then_inc(S.act.sem, S.ACT.tick(f"{name}_exp"))
                        keep("v", "v_kept", "v")
                        yield
                        exp("k")
                        yield
                        keep("turn_u", "u_turned", "uT")
                        yield
                        exp("q")
                        yield
                        keep("turn_q", "q_turned", "qT")
                        yield
                        keep("turn_o", "o_turned", "uT")
                        yield
                        yield from tail_act(act, g, i, S, t["tl"], B_)
                    with act.Fori(0, TURNS) as i:
                        weave(body(w, i, SS[w], T[w]) for w in range(W))

                @block.tensor
                def _(pe):
                    def biased(out_, which, lhs, w):
                        for j in range(G):
                            pe.matmul(out_[:, j * P:(j + 1) * P], ones[0:3, :], rows3[:, R_SMALL + which * P:R_SMALL + (which + 1) * P],
                                      start=(j == 0), stop=False, skip_group_check=True)
                        for j in range(G):
                            ins = pe.matmul(out_[:, j * P:(j + 1) * P], lhs[:, j, :], w, start=False, stop=True, skip_group_check=True)
                        return ins

                    def body(w, i, S, t):
                        g, A_, B_ = i * W + w, t["A"], t["B"]
                        pe.wait_ge(S.dve.sem, turn_before(S.DVE, i))
                        pe.wait_ge(ctx_copied[w].sem, i + (ctx_copied[w].value + 1))
                        biased(A_, 1, t["ctx"], wsmall[:, 3, :]).then_inc(S.pe.sem, S.PE.tick("k"))
                        biased(B_, 2, t["ctx"], wsmall[:, 4, :]).then_inc(S.pe.sem, S.PE.tick("v"))
                        yield
                        pe.wait_ge(S.act.sem, S.ACT.at(i, "v_kept"))
                        pe.wait_ge(S.dve.sem, S.DVE.at(i, "u_normed"))
                        turn_group(pe, B_, tile_in(t["u"])).then_inc(S.pe.sem, S.PE.tick("turn_u"))
                        yield
                        pe.wait_ge(S.act.sem, S.ACT.at(i, "u_turned"))
                        biased(A_, 0, t["uT"], wsmall[:, 2, :]).then_inc(S.pe.sem, S.PE.tick("q"))
                        yield
                        pe.wait_ge(S.dve.sem, S.DVE.at(i, "q_soft"))
                        turn_group(pe, B_, lambda j: t["q"][:, j * P:(j + 1) * P]).then_inc(S.pe.sem, S.PE.tick("turn_q"))
                        for j in range(G):
                            pe.matmul(A_[:, j * P:(j + 1) * P], t["k"][:, j * P:(j + 1) * P], t["v"][:, j, :], start=True, stop=True)
                        yield
                        pe.wait_ge(S.act.sem, S.ACT.at(i, "q_turned"))
                        for j in range(G):
                            ins = pe.matmul(B_[:, j:j + 1], t["k"][:, j * P:(j + 1) * P], one[:, :], start=True, stop=True)
                        ins.then_inc(S.pe.sem, S.PE.tick("kv"))
                        yield
                        pe.wait_ge(S.dve.sem, S.DVE.at(i, "kv_masked"))
                        for j in range(G):
                            pe.matmul(A_[:, j * P:(j + 1) * P], t["qT"][:, j, :], t["kvm"][:, j, 0:P], start=True, stop=True)
                            ins = pe.matmul(B_[:, j * 16:(j + 1) * 16], t["qT"][:, j, :], t["kvm"][:, j, P:VX], start=True, stop=True)
                        ins.then_inc(S.pe.sem, S.PE.tick("out"))
                        yield
                        pe.wait_ge(S.dve.sem, S.DVE.at(i, "o"))
                        turn_group(pe, B_, tile_in(t["u"])).then_inc(S.pe.sem, S.PE.tick("turn_o"))
                        yield
                        pe.wait_ge(S.act.sem, S.ACT.at(i, "o_turned"))
                        biased(A_, 3, t["uT"], wsmall[:, 5, :]).then_inc(S.pe.sem, S.PE.tick("proj"))
                        yield
                        yield from tail_pe(pe, i, S, t["tl"], 1, B_, A_)
                    with pe.Fori(0, TURNS) as i:
                        weave(body(w, i, SS[w], T[w]) for w in range(W))
                close_streams(SS, ctx=True)
                close_gathers(top_before)

        HEADS, HD = 16, 64
        INNER = HEADS * HD
        LT = SETB1[:, :].rearrange("p (b d) -> p b d", d=P)
        CNT = SETB2[:, :].rearrange("p (b d) -> p b d", d=P)

        def attention_2_norms(top_before):
            with ExitStack() as ph:
                SS = streams(pe=["turn_c", "turn_l"], act=["c_kept", "l_kept"], dve=["c", "l"], tail=False)
                T = [{"u": sb_in(ph, "u_rows2", [P, G, P]), "l": sb_in(ph, "latent_rows", [P, G, P]), "c": sb_in(ph, "ctx_normed", [P, G, P]),
                      "A": bank[2 * w], "B": bank[2 * w + 1]} for w in range(W)]
                st = norm_tiles(ph)
                block = ph.enter_context(nc.Block())

                @block.sync
                def _(sp):
                    load_expert_weights(sp, 2)

                @block.gpsimd
                def _(pool):
                    gather_turns(pool, top_before)

                @block.vector
                def _(dve):
                    ch = Chain(dve)

                    def last_turned(w):
                        dve.wait_ge(SS[w].pe.sem, turn_before(SS[w].PE, i))

                    def signal(name):
                        return lambda w, ins: ins.then_inc(SS[w].dve.sem, SS[w].DVE.tick(name))
                    with dve.Fori(0, TURNS) as i:
                        norm_all(dve, ch, st, lambda w: (lambda j: flat(CT[:, bass.ds((i * W + w) * G + j, 1), :])), lambda w: tile_in(T[w]["c"]),
                                 signal("c"), last_turned)
                        combine_turn(dve, ch, i, top_before)
                        norm_all(dve, ch, st, lambda w: x_tile(i * W + w), lambda w: tile_in(T[w]["u"]), lambda w, ins: None)
                        ch.link()
                        norm_all(dve, ch, st, lambda w: tile_in(T[w]["u"]), lambda w: tile_in(T[w]["l"]), signal("l"))
                        ch.link()

                @block.tensor
                def _(pe):
                    def body(w, i, S, t):
                        for src, b_, step, kept in (("c", t["A"], "turn_c", "c_kept"), ("l", t["B"], "turn_l", "l_kept")):
                            pe.wait_ge(S.dve.sem, S.DVE.at(i, src))
                            pe.wait_ge(S.act.sem, turn_before(S.ACT, i))
                            turn_group(pe, b_, tile_in(t[src])).then_inc(S.pe.sem, S.PE.tick(step))
                            yield
                    with pe.Fori(0, TURNS) as i:
                        weave(body(w, i, SS[w], T[w]) for w in range(W))

                @block.scalar
                def _(act):
                    def body(w, i, S, t):
                        for b_, dst, step, kept, at in ((t["A"], CNT, "turn_c", "c_kept", 2), (t["B"], LT, "turn_l", "l_kept", 4)):
                            act.wait_ge(S.pe.sem, S.PE.at(i, step))
                            act.activation(flat(group(dst, i * W + w)), b_[:, :], ACT.Identity, scale=cols[:, at:at + 1],
                                           bias=cols[:, at + 1:at + 2]).then_inc(S.act.sem, S.ACT.tick(kept))
                            yield
                    with act.Fori(0, TURNS) as i:
                        weave(body(w, i, SS[w], T[w]) for w in range(W))
                close_streams(SS)
                close_gathers(top_before)

        def attention_2():
            with ExitStack() as ph:
                wq = sb_in(ph, "wq", [P, INNER])
                wkv = sb_in(ph, "wkv", [P, 2 * INNER])
                wo = sb_in(ph, "wo", [P, INNER])
                kv_in = sb_in(ph, "kv_in", [P, 2, 2 * P])
                qT = SETA2[:, 2048:4096].rearrange("p (s c q) -> p s c q", s=2, c=8)
                kT = Y1[:, :, :].rearrange("p a d -> p (a d)").rearrange("p (s c k) -> p s c k", s=2, c=8)
                v = XN[:, :, :].rearrange("p a d -> p (a d)").rearrange("p (s t f) -> p s t f", s=2, t=2)
                probs = sb_in(ph, "probs2", [P, 2, 4, 256])
                pT = sb_in(ph, "probs_turned2", [P, 2, 2, 512])
                orow = spare[:, 0:INNER]
                oT = spare[:, INNER:2 * INNER]
                nmax = sb_in(ph, "neg_max2", [P, 4, 4])
                sums = sb_in(ph, "sums2", [P, HEADS])
                rinv = sb_in(ph, "rinv2", [P, HEADS])
                PEs = Steps(pe_done, ["S1", "OT1p", "T00", "Q0", "T01", "Q1", "PV0", "K0",
                                      "S2", "Yp", "T10", "K1", "T11", "K2", "PV1", "K3",
                                      "S3", "V0", "T20", "OT0", "T21", "V1", "PV2", "V2",
                                      "S0n", "V3", "T30", "T31", "PV3"])
                ACs = Steps(act_done, ["OT1p", "exp1", "T01", "Q1", "exp2", "T11", "K2", "V0", "exp3", "T21", "V1", "V3", "exp0n", "T31"])
                D = Steps(dve_done, ["max1", "T00", "Q0", "K0", "Yp", "max2", "T10", "K1", "O0", "K3",
                                     "max3", "T20", "OT0", "V2", "max0n", "T30", "O1"])
                FIRST = ["Q0", "Q1", "K0", "K1", "K2", "K3", "V0", "V1", "V2", "V3"]
                PE0, AC0, D0 = PEs.base, ACs.base, D.base
                PEs.base += len(FIRST) + 1
                ACs.base += 6
                D.base += 6
                PO = Steps(pool_done, ["kv_in"])
                block = ph.enter_context(nc.Block())
                PJ, BO, BT, BS = 0, 1, (2, 3), (4, 6)

                def cols_of_k(c):
                    return wkv[:, c * P:(c + 1) * P]

                @block.sync
                def _(sp):
                    sp.dma_start(wq[:, :], A["L2_xattn_Wq"]).then_inc(weights_x.sem, 16)
                    sp.dma_start(wkv[:, :], A["L2_xattn_Wkv"]).then_inc(weights_x.sem, 16)
                    sp.dma_start(wo[:, :].rearrange("p (c d) -> p c d", d=P), A["L2_xattn_Wo"].rearrange("(c p) d -> p c d", p=P)).then_inc(weights_x.sem, 16)

                @block.gpsimd
                def _(pool):
                    def copy(b, s):
                        pool.tensor_copy(kv_in[:, s, 0:P], flat(CNT[:, bass.ds(b, 1), :]))
                        pool.tensor_copy(kv_in[:, s, P:2 * P], flat(LT[:, bass.ds(b, 1), :])).then_inc(pool_done.sem, 1)
                    copy(0, 0)
                    copy(1, 1)
                    PO.seen = 1
                    with pool.Fori(1, B // 2) as i:
                        for s in range(2):
                            pool.wait_ge(pe_done.sem, (i * 2 + s - 3) * len(PEs.names) + (PEs.base + PEs.names.index("V3") + 1) if s == 1
                                         else (i * 2 - 2) * len(PEs.names) + PEs.base)
                            copy(i * 2 + s, s)

                def idle(eng, sem, S, name):
                    eng.drain().then_inc(sem, S.tick(name))

                PJ_ORDER = ["OT1p", "Q0", "Q1", "K0", "Yp", "K1", "K2", "K3", "V0", "OT0", "V1", "V2", "V3"]

                def pe_batch(pe, b, s, prev, nxt, mark):
                    def bank_free(name):
                        i = PJ_ORDER.index(name)
                        before = PJ_ORDER[i - 1]
                        t = b if i else b - 1
                        if i == 0 and isinstance(b, int) and b == 0:
                            return
                        if before in ACs.names:
                            pe.wait_ge(act_done.sem, ACs.at(t, before))
                        else:
                            pe.wait_ge(dve_done.sem, D.at(t, before))

                    def q_chunks(n, slot, name):
                        for c in range(4):
                            ins = pe.matmul(bank[PJ][:, c * P:(c + 1) * P], wq[:, (4 * n + c) * P:(4 * n + c + 1) * P], kv_in[:, slot, P:2 * P], start=True, stop=True)
                        return ins

                    def k_chunks(n, slot):
                        for c in range(2):
                            ins = pe.matmul(bank[PJ][:, c * 256:(c + 1) * 256], cols_of_k(2 * n + c), kv_in[:, slot, :], start=True, stop=True)
                        return ins

                    def v_rows(n, slot):
                        t, half = n // 2, n % 2
                        return pe.matmul(bank[PJ][:, :], kv_in[:, slot, t * P:(t + 1) * P], wkv[:, INNER + half * 512:INNER + (half + 1) * 512], start=True, stop=True)

                    def project(name):
                        make = {"Q": lambda n: q_chunks(n, 1 - s, name), "K": lambda n: k_chunks(n, 1 - s), "V": lambda n: v_rows(n, 1 - s)}
                        bank_free(name)
                        if nxt:
                            make[name[0]](int(name[1])).then_inc(pe_done.sem, PEs.tick(name))
                        else:
                            idle(pe, pe_done.sem, PEs, name)

                    def scores(u, slot, name):
                        for pp in range(2):
                            for par in range(2):
                                c = 2 * u + pp
                                ins = pe.matmul(bank[BS[u % 2] + par][:, pp * 256:(pp + 1) * 256], qT[par * HD:(par + 1) * HD, slot, c, :],
                                                kT[par * HD:(par + 1) * HD, slot, c, :], start=True, stop=True)
                        return ins

                    def turn_probs(u, pp, name):
                        for par in range(2):
                            for c in range(2):
                                ins = pe.transpose(bank[BT[pp]][:, (2 * par + c) * P:(2 * par + c + 1) * P], probs[:, u % 2, 2 * par + pp, c * P:(c + 1) * P], ident[:, :])
                        ins.then_inc(pe_done.sem, PEs.tick(name))

                    def mix(u):
                        if u % 2 == 0:
                            if u == 2:
                                pe.wait_ge(dve_done.sem, D.at(b, "O0"))
                            elif prev:
                                pe.wait_ge(dve_done.sem, D.at(b - 1, "O1"))
                        pe.wait_ge(dve_done.sem, D.at(b, f"T{u}0"))
                        pe.wait_ge(act_done.sem, ACs.at(b, f"T{u}1"))
                        for pp in range(2):
                            for par in range(2):
                                h = 4 * u + 2 * pp + par
                                for c in range(2):
                                    ins = pe.matmul(bank[BO][:, (h % 8) * HD:(h % 8 + 1) * HD], pT[:, u % 2, pp, (2 * par + c) * P:(2 * par + c + 1) * P],
                                                    v[:, s, c, h * HD:(h + 1) * HD], start=(c == 0), stop=(c == 1))
                        ins.then_inc(pe_done.sem, PEs.tick(f"PV{u}"))

                    def turn_out(half, name):
                        bank_free(name)
                        for c in range(4):
                            cc = 4 * half + c
                            ins = pe.transpose(bank[PJ][:, c * P:(c + 1) * P], orow[:, cc * P:(cc + 1) * P], ident[:, :])
                        ins.then_inc(pe_done.sem, PEs.tick(name))

                    def out_rows(name):
                        bank_free(name)
                        for c in range(8):
                            ins = pe.matmul(bank[PJ][:, 0:P], oT[:, c * P:(c + 1) * P], wo[:, c * P:(c + 1) * P], start=(c == 0), stop=(c == 7))
                        ins.then_inc(pe_done.sem, PEs.tick(name))

                    if mark == "first":
                        for i, name in enumerate(FIRST):
                            if i:
                                if (i - 1) % 2 == 0:
                                    pe.wait_ge(act_done.sem, AC0 + (i - 1) // 2 + 1)
                                else:
                                    pe.wait_ge(dve_done.sem, D0 + (i - 1) // 2 + 1)
                            n = int(name[1])
                            {"Q": lambda: q_chunks(n, 0, name), "K": lambda: k_chunks(n, 0), "V": lambda: v_rows(n, 0)}[name[0]]().then_inc(pe_done.sem, 1)
                        pe.wait_ge(dve_done.sem, D0 + 5)
                        scores(0, 0, "S0").then_inc(pe_done.sem, 1)
                        return
                    for u in range(4):
                        if u < 3:
                            scores(u + 1, s, None).then_inc(pe_done.sem, PEs.tick(f"S{u + 1}"))
                        elif nxt:
                            pe.wait_ge(dve_done.sem, D.at(b, "K3"))
                            pe.wait_ge(act_done.sem, ACs.at(b, "K2"))
                            scores(0, 1 - s, None).then_inc(pe_done.sem, PEs.tick("S0n"))
                        else:
                            idle(pe, pe_done.sem, PEs, "S0n")
                        if u == 0:
                            if prev:
                                pe.wait_ge(dve_done.sem, D.at(b - 1, "O1"))
                                turn_out(1, "OT1p")
                            else:
                                idle(pe, pe_done.sem, PEs, "OT1p")
                        elif u == 1:
                            if prev:
                                out_rows("Yp")
                            else:
                                idle(pe, pe_done.sem, PEs, "Yp")
                        elif u == 2:
                            project("V0")
                        else:
                            project("V3")
                        if u == 0:
                            if isinstance(b, int) and b == 0:
                                pe.wait_ge(act_done.sem, ACs.base)
                            else:
                                pe.wait_ge(act_done.sem, ACs.at(b - 1, "exp0n"))
                        else:
                            pe.wait_ge(act_done.sem, ACs.at(b, f"exp{u}"))
                        if u:
                            pe.wait_ge(dve_done.sem, D.at(b, f"T{u - 1}0"))
                        turn_probs(u, 0, f"T{u}0")
                        if u == 0:
                            project("Q0")
                        elif u == 1:
                            project("K1")
                        elif u == 2:
                            pe.wait_ge(dve_done.sem, D.at(b, "O0"))
                            turn_out(0, "OT0")
                        if u:
                            pe.wait_ge(act_done.sem, ACs.at(b, f"T{u - 1}1"))
                        turn_probs(u, 1, f"T{u}1")
                        if u < 3:
                            project(("Q1", "K2", "V1")[u])
                        mix(u)
                        if u < 3:
                            project(("K0", "K3", "V2")[u])
                    if mark == "last":
                        pe.wait_ge(dve_done.sem, D.at(b, "O1"))
                        for c in range(4):
                            ins = pe.transpose(bank[PJ][:, c * P:(c + 1) * P], orow[:, (4 + c) * P:(5 + c) * P], ident[:, :])
                        ins.then_inc(pe_done.sem, 1)
                        pe.wait_ge(act_done.sem, ACs.base + B * len(ACs.names) + 1)
                        for c in range(8):
                            ins = pe.matmul(bank[PJ][:, 0:P], oT[:, c * P:(c + 1) * P], wo[:, c * P:(c + 1) * P], start=(c == 0), stop=(c == 7))
                        ins.then_inc(pe_done.sem, 1)

                def kept(name, slot):
                    n = int(name[1])
                    if name[0] == "Q":
                        return qT[:, slot, 4 * n:4 * n + 4, :].rearrange("p c q -> p (c q)"), 0.125
                    if name[0] == "K":
                        return kT[:, slot, 2 * n:2 * n + 2, :].rearrange("p c k -> p (c k)"), None
                    return v[:, slot, n // 2, (n % 2) * 512:(n % 2 + 1) * 512], None

                def act_batch(act, b, s, prev, nxt, mark):
                    def keep(name):
                        if nxt:
                            act.wait_ge(pe_done.sem, PEs.at(b, name))
                            dst, scale = kept(name, 1 - s)
                            (act.mul(dst, bank[PJ][:, :], scale) if scale else act.copy(dst, bank[PJ][:, :])).then_inc(act_done.sem, ACs.tick(name))
                        else:
                            idle(act, act_done.sem, ACs, name)

                    def exps(u, tick):
                        for par in range(2):
                            for pp in range(2):
                                h = 4 * u + 2 * pp + par
                                ins = act.activation(probs[:, u % 2, 2 * par + pp, :], bank[BS[u % 2] + par][:, pp * 256:(pp + 1) * 256], ACT.Exp,
                                                     bias=nmax[:, u, 2 * par + pp:2 * par + pp + 1], accum_out=sums[:, h:h + 1])
                        ins.then_inc(act_done.sem, tick)

                    if mark == "first":
                        for i in range(0, 10, 2):
                            act.wait_ge(pe_done.sem, PE0 + i + 1)
                            dst, scale = kept(FIRST[i], 0)
                            (act.mul(dst, bank[PJ][:, :], scale) if scale else act.copy(dst, bank[PJ][:, :])).then_inc(act_done.sem, 1)
                        act.wait_ge(dve_done.sem, D0 + 6)
                        exps(0, 1)
                        return
                    for u in range(4):
                        if u == 0:
                            if prev:
                                act.wait_ge(pe_done.sem, PEs.at(b, "OT1p"))
                                act.copy(oT[:, 512:1024], bank[PJ][:, :]).then_inc(act_done.sem, ACs.tick("OT1p"))
                            else:
                                idle(act, act_done.sem, ACs, "OT1p")
                        elif u == 2:
                            keep("V0")
                        elif u == 3:
                            keep("V3")
                        if u < 3:
                            act.wait_ge(dve_done.sem, D.at(b, f"max{u + 1}"))
                            exps(u + 1, ACs.tick(f"exp{u + 1}"))
                        elif nxt:
                            act.wait_ge(dve_done.sem, D.at(b, "max0n"))
                            exps(0, ACs.tick("exp0n"))
                        else:
                            idle(act, act_done.sem, ACs, "exp0n")
                        act.wait_ge(pe_done.sem, PEs.at(b, f"T{u}1"))
                        act.copy(pT[:, u % 2, 1, :], bank[BT[1]][:, :]).then_inc(act_done.sem, ACs.tick(f"T{u}1"))
                        if u < 3:
                            keep(("Q1", "K2", "V1")[u])
                    if mark == "last":
                        act.wait_ge(pe_done.sem, PEs.base + B * len(PEs.names) + 1)
                        act.copy(oT[:, 512:1024], bank[PJ][:, :]).then_inc(act_done.sem, 1)

                def dve_batch(dve, ch, b, s, prev, nxt, mark):
                    def keep(name):
                        if nxt:
                            dve.wait_ge(pe_done.sem, PEs.at(b, name))
                            dst, scale = kept(name, 1 - s)
                            dve.tensor_scalar(dst, bank[PJ][:, :], scale or 1.0, None, ALU.mult).then_inc(dve_done.sem, D.tick(name))
                        else:
                            idle(dve, dve_done.sem, D, name)

                    def maxima(u, tick):
                        dve.tensor_reduce(nmax[:, u, :], ps[:, BS[u % 2]:BS[u % 2] + 2, :].rearrange("p r (h k) -> p (r h) k", k=256), AX.X, ALU.max,
                                          negate=True).then_inc(dve_done.sem, tick)

                    def heads_out(half, tick):
                        ch.link(dve.reciprocal(rinv[:, half * 8:half * 8 + 8], sums[:, half * 8:half * 8 + 8]))
                        dve.tensor_tensor(orow[:, half * 512:(half + 1) * 512].rearrange("p (h d) -> p h d", d=HD), bank[BO][:, :].rearrange("p (h d) -> p h d", d=HD),
                                          rinv[:, half * 8:half * 8 + 8].unsqueeze(2).to_broadcast([P, 8, HD]), ALU.mult).then_inc(dve_done.sem, tick)

                    def add_rows(bb, tick):
                        xt = flat(X[:, bass.ds(bb, 1), :])
                        dve.tensor_tensor(xt, xt, bank[PJ][:, 0:P], ALU.add).then_inc(dve_done.sem, tick)

                    if mark == "first":
                        for i in range(1, 10, 2):
                            dve.wait_ge(pe_done.sem, PE0 + i + 1)
                            dst, scale = kept(FIRST[i], 0)
                            dve.tensor_scalar(dst, bank[PJ][:, :], scale or 1.0, None, ALU.mult).then_inc(dve_done.sem, 1)
                        dve.wait_ge(pe_done.sem, PE0 + 11)
                        maxima(0, 1)
                        return
                    for u in range(4):
                        if u == 1:
                            if prev:
                                dve.wait_ge(pe_done.sem, PEs.at(b, "Yp"))
                                add_rows(b - 1, D.tick("Yp"))
                            else:
                                idle(dve, dve_done.sem, D, "Yp")
                        if u < 3:
                            dve.wait_ge(pe_done.sem, PEs.at(b, f"S{u + 1}"))
                            maxima(u + 1, D.tick(f"max{u + 1}"))
                        elif nxt:
                            dve.wait_ge(pe_done.sem, PEs.at(b, "S0n"))
                            maxima(0, D.tick("max0n"))
                        else:
                            idle(dve, dve_done.sem, D, "max0n")
                        dve.wait_ge(pe_done.sem, PEs.at(b, f"T{u}0"))
                        dve.tensor_copy(pT[:, u % 2, 0, :], bank[BT[0]][:, :]).then_inc(dve_done.sem, D.tick(f"T{u}0"))
                        if u < 2:
                            keep(("Q0", "K1")[u])
                        elif u == 2:
                            dve.wait_ge(pe_done.sem, PEs.at(b, "OT0"))
                            dve.tensor_copy(oT[:, 0:512], bank[PJ][:, :]).then_inc(dve_done.sem, D.tick("OT0"))
                        if u % 2 == 1:
                            dve.wait_ge(pe_done.sem, PEs.at(b, f"PV{u}"))
                            heads_out(u // 2, D.tick(f"O{u // 2}"))
                        if u < 3:
                            keep(("K0", "K3", "V2")[u])
                    if mark == "last":
                        dve.wait_ge(pe_done.sem, PEs.base + B * len(PEs.names) + 2)
                        add_rows(b, 1)

                def all_batches(eng, batch):
                    batch(0, 0, False, True, "first")
                    batch(0, 0, False, True, None)
                    with eng.Fori(0, B // 2 - 1) as i:
                        batch(i * 2 + 1, 1, True, True, None)
                        batch(i * 2 + 2, 0, True, True, None)
                    batch(B - 1, 1, True, False, "last")

                @block.tensor
                def _(pe):
                    pe.wait_ge(weights_x.sem, weights_x.value + 48)
                    pe.wait_ge(pool_done.sem, PO.base + 1)

                    def batch(b, s, prev, nxt, mark):
                        if nxt and mark != "first":
                            pe.wait_ge(pool_done.sem, PO.at(b + 1, "kv_in"))
                        pe_batch(pe, b, s, prev, nxt, mark)
                    all_batches(pe, batch)

                @block.scalar
                def _(act):
                    all_batches(act, lambda *a: act_batch(act, *a))

                @block.vector
                def _(dve):
                    ch = Chain(dve)
                    all_batches(dve, lambda *a: dve_batch(dve, ch, *a))
                for c in (PEs, ACs, D):
                    c.close(B)
                PO.close(B)
                pe_done.value += 2
                act_done.value += 1
                dve_done.value += 1
                weights_x.value += 48

        def tail_only(layer):
            with ExitStack() as ph:
                SS = streams()
                T = [{"tl": tail_tiles(ph, sb_in(ph, "tail_rows", [P, G, P]), sb_in(ph, "tail_turned", [P, G, P]))} for w in range(W)]
                st = norm_tiles(ph)
                block = ph.enter_context(nc.Block())

                @block.vector
                def _(dve):
                    ch = Chain(dve)
                    with dve.Fori(0, TURNS) as i:
                        tail_norms(dve, ch, i, SS, st, T, lambda w: dve.wait_ge(SS[w].act.sem, turn_before(SS[w].ACT, i)))
                        weave(tail_dve(dve, ch, i * W + w, i, SS[w], T[w]["tl"], bank[2 * w]) for w in range(W))

                @block.tensor
                def _(pe):
                    with pe.Fori(0, TURNS) as i:
                        weave(tail_pe(pe, i, SS[w], T[w]["tl"], layer, bank[2 * w + 1], bank[2 * w]) for w in range(W))

                @block.scalar
                def _(act):
                    with act.Fori(0, TURNS) as i:
                        weave(tail_act(act, i * W + w, i, SS[w], T[w]["tl"], bank[2 * w + 1]) for w in range(W))
                close_streams(SS)

        def attention_3(top_before):
            SCALE = float(P) ** -0.5
            with ExitStack() as ph:
                SS = streams(pe=["k", "turn_u", "q", "scores", "turn_p", "mixed"],
                             act=["k_kept", "u_turned", "q_kept", "exp", "p_turned"], dve=["u_normed", "max"])
                T = []
                for w in range(W):
                    t = {"kT": carve(SETA1, 2 * w * G * P, [P, G, P]), "qT": carve(SETA1, (2 * w + 1) * G * P, [P, G, P]),
                         "probs": carve(SETA2, 2 * w * G * P, [P, G, P]), "probsT": carve(SETA2, (2 * w + 1) * G * P, [P, G, P]),
                         "u": sb_in(ph, "u_rows3", [P, G, P]), "uT": sb_in(ph, "u_turned3", [P, G, P]),
                         "sums": sb_in(ph, "sums3", [P, G]), "nmax": sb_in(ph, "neg_max3", [P, G]), "rinv": sb_in(ph, "rinv3", [P, G]),
                         "A": bank[2 * w], "B": bank[2 * w + 1]}
                    t["tl"] = tail_tiles(ph, t["u"], t["uT"])
                    T.append(t)
                st = norm_tiles(ph)
                mask_here = masks_loaded.value + 16
                block = ph.enter_context(nc.Block())

                @block.sync
                def _(sp):
                    sp.dma_start(mask[:, :], mask_dram[1:2, :]).then_inc(masks_loaded.sem, 16)

                @block.gpsimd
                def _(pool):
                    gather_turns(pool, top_before)

                @block.tensor
                def _(pe):
                    def body(w, i, S, t):
                        g, A_, B_ = i * W + w, t["A"], t["B"]
                        pe.wait_ge(S.dve.sem, turn_before(S.DVE, i))
                        pe.matmul(A_[:, :], wsmall[:, 7, :], flat(group(CTT, g)), start=True, stop=True).then_inc(S.pe.sem, S.PE.tick("k"))
                        yield
                        pe.wait_ge(S.dve.sem, S.DVE.at(i, "u_normed"))
                        turn_group(pe, B_, tile_in(t["u"])).then_inc(S.pe.sem, S.PE.tick("turn_u"))
                        yield
                        pe.wait_ge(S.act.sem, S.ACT.at(i, "u_turned"))
                        pe.matmul(B_[:, :], wsmall[:, 6, :], flat(t["uT"][:, :, :]), start=True, stop=True).then_inc(S.pe.sem, S.PE.tick("q"))
                        pe.matmul(A_[:, :], ones[0:1, :], mask[:, bass.ds(g * (G * P), G * P)], start=True, stop=False, skip_group_check=True)
                        yield
                        pe.wait_ge(S.act.sem, S.ACT.at(i, "q_kept"))
                        for j in range(G):
                            ins = pe.matmul(A_[:, j * P:(j + 1) * P], t["qT"][:, j, :], t["kT"][:, j, :], start=False, stop=True, skip_group_check=True)
                        ins.then_inc(S.pe.sem, S.PE.tick("scores"))
                        yield
                        pe.wait_ge(S.act.sem, S.ACT.at(i, "exp"))
                        turn_group(pe, B_, tile_in(t["probs"])).then_inc(S.pe.sem, S.PE.tick("turn_p"))
                        yield
                        pe.wait_ge(S.act.sem, S.ACT.at(i, "p_turned"))
                        for j in range(G):
                            ins = pe.matmul(A_[:, j * P:(j + 1) * P], t["probsT"][:, j, :], flat(CT[:, bass.ds(g * G + j, 1), :]), start=True, stop=True)
                        ins.then_inc(S.pe.sem, S.PE.tick("mixed"))
                        yield
                        yield from tail_pe(pe, i, S, t["tl"], 3, B_, A_)
                    pe.wait_ge(masks_loaded.sem, mask_here)
                    with pe.Fori(0, TURNS) as i:
                        weave(body(w, i, SS[w], T[w]) for w in range(W))

                @block.scalar
                def _(act):
                    def body(w, i, S, t):
                        g, A_, B_ = i * W + w, t["A"], t["B"]
                        act.wait_ge(S.pe.sem, S.PE.at(i, "k"))
                        act.activation(flat(t["kT"]), A_[:, :], ACT.Identity, bias=cols[:, 1:2]).then_inc(S.act.sem, S.ACT.tick("k_kept"))
                        yield
                        act.wait_ge(S.pe.sem, S.PE.at(i, "turn_u"))
                        act.copy(flat(t["uT"][:, :, :]), B_[:, :]).then_inc(S.act.sem, S.ACT.tick("u_turned"))
                        yield
                        act.wait_ge(S.pe.sem, S.PE.at(i, "q"))
                        act.activation(flat(t["qT"]), B_[:, :], ACT.Identity, bias=cols[:, 0:1]).then_inc(S.act.sem, S.ACT.tick("q_kept"))
                        yield
                        act.wait_ge(S.dve.sem, S.DVE.at(i, "max"))
                        for j in range(G):
                            ins = act.activation(t["probs"][:, j, :], A_[:, j * P:(j + 1) * P], ACT.Exp, bias=t["nmax"][:, j:j + 1], scale=SCALE, accum_out=t["sums"][:, j:j + 1])
                        ins.then_inc(S.act.sem, S.ACT.tick("exp"))
                        yield
                        act.wait_ge(S.pe.sem, S.PE.at(i, "turn_p"))
                        act.copy(flat(t["probsT"]), B_[:, :]).then_inc(S.act.sem, S.ACT.tick("p_turned"))
                        yield
                        yield from tail_act(act, g, i, S, t["tl"], B_)
                    with act.Fori(0, TURNS) as i:
                        weave(body(w, i, SS[w], T[w]) for w in range(W))

                @block.vector
                def _(dve):
                    ch = Chain(dve)

                    def body(w, i, S, t):
                        g, A_ = i * W + w, t["A"]
                        dve.wait_ge(S.pe.sem, S.PE.at(i, "scores"))
                        ch.link(dve.tensor_reduce(t["nmax"][:, :], A_[:, :].rearrange("p (j l) -> p j l", j=G), AX.X, ALU.max, negate=True))
                        dve.tensor_scalar(t["nmax"][:, :], t["nmax"][:, :], SCALE, None, ALU.mult).then_inc(S.dve.sem, S.DVE.tick("max"))
                        yield
                        dve.wait_ge(S.act.sem, S.ACT.at(i, "exp"))
                        ch.link(dve.reciprocal(t["rinv"][:, :], t["sums"][:, :]))
                        yield
                        dve.wait_ge(S.pe.sem, S.PE.at(i, "mixed"))
                        for j in range(G):
                            xt = x_tile(g)(j)
                            dve.scalar_tensor_tensor(xt, A_[:, j * P:(j + 1) * P], t["rinv"][:, j:j + 1], xt, ALU.mult, ALU.add)
                        yield
                    with dve.Fori(0, TURNS) as i:
                        combine_turn(dve, ch, i, top_before)
                        norm_all(dve, ch, st, lambda w: x_tile(i * W + w), lambda w: tile_in(T[w]["u"]),
                                 lambda w, ins: ins.then_inc(SS[w].dve.sem, SS[w].DVE.tick("u_normed")),
                                 lambda w: dve.wait_ge(SS[w].act.sem, turn_before(SS[w].ACT, i)))
                        weave(body(w, i, SS[w], T[w]) for w in range(W))
                        ch.link()
                        tail_norms(dve, ch, i, SS, st, T)
                        weave(tail_dve(dve, ch, i * W + w, i, SS[w], T[w]["tl"], T[w]["A"]) for w in range(W))
                close_streams(SS)
                close_gathers(top_before)

        route(0, 2, 0)
        experts(0)
        attention_1(2)
        route(1, 2, CAPACITY)
        experts(1)
        attention_2_norms(2)
        attention_2()
        tail_only(2)
        route(2, 2, 0)
        experts(2)
        attention_3(2)
        route(3, 1, 0)
        experts(3)
        combine_only(1)


        with nc.Block() as block:
            @block.sync
            def _(sp):
                sp.dma_start(out.rearrange("t p d -> p t d"), X[:, :, :]).then_inc(stored.sem, 16)
                sp.wait_ge(stored.sem, 16)


_INS = ['x', 'ctx_1024', 'mask_BxS2_if1', 'mask_BxS2_ik1', 'L0_xattn_W0', 'L0_xattn_W1', 'L0_ffn_router_w', 'L0_ffn_w1', 'L0_ffn_b1', 'L0_ffn_w2', 'L0_ffn_b2', 'L1_xattn_Wq', 'L1_xattn_bq', 'L1_xattn_Wk', 'L1_xattn_bk', 'L1_xattn_Wv', 'L1_xattn_bv', 'L1_xattn_Wp', 'L1_xattn_bp', 'L1_ffn_router_w', 'L1_ffn_router_b', 'L1_ffn_W', 'L1_ffn_V', 'L1_ffn_W_out', 'L2_xattn_ln1_w', 'L2_xattn_ln1_b', 'L2_xattn_ln2_w', 'L2_xattn_ln2_b', 'L2_xattn_Wq', 'L2_xattn_Wkv', 'L2_xattn_Wo', 'L2_ffn_gate_w', 'L2_ffn_gate_up_w', 'L2_ffn_down_w', 'L3_xattn_Wq_w', 'L3_xattn_Wq_b', 'L3_xattn_Wk_w', 'L3_xattn_Wk_b', 'L3_ffn_gate_w', 'L3_ffn_w1', 'L3_ffn_b1', 'L3_ffn_w2', 'L3_ffn_b2']


def kernel(**inputs):
    import numpy as _np
    import concourse.bacc as _bacc
    from concourse import mybir as _mybir
    from concourse.bass_utils import run_bass_kernel_spmd as _run

    nc = _bacc.Bacc("TRN2", target_bir_lowering=False, num_devices=1)
    arrays, handles = {}, {}
    for name in _INS:
        a = _np.ascontiguousarray(inputs[name])
        arrays[f"in_{name}_dram"] = a
        handles[name] = nc.dram_tensor(f"in_{name}_dram", a.shape, _mybir.dt.from_np(a.dtype), kind="ExternalInput").ap()
    out = nc.dram_tensor("out_0_dram", (B, P, P), _mybir.dt.float32, kind="ExternalOutput").ap()
    build(nc, handles, out)
    r = _run(nc, [arrays], core_ids=[0])
    return r.results[0]["out_0_dram"]
```

```python
from contextlib import ExitStack

import concourse.bass as bass
from concourse import mybir
import numpy as np

ALU = mybir.AluOpType
ACT = mybir.ActivationFunctionType
AX = mybir.AxisListType
F32 = mybir.dt.float32
BF16 = mybir.dt.bfloat16
I32 = mybir.dt.int32
U32 = mybir.dt.uint32
F32R = mybir.dt.float32r

P = 128
B = 32
G = 4
NG = B // G
E = 8
H1 = 512
EPS = 1e-5
assert B * P <= 1 << 12
MASKED = -1e30
FAR = 1.0e6
CAPACITY = 256
RSQRT_SEED = 1597463007.0

TILES_TOP2 = (2 * B * P + E * (P - 1)) // P + 1
TILES_TOP1 = (B * P + E * (P - 1)) // P + 1
TILES_CAP = E * CAPACITY // P

BIAS_PARTS = [("L0_ffn_b1", E * H1), ("L3_ffn_b1", E * H1), ("L0_ffn_b2", E * P), ("L3_ffn_b2", E * P),
              ("L1_xattn_bq", P), ("L1_xattn_bk", P), ("L1_xattn_bv", P), ("L1_xattn_bp", P)]
BIAS_AT = {}
_at = 0
for _n, _w in BIAS_PARTS:
    BIAS_AT[_n] = (_at, _w)
    _at += _w
BIAS_WIDTH = _at
ROUTER_B_AT = BIAS_WIDTH
BIAS_TOTAL = BIAS_WIDTH + P


class Steps:

    def __init__(self, counter, names):
        self.base, self.names = counter.value, names
        self.counter, self.seen = counter, 0

    def tick(self, name):
        assert self.names[self.seen % len(self.names)] == name, (name, self.names[self.seen % len(self.names)])
        self.seen += 1
        return 1

    def at(self, turn, name):
        return turn * len(self.names) + (self.base + self.names.index(name) + 1)

    def close(self, turns):
        assert self.names == [] or (self.seen and self.seen % len(self.names) == 0), (self.seen, len(self.names))
        self.counter.value = self.base + turns * len(self.names)


class Chain:

    def __init__(self, eng):
        self.eng = eng

    def link(self, ins=None):
        self.eng.drain()


class Counter:
    def __init__(self, sem):
        self.sem, self.value = sem, 0


def weave(bodies):
    bodies = list(bodies)
    while bodies:
        bodies = [b for b in bodies if next(b, "end") != "end"]


class Stream:

    def __init__(self, counters, pe=(), act=(), dve=(), pool=()):
        self.pe, self.act, self.dve, self.pool = counters
        self.PE, self.ACT, self.DVE, self.POOL = (Steps(c, n) for c, n in zip(counters, (pe, act, dve, pool)))

    def close(self, turns):
        for steps in (self.PE, self.ACT, self.DVE, self.POOL):
            steps.close(turns)


def build(nc, A, out):
    with ExitStack() as top:
        names = set()

        def sb_in(ctx, name, shape, dt=F32):
            while name in names:
                name += "_"
            names.add(name)
            return ctx.enter_context(nc.sbuf_tensor(name, shape, dt))

        def sb(name, shape, dt=F32):
            return sb_in(top, name, shape, dt)

        def counter(name):
            return Counter(top.enter_context(nc.semaphore(name)))

        ps = top.enter_context(nc.psum_tensor("psum_banks", [P, 8, 512], F32))
        bank = [ps[:, i, :] for i in range(8)]

        X = sb("x_rows", [P, B, P])
        XN = sb("normed_rows", [P, B, P])
        Y1 = sb("gathered_rows", [P, B, P])
        CT = sb("ctx_rows", [P, B, P])
        CTT = sb("ctx_turned", [P, B, P])
        SETA1 = sb("expert_w1_a", [P, E * H1])
        SETA2 = sb("expert_w2_a", [P, E * H1])
        SETB = sb("expert_w_b", [P, 2 * E * H1])
        SETB1, SETB2 = SETB[:, 0:E * H1], SETB[:, E * H1:2 * E * H1]
        ident = sb("ident", [P, P])
        tri = sb("tri", [P, P], BF16)
        ones = sb("ones", [P, P], BF16)
        iota8 = sb("iota8", [P, E])
        blocks = sb("head_blocks", [P, P + 16])
        wsmall = sb("wsmall", [P, 8, P])
        router = sb("router", [P, 4, E])
        rows3 = sb("bias_rows", [3, 2 * E * P + 4 * P + P], BF16)
        cols = sb("bias_cols", [P, 6])
        MX = sb("top_logits", [P, B, E])
        IX = sb("top_experts", [P, B, E])
        LG = sb("logits", [P, B, E])
        POS = sb("slots", [P, 2, B], U32)
        SOURCE = sb("source_rows", [P, TILES_TOP2], U32)
        WT = sb("mix_weights", [P, 2, B])
        tile_expert = sb("tile_expert", [1, TILES_TOP2], I32)
        iota_tile = sb("iota_tile", [P, TILES_TOP2])
        iota_slot = sb("iota_slot", [P, P])
        row_number = sb("row_number", [P, B])

        mask = sb("mask_row", [1, B * P], BF16)
        xn = nc.dram_tensor("normed_rows_dram", [B * P, P], F32).ap()
        ys = nc.dram_tensor("expert_rows", [TILES_TOP2 * P, P], F32).ap()
        bias_dram = nc.dram_tensor("bias_split", [3, BIAS_TOTAL], BF16).ap()
        mask_dram = nc.dram_tensor("mask_rows", [2, B * P], BF16).ap()

        loaded = counter("loaded")
        x_loaded = counter("x_loaded")
        ctx_loaded = counter("ctx_loaded")
        masks_loaded = counter("masks_loaded")
        W = 4
        stream_counters = [[counter(f"{n}{w}") for n in ("pe_step", "act_step", "dve_step", "pool_step")] for w in range(W)]
        ctx_copied = [counter(f"ctx_copied{w}") for w in range(W)]
        pe_done = counter("pe_done")
        act_done = counter("act_done")
        dve_done = counter("dve_done")
        pool_done = counter("pool_done")
        bias_stored = counter("bias_stored")
        rows_loaded = counter("rows_loaded")
        rows_stored = counter("rows_stored")
        tiles_marked = counter("tiles_marked")
        pairs_made = counter("pairs_made")
        pairs_summed = counter("pairs_summed")
        gathered = [counter("gathered_even"), counter("gathered_odd")]
        rows_here = counter("rows_here")
        sorted_in = [counter(f"sorted_in{i}") for i in range(4)]
        expert_out = [counter(f"expert_out{i}") for i in range(4)]
        rows_turned = counter("rows_turned")
        hidden_made = counter("hidden_made")
        hidden_turned = counter("hidden_turned")
        expert_made = counter("expert_made")
        rows_turned_kept = counter("rows_turned_kept")
        gates_kept = counter("gates_kept")
        hidden_kept = counter("hidden_kept")
        hidden_turned_kept = counter("hidden_turned_kept")
        expert_kept = counter("expert_kept")
        combined = counter("combined")
        stored = counter("stored")
        weights_a = counter("weights_a")
        weights_b = counter("weights_b")
        weights_x = counter("weights_x")
        y_turned = counter("y_turned")
        y_hi = counter("y_hi")
        y_kept = counter("y_kept")
        y_added = counter("y_added")

        def group(t, g):
            return t[:, bass.ds(g * G, G), :]

        def flat(ap):
            return ap.rearrange("p a d -> p (a d)")

        with ExitStack() as ph:
            wraw = sb_in(ph, "small_raw", [P, 6, P])
            rraw = sb_in(ph, "router_raw", [E, 2, P])
            NBC = BIAS_TOTAL // P
            braw = sb_in(ph, "bias_raw", [P, NBC])
            bres = sb_in(ph, "bias_rest", [P, 2, NBC])
            bsp = sb_in(ph, "bias_split_sb", [P, 3, NBC], BF16)
            mraw = sb_in(ph, "mask_raw", [P, 2, B], I32)
            mbf = sb_in(ph, "mask_bf", [P, 2, B], BF16)
            block = ph.enter_context(nc.Block())
            n_loads = 0

            @block.sync
            def _(sp):
                nonlocal n_loads

                def load(dst, src):
                    nonlocal n_loads
                    sp.dma_start(dst, src).then_inc(loaded.sem, 16)
                    n_loads += 1
                sp.wait_ge(dve_done.sem, 1)
                for name, width in BIAS_PARTS:
                    at = BIAS_AT[name][0] // P
                    src = A[name] if len(A[name].shape) == 1 else A[name].rearrange("e f -> (e f)")
                    load(braw[:, at:at + width // P], src.rearrange("(p c) -> p c", p=P))
                load(braw[0:E, NBC - 1:NBC], A["L1_ffn_router_b"].rearrange("(e a) -> e a", a=1))
                for m, name in enumerate(("mask_BxS2_if1", "mask_BxS2_ik1")):
                    load(mraw[:, m, :], A[name].rearrange("b (q c) -> (b q) c", c=B))
                for i, name in enumerate(("L1_xattn_Wq", "L1_xattn_Wk", "L1_xattn_Wv", "L1_xattn_Wp",
                                          "L3_xattn_Wq_w", "L3_xattn_Wk_w")):
                    load(wraw[:, i, :], A[name])
                load(wsmall[:, 0, :], A["L0_xattn_W0"])
                load(wsmall[:, 1, :], A["L0_xattn_W1"])
                load(rraw[:, 0, :], A["L0_ffn_router_w"])
                load(rraw[:, 1, :], A["L1_ffn_router_w"])
                load(router[:, 2, :], A["L2_ffn_gate_w"])
                load(router[:, 3, :], A["L3_ffn_gate_w"])
                for i, name in enumerate(("L3_xattn_Wq_b", "L3_xattn_Wk_b", "L2_xattn_ln1_w", "L2_xattn_ln1_b",
                                          "L2_xattn_ln2_w", "L2_xattn_ln2_b")):
                    load(cols[:, i:i + 1], A[name].rearrange("(p a) -> p a", a=1))
                sp.wait_ge(dve_done.sem, 4)
                for k in range(3):
                    for name, width in BIAS_PARTS + [("router_b", P)]:
                        at = BIAS_AT.get(name, (ROUTER_B_AT,))[0]
                        sp.dma_start(bias_dram[k, at:at + width].rearrange("(p c) -> p c", p=P),
                                     bsp[:, k, at // P:(at + width) // P]).then_inc(bias_stored.sem, 16)
                for m in range(2):
                    sp.dma_start(mask_dram[m, :].rearrange("(p c) -> p c", p=P), mbf[:, m, :]).then_inc(bias_stored.sem, 16)
                sp.wait_ge(bias_stored.sem, 16 * (3 * (len(BIAS_PARTS) + 1) + 2))
                sp.dma_start(mask[:, :], mask_dram[0:1, :]).then_inc(masks_loaded.sem, 16)
                at = BIAS_AT["L0_ffn_b2"][0]
                sp.dma_start(rows3[:, :], bias_dram[:, at:at + 2 * E * P + 5 * P]).then_inc(rows_loaded.sem, 16)
                sp.dma_start(SETB1[:, :].rearrange("p (c h) -> p c h", h=P), A["L0_ffn_w1"].rearrange("e (c p) h -> p (e c) h", p=P)).then_inc(weights_b.sem, 16)
                sp.dma_start(SETB2[:, :].rearrange("p (e f) -> p e f", e=E), A["L0_ffn_w2"].rearrange("e h f -> h e f")).then_inc(weights_b.sem, 16)

            @block.gpsimd
            def _(pool):
                for c in stream_counters:
                    pool.drain().then_inc(c[3].sem, 1)
                pool.memset(blocks[:, :], 1.0).then_inc(pool_done.sem, 1)
                pool.wait_ge(pool_done.sem, 1)
                for base, sign in ((0, 1), (7, -1)):
                    pool.affine_select(out=blocks[:, 0:P].rearrange("p (h c) -> p h c", c=8), in_=blocks[:, 0:P].rearrange("p (h c) -> p h c", c=8),
                                       compare_op=ALU.is_ge, fill=0.0, base=base, pattern=[[-8 * sign, 16], [0, 8]], channel_multiplier=sign)
                    pool.affine_select(out=blocks[:, P:P + 16], in_=blocks[:, P:P + 16], compare_op=ALU.is_ge, fill=0.0, base=base,
                                       pattern=[[-8 * sign, 16]], channel_multiplier=sign).then_inc(pool_done.sem, 1)
                    pool.wait_ge(pool_done.sem, 2 if sign == 1 else 3)
                pool.memset(ident[:, :], 0.0).then_inc(pool_done.sem, 1)
                pool.memset(tri[:, :], 1.0).then_inc(pool_done.sem, 1)
                pool.iota(iota8[:, :], [[1, E]], base=0, channel_multiplier=0,
                          allow_small_or_imprecise_dtypes=True).then_inc(pool_done.sem, 1)
                pool.iota(iota_tile[:, :], [[1, TILES_TOP2]], base=0, channel_multiplier=0,
                          allow_small_or_imprecise_dtypes=True).then_inc(pool_done.sem, 1)
                pool.iota(iota_slot[:, :], [[1, P]], base=0, channel_multiplier=0, allow_small_or_imprecise_dtypes=True)
                pool.iota(row_number[:, :], [[P, B]], base=0, channel_multiplier=1, allow_small_or_imprecise_dtypes=True)
                pool.wait_ge(pool_done.sem, 7)
                pool.affine_select(out=ident[:, :], in_=ident[:, :], compare_op=ALU.not_equal, fill=1.0, base=0,
                                   pattern=[[-1, P]], channel_multiplier=1).then_inc(pool_done.sem, 1)
                pool.affine_select(out=tri[:, :], in_=tri[:, :], compare_op=ALU.is_gt, fill=0.0, base=0,
                                   pattern=[[1, P]], channel_multiplier=-1).then_inc(pool_done.sem, 1)

            @block.vector
            def _(dve):
                for c in stream_counters:
                    dve.drain().then_inc(c[2].sem, 1)
                dve.memset(braw[:, :], 0.0).then_inc(dve_done.sem, 1)
                dve.memset(ones[:, :], 1.0).then_inc(dve_done.sem, 1)
                ch = Chain(dve)
                dve.wait_ge(loaded.sem, 16 * n_loads)
                for m in range(2):
                    ins = dve.tensor_scalar(mbf[:, m, :], mraw[:, m, :], 0.0, MASKED, ALU.is_equal, ALU.mult)
                ins.then_inc(dve_done.sem, 1)
                ch.link(dve.tensor_copy(bsp[:, 0, :], braw[:, :]))
                ch.link(dve.tensor_tensor(bres[:, 0, :], braw[:, :], bsp[:, 0, :], ALU.subtract))
                ch.link(dve.tensor_copy(bsp[:, 1, :], bres[:, 0, :]))
                ch.link(dve.tensor_tensor(bres[:, 1, :], bres[:, 0, :], bsp[:, 1, :], ALU.subtract))
                dve.tensor_copy(bsp[:, 2, :], bres[:, 1, :]).then_inc(dve_done.sem, 1)

            @block.tensor
            def _(pe):
                for c in stream_counters:
                    pe.drain().then_inc(c[0].sem, 1)
                pe.wait_ge(pool_done.sem, 9)
                pe.wait_ge(loaded.sem, 16 * n_loads)
                for i in range(6):
                    ins = pe.transpose(bank[i // 4][:, (i % 4) * P:(i % 4 + 1) * P], wraw[:, i, :], ident[:, :])
                for i in range(2):
                    ins = pe.transpose(bank[2][:, i * E:(i + 1) * E], rraw[:, i, :], ident[0:E, 0:E])
                ins.then_inc(pe_done.sem, 1)

            @block.scalar
            def _(act):
                for c in stream_counters:
                    act.drain().then_inc(c[1].sem, 1)
                act.dma_start(CT[:, :, :], A["ctx_1024"].rearrange("t p d -> p t d")).then_inc(ctx_loaded.sem, 16)
                act.dma_start(X[:, :, :], A["x"].rearrange("t p d -> p t d")).then_inc(x_loaded.sem, 16)
                act.wait_ge(pe_done.sem, 1)
                act.copy(flat(wsmall[:, 2:6, :]), bank[0][:, :])
                act.copy(flat(wsmall[:, 6:8, :]), bank[1][:, 0:2 * P])
                act.copy(flat(router[:, 0:2, :]), bank[2][:, 0:2 * E]).then_inc(act_done.sem, 1)
        loaded.value = 16 * n_loads
        pe_done.value, act_done.value, dve_done.value, pool_done.value = 1, 1, 4, 9
        bias_stored.value = 16 * (3 * (len(BIAS_PARTS) + 1) + 2)
        rows_loaded.value, masks_loaded.value = 16, 16
        for cs in stream_counters:
            for c in cs:
                c.value = 1
        weights_b.value = 32

        R_B2 = {"L0": 0, "L3": E * P}
        R_SMALL = 2 * E * P
        R_ROUTER = R_SMALL + 4 * P

        def norm_scales(ch, dve, var, rstd, work):
            half, sq = work[:, 0, :], work[:, 1, :]
            bits = work[:, 2, :].bitcast(I32)
            ch.link(dve.tensor_scalar(sq, var, EPS, None, ALU.add))
            dve.tensor_scalar(half, sq, -0.5, None, ALU.mult)
            ch.link(dve.tensor_scalar(bits, sq.bitcast(I32), 1, None, ALU.logical_shift_right))
            ch.link(dve.tensor_scalar(rstd.bitcast(I32), bits, -1.0, RSQRT_SEED, ALU.mult, ALU.add))
            for _ in range(3):
                ch.link(dve.tensor_tensor(sq, rstd, rstd, ALU.mult))
                ch.link(dve.tensor_tensor(sq, sq, half, ALU.mult))
                ch.link(dve.scalar_tensor_tensor(rstd, sq, 1.5, rstd, ALU.add, ALU.mult))

        def norm_all(dve, ch, st, src, dst, signal, free=None):
            for w in range(W):
                for j in range(G):
                    dve.bn_stats(st["stats"][:, w * G + j, :], src(w)(j))
            ch.link()
            for j in range(W * G):
                dve.bn_aggr(st["mv"][:, j, :], st["stats"][:, j, :])
            ch.link()
            norm_scales(ch, dve, st["mv"][:, :, 1], st["rstd"][:, :], st["work"])
            for w in range(W):
                if free:
                    free(w)
                for j in range(G):
                    n = w * G + j
                    ins = dve.tensor_scalar(dst(w)(j), src(w)(j), st["mv"][:, n, 0:1], st["rstd"][:, n:n + 1],
                                            ALU.subtract, ALU.mult)
                signal(w, ins)

        def combine_turn(dve, ch, i, slots):
            for w in range(W):
                dve.wait_ge(rows_here.sem, i * W + (w + rows_here.value + 1))
                combine(dve, ch, i * W + w, slots)

        def close_streams(SS, ctx=False):
            for w, S in enumerate(SS):
                S.close(TURNS)
                if ctx:
                    ctx_copied[w].value += TURNS

        def combine(dve, ch, g, slots):
            for k in range(slots):
                for j in range(G):
                    t = g * G + j
                    xt = flat(X[:, bass.ds(t, 1), :])
                    ins = dve.scalar_tensor_tensor(xt, flat((XN, Y1)[k][:, bass.ds(t, 1), :]), WT[:, k, bass.ds(t, 1)], xt,
                                                   ALU.mult, ALU.add)
                ch.link(ins)

        def x_tile(g):
            return lambda j: flat(X[:, bass.ds(g * G + j, 1), :])

        def tile_in(t):
            return lambda j: t[:, j, :]

        TAIL = dict(pe=["turn_tail", "logits"], act=["tail_turned", "tail_kept"], dve=["tail_normed", "logits_kept"])

        def norm_tiles(ph):
            return {"stats": sb_in(ph, "norm_stats", [P, W * G, 6]), "mv": sb_in(ph, "mean_var", [P, W * G, 2]),
                    "rstd": sb_in(ph, "rstd", [P, W * G]), "work": sb_in(ph, "newton", [P, 3, W * G])}

        def tail_tiles(ph, rows, turned):
            return {"rows": rows, "turned": turned, "mx": sb_in(ph, "tail_max", [P, G, E]),
                    "ix": sb_in(ph, "tail_index", [P, G, E], U32), "lg": sb_in(ph, "tail_logits", [P, G, E])}

        def tail_norms(dve, ch, i, SS, st, T, free=None):
            norm_all(dve, ch, st, lambda w: x_tile(i * W + w), lambda w: tile_in(T[w]["tl"]["rows"]),
                     lambda w, ins: ins.then_inc(SS[w].dve.sem, SS[w].DVE.tick("tail_normed")), free)

        def tail_dve(dve, ch, g, i, S, tl, logits_bank):
            dve.wait_ge(S.pe.sem, S.PE.at(i, "logits"))
            ch.link(dve.tensor_copy(flat(tl["lg"][:, :, :]), logits_bank[:, 0:G * E]))
            for j in range(G):
                ins = dve.max(tl["mx"][:, j, :], tl["lg"][:, j, :])
            ch.link(ins)
            for j in range(G):
                ins = dve.max_index(tl["ix"][:, j, :], tl["mx"][:, j, :], tl["lg"][:, j, :])
            dve.tensor_copy(flat(group(MX, g)), flat(tl["mx"][:, :, :]))
            dve.tensor_copy(flat(group(LG, g)), flat(tl["lg"][:, :, :]))
            ch.link()
            dve.tensor_copy(flat(group(IX, g)), flat(tl["ix"][:, :, :])).then_inc(S.dve.sem, S.DVE.tick("logits_kept"))
            yield

        def tail_pe(pe, i, S, tl, layer, turn_bank, logits_bank):
            pe.wait_ge(S.dve.sem, S.DVE.at(i, "tail_normed"))
            for j in range(G):
                ins = pe.transpose(turn_bank[:, j * P:(j + 1) * P], tl["rows"][:, j, :], ident[:, :])
            ins.then_inc(S.pe.sem, S.PE.tick("turn_tail"))
            yield
            pe.wait_ge(S.act.sem, S.ACT.at(i, "tail_turned"))
            if layer == 1:
                for j in range(G):
                    pe.matmul(logits_bank[:, j * E:(j + 1) * E], ones[0:3, :], rows3[:, R_ROUTER:R_ROUTER + E],
                              start=(j == 0), stop=False, skip_group_check=True)
            for j in range(G):
                ins = pe.matmul(logits_bank[:, j * E:(j + 1) * E], tl["turned"][:, j, :], router[:, layer, :],
                                start=(layer != 1 and j == 0), stop=True, skip_group_check=True)
            ins.then_inc(S.pe.sem, S.PE.tick("logits"))
            yield

        def tail_act(act, g, i, S, tl, turn_bank):
            act.wait_ge(S.pe.sem, S.PE.at(i, "turn_tail"))
            act.copy(flat(tl["turned"][:, :, :]), turn_bank[:, :]).then_inc(S.act.sem, S.ACT.tick("tail_turned"))
            yield
            act.copy(flat(group(XN, g)), flat(tl["rows"][:, :, :])).then_inc(S.act.sem, S.ACT.tick("tail_kept"))
            yield

        def turn_before(steps, i):
            return i * len(steps.names) + steps.base

        def streams(pe=(), act=(), dve=(), pool=(), tail=True):
            t = TAIL if tail else {}
            return [Stream(c, list(pe) + t.get("pe", []), list(act) + t.get("act", []), list(dve) + t.get("dve", []),
                           list(pool) + t.get("pool", [])) for c in stream_counters]

        def carve(big, at, shape):
            n = int(np.prod(shape[1:]))
            v = big[:, at:at + n]
            return v.rearrange("p (a b) -> p a b", b=shape[2]) if len(shape) == 3 else v

        def turn_group(pe, bank_, src):
            for j in range(G):
                ins = pe.transpose(bank_[:, j * P:(j + 1) * P], src(j), ident[:, :])
            return ins

        TURNS = NG // W

        def attention_0():
            with ExitStack() as ph:
                SS = streams(pe=["turn_ctx", "keys"] + [f"{n}{h}" for h in range(2) for n in ("turn_u", "scores", "turn_p", "mixed")],
                             act=["ctx_turned", "keys_kept"] + [f"{n}{h}" for h in range(2) for n in ("u_turned", "exp", "p_turned")],
                             dve=["u_normed", "max0", "u_new", "max1"], pool=["x_and_u"])
                T = []
                for w in range(W):
                    t = {"keys": carve(SETA1, w * 2 * G * P, [P, 2, G * P]), "cg": carve(SETA2, w * 2 * G * P, [P, G, P]),
                         "probsT": carve(SETA2, (2 * w + 1) * G * P, [P, G, P]), "u": sb_in(ph, "u_rows", [P, G, P]),
                         "uT": sb_in(ph, "u_turned", [P, G, P]), "probs": sb_in(ph, "probs", [P, G, P]),
                         "xu": sb_in(ph, "x_plus_u", [P, G, P]),
                         "sums": sb_in(ph, "sums", [P, 2, G]), "nmax": sb_in(ph, "neg_max", [P, 2, G]), "rinv": sb_in(ph, "rinv", [P, 2, G]),
                         "A": bank[2 * w], "B": bank[2 * w + 1]}
                    t["tl"] = tail_tiles(ph, t["u"], t["uT"])
                    T.append(t)
                st = norm_tiles(ph)
                block = ph.enter_context(nc.Block())

                @block.gpsimd
                def _(pool):
                    def copy_ctx(w, i, S, t):
                        pool.tensor_copy(flat(t["cg"]), flat(group(CT, i * W + w))).then_inc(ctx_copied[w].sem, 1)

                    def body(w, i, S, t, more):
                        g = i * W + w
                        if more:
                            pool.wait_ge(S.pe.sem, S.PE.at(i, "turn_ctx"))
                            copy_ctx(w, i + 1, S, t)
                        yield
                        pool.wait_ge(S.dve.sem, S.DVE.at(i, "u_new"))
                        pool.tensor_tensor(flat(t["xu"][:, :, :]), flat(t["u"][:, :, :]), flat(group(X, g)), ALU.add).then_inc(S.pool.sem, S.POOL.tick("x_and_u"))
                        yield
                    pool.wait_ge(ctx_loaded.sem, 16)
                    for w in range(W):
                        copy_ctx(w, 0, SS[w], T[w])
                    with pool.Fori(0, TURNS - 1) as i:
                        weave(body(w, i, SS[w], T[w], True) for w in range(W))
                    weave(body(w, TURNS - 1, SS[w], T[w], False) for w in range(W))

                @block.tensor
                def _(pe):
                    def body(w, i, S, t):
                        g, A_, B_ = i * W + w, t["A"], t["B"]
                        pe.wait_ge(S.dve.sem, turn_before(S.DVE, i))
                        pe.wait_ge(ctx_copied[w].sem, i + (ctx_copied[w].value + 1))
                        turn_group(pe, A_, tile_in(t["cg"])).then_inc(S.pe.sem, S.PE.tick("turn_ctx"))
                        yield
                        pe.wait_ge(S.act.sem, S.ACT.at(i, "ctx_turned"))
                        for h, b_ in ((0, B_), (1, A_)):
                            ins = pe.matmul(b_[:, :], wsmall[:, h, :], flat(group(CTT, g)), start=True, stop=True)
                        ins.then_inc(S.pe.sem, S.PE.tick("keys"))
                        yield
                        pe.wait_ge(S.act.sem, S.ACT.at(i, "keys_kept"))
                        for h in range(2):
                            pe.wait_ge(S.dve.sem, S.DVE.at(i, ("u_normed", "u_new")[h]))
                            turn_group(pe, B_, tile_in(t["u"])).then_inc(S.pe.sem, S.PE.tick(f"turn_u{h}"))
                            pe.matmul(A_[:, :], ones[0:1, :], mask[:, bass.ds(g * (G * P), G * P)], start=True, stop=False, skip_group_check=True)
                            yield
                            pe.wait_ge(S.act.sem, S.ACT.at(i, f"u_turned{h}"))
                            for j in range(G):
                                ins = pe.matmul(A_[:, j * P:(j + 1) * P], t["uT"][:, j, :], t["keys"][:, h, j * P:(j + 1) * P], start=False, stop=True, skip_group_check=True)
                            ins.then_inc(S.pe.sem, S.PE.tick(f"scores{h}"))
                            yield
                            pe.wait_ge(S.act.sem, S.ACT.at(i, f"exp{h}"))
                            turn_group(pe, B_, tile_in(t["probs"])).then_inc(S.pe.sem, S.PE.tick(f"turn_p{h}"))
                            yield
                            pe.wait_ge(S.act.sem, S.ACT.at(i, f"p_turned{h}"))
                            for j in range(G):
                                ins = pe.matmul(A_[:, j * P:(j + 1) * P], t["probsT"][:, j, :], flat(CT[:, bass.ds(g * G + j, 1), :]), start=True, stop=True)
                            ins.then_inc(S.pe.sem, S.PE.tick(f"mixed{h}"))
                            yield
                        yield from tail_pe(pe, i, S, t["tl"], 0, B_, A_)
                    pe.wait_ge(masks_loaded.sem, 16)
                    with pe.Fori(0, TURNS) as i:
                        weave(body(w, i, SS[w], T[w]) for w in range(W))

                @block.scalar
                def _(act):
                    def body(w, i, S, t):
                        g, A_, B_ = i * W + w, t["A"], t["B"]
                        act.wait_ge(S.pe.sem, S.PE.at(i, "turn_ctx"))
                        act.copy(flat(group(CTT, g)), A_[:, :]).then_inc(S.act.sem, S.ACT.tick("ctx_turned"))
                        yield
                        act.wait_ge(S.pe.sem, S.PE.at(i, "keys"))
                        act.copy(t["keys"][:, 0, :], B_[:, :])
                        act.copy(t["keys"][:, 1, :], A_[:, :]).then_inc(S.act.sem, S.ACT.tick("keys_kept"))
                        yield
                        for h in range(2):
                            act.wait_ge(S.pe.sem, S.PE.at(i, f"turn_u{h}"))
                            act.copy(flat(t["uT"][:, :, :]), B_[:, :]).then_inc(S.act.sem, S.ACT.tick(f"u_turned{h}"))
                            yield
                            act.wait_ge(S.dve.sem, S.DVE.at(i, f"max{h}"))
                            for j in range(G):
                                ins = act.activation(t["probs"][:, j, :], A_[:, j * P:(j + 1) * P], ACT.Exp, bias=t["nmax"][:, h, j:j + 1], accum_out=t["sums"][:, h, j:j + 1])
                            ins.then_inc(S.act.sem, S.ACT.tick(f"exp{h}"))
                            yield
                            act.wait_ge(S.pe.sem, S.PE.at(i, f"turn_p{h}"))
                            act.copy(flat(t["probsT"]), B_[:, :]).then_inc(S.act.sem, S.ACT.tick(f"p_turned{h}"))
                            yield
                        yield from tail_act(act, g, i, S, t["tl"], B_)
                    with act.Fori(0, TURNS) as i:
                        weave(body(w, i, SS[w], T[w]) for w in range(W))

                @block.vector
                def _(dve):
                    ch = Chain(dve)

                    def body(w, i, S, t):
                        g, A_ = i * W + w, t["A"]
                        for h in range(2):
                            dve.wait_ge(S.pe.sem, S.PE.at(i, f"scores{h}"))
                            dve.tensor_reduce(t["nmax"][:, h, :], A_[:, :].rearrange("p (j l) -> p j l", j=G), AX.X, ALU.max, negate=True).then_inc(S.dve.sem, S.DVE.tick(f"max{h}"))
                            yield
                            dve.wait_ge(S.act.sem, S.ACT.at(i, f"exp{h}"))
                            ch.link(dve.reciprocal(t["rinv"][:, h, :], t["sums"][:, h, :]))
                            yield
                            dve.wait_ge(S.pe.sem, S.PE.at(i, f"mixed{h}"))
                            if h == 1:
                                dve.wait_ge(S.pool.sem, S.POOL.at(i, "x_and_u"))
                            for j in range(G):
                                dst, add = (t["u"][:, j, :], t["u"][:, j, :]) if h == 0 else (x_tile(g)(j), t["xu"][:, j, :])
                                ins = dve.scalar_tensor_tensor(dst, A_[:, j * P:(j + 1) * P], t["rinv"][:, h, j:j + 1], add, ALU.mult, ALU.add)
                            if h == 0:
                                ins.then_inc(S.dve.sem, S.DVE.tick("u_new"))
                            yield
                        ch.link()
                    dve.wait_ge(x_loaded.sem, 16)
                    with dve.Fori(0, TURNS) as i:
                        norm_all(dve, ch, st, lambda w: x_tile(i * W + w), lambda w: tile_in(T[w]["u"]),
                                 lambda w, ins: ins.then_inc(SS[w].dve.sem, SS[w].DVE.tick("u_normed")),
                                 lambda w: dve.wait_ge(SS[w].act.sem, turn_before(SS[w].ACT, i)))
                        weave(body(w, i, SS[w], T[w]) for w in range(W))
                        tail_norms(dve, ch, i, SS, st, T)
                        weave(tail_dve(dve, ch, i * W + w, i, SS[w], T[w]["tl"], T[w]["A"]) for w in range(W))
                close_streams(SS, ctx=True)

        attention_0()

        EIGHT = 8

        def route(layer, top, capacity):
            n_tiles = {0: TILES_TOP2, 1: TILES_CAP, 2: TILES_TOP2, 3: TILES_TOP1}[layer]
            with ExitStack() as ph:
                oh = sb_in(ph, "one_hot", [P, 2, B, E])
                ohb = sb_in(ph, "one_hot_bf", [P, B, E], BF16)
                tot = sb_in(ph, "totals", [P, B, E])
                run = sb_in(ph, "running", [P, B, E])
                pos = sb_in(ph, "positions", [P, B, E])
                tmp = sb_in(ph, "picked", [P, B, E])
                zeros = sb_in(ph, "zeros", [P, B])
                posf = sb_in(ph, "slot_f", [P, 2, B])
                keep = sb_in(ph, "kept", [P, 2, B])
                small = sb_in(ph, "tile_counts", [P, 4, E])
                cnt_i = sb_in(ph, "count_bits", [P, E], I32)
                expo = sb_in(ph, "exp_logits", [P, B, E])
                slot_i = sb_in(ph, "slot_bits", [P, top * B], I32)
                slot_f = sb_in(ph, "slot_value", [P, B, top])
                slot_tile = sb_in(ph, "slot_tile", [P, top * B])
                slot_row = sb_in(ph, "slot_row", [P, top * B])
                pair_row = sb_in(ph, "pair_row_number", [P, B, top])
                hot_row = sb_in(ph, "hot_slot_row", [P, 2, EIGHT, P], F32R)
                hot_tile = sb_in(ph, "row_at_tile", [P, 2, EIGHT, n_tiles], F32R)
                tcmp = sb_in(ph, "tile_compare", [1, TILES_TOP2, E])
                tsum = sb_in(ph, "tile_sum", [1, TILES_TOP2])
                block = ph.enter_context(nc.Block())
                PAIRS = top * B
                marked0, pairs0, summed0 = tiles_marked.value, pairs_made.value, pairs_summed.value

                @block.sync
                def _(sp):
                    sp.dma_start(xn.rearrange("(t p) d -> p t d", p=P), XN[:, :, :]).then_inc(rows_stored.sem, 16)
                    sp.wait_ge(rows_stored.sem, rows_stored.value + 16)

                def eights(eng, eight):
                    for s in range(2):
                        eight(s, s, True)
                    with eng.Fori(1, PAIRS // EIGHT // 2) as i:
                        for s in range(2):
                            eight(i * 2 + s, s, False)

                @block.gpsimd
                def _(pool):
                    def eight(i, s, first):
                        pool.wait_ge(tiles_marked.sem, i + (marked0 + 1))
                        pool.tensor_tensor(hot_tile[:, s, :, :], hot_tile[:, s, :, :].bitcast(F32),
                                           pair_row[:, :, :].rearrange("p b k -> p (b k)")[:, bass.ds(i * EIGHT, EIGHT)].unsqueeze(2).to_broadcast([P, EIGHT, n_tiles]),
                                           ALU.mult).then_inc(pairs_made.sem, 1)
                    eights(pool, eight)
                dv, pv, av = dve_done.value, pe_done.value, act_done.value

                @block.vector
                def _(dve):
                    ch = Chain(dve)

                    def eight(i, s, first):
                        if not first:
                            dve.wait_ge(pairs_summed.sem, i + (summed0 - 1))
                        for hot, iota, which, n in ((hot_row, iota_slot, slot_row, P), (hot_tile, iota_tile, slot_tile, n_tiles)):
                            ins = dve.tensor_tensor(hot[:, s, :, :], iota[:, 0:n].unsqueeze(1).to_broadcast([P, EIGHT, n]),
                                                    which[:, bass.ds(i * EIGHT, EIGHT)].unsqueeze(2).to_broadcast([P, EIGHT, n]), ALU.is_equal)
                        ins.then_inc(tiles_marked.sem, 1)
                    dve.memset(zeros[:, :], 0.0)
                    for k in range(top):
                        dve.tensor_tensor(oh[:, k, :, :], IX[:, :, k:k + 1].to_broadcast([P, B, E]),
                                          iota8[:, :].unsqueeze(1).to_broadcast([P, B, E]), ALU.is_equal)
                    ch.link()
                    if top == 2:
                        dve.tensor_tensor(ohb[:, :, :], oh[:, 0, :, :], oh[:, 1, :, :], ALU.add).then_inc(dve_done.sem, 1)
                        dve.tensor_tensor(expo[:, :, 0], MX[:, :, 1], MX[:, :, 0], ALU.subtract).then_inc(dve_done.sem, 1)
                    else:
                        dve.tensor_copy(ohb[:, :, :], oh[:, 0, :, :]).then_inc(dve_done.sem, 1)
                        dve.tensor_tensor(expo[:, :, :], LG[:, :, :], MX[:, :, 0:1].to_broadcast([P, B, E]), ALU.subtract).then_inc(dve_done.sem, 1)
                    dve.wait_ge(pe_done.sem, pv + 1)
                    ch.link(dve.tensor_copy(tot[:, :, :].rearrange("p b e -> p (b e)"), bank[1][:, 0:B * E]))
                    for e in range(E):
                        dve.tensor_tensor_scan(run[:, :, e], tot[:, :, e], zeros[:, :], 0.0, ALU.add, ALU.add)
                    ch.link()
                    ch.link(dve.tensor_tensor(pos[:, :, :], run[:, :, :], tot[:, :, :], ALU.subtract))
                    ch.link(dve.tensor_tensor(pos[:, :, :], pos[:, :, :], bank[0][:, 0:B * E].rearrange("p (b e) -> p b e", e=E), ALU.add))
                    if capacity:
                        for k in range(top):
                            ch.link(dve.scalar_tensor_tensor(tmp[:, :, :], pos[:, :, :], float(capacity), oh[:, k, :, :], ALU.is_lt, ALU.mult))
                            ch.link(dve.tensor_reduce(keep[:, k, :], tmp[:, :, :], AX.X, ALU.add))
                        ch.link(dve.tensor_scalar(small[:, 3, :], iota8[:, :], float(capacity), None, ALU.mult))
                    else:
                        ch.link(dve.tensor_scalar(cnt_i[:, :], run[:, B - 1, :], float(P - 1), None, ALU.add))
                        ch.link(dve.tensor_scalar(cnt_i[:, :], cnt_i[:, :], 7, None, ALU.arith_shift_right))
                        ch.link(dve.tensor_copy(small[:, 0, :], cnt_i[:, :]))
                        ch.link(dve.tensor_tensor_scan(small[:, 1, :], small[:, 0, :], zeros[:, 0:E], 0.0, ALU.add, ALU.add))
                        ch.link(dve.tensor_tensor(small[:, 2, :], small[:, 1, :], small[:, 0, :], ALU.subtract))
                        ch.link(dve.tensor_scalar(small[:, 3, :], small[:, 2, :], float(P), None, ALU.mult))
                    ch.link(dve.tensor_tensor(pos[:, :, :], pos[:, :, :], small[:, 3, :].unsqueeze(1).to_broadcast([P, B, E]), ALU.add))
                    for k in range(top):
                        ch.link(dve.tensor_tensor(tmp[:, :, :], oh[:, k, :, :], pos[:, :, :], ALU.mult))
                        ch.link(dve.tensor_reduce(posf[:, k, :], tmp[:, :, :], AX.X, ALU.add))
                    if capacity:
                        ch.link(dve.tensor_tensor(posf[:, :, :], posf[:, :, :], keep[:, :, :], ALU.mult))
                        dve.tensor_copy(POS[:, :, :], posf[:, :, :])
                        ch.link(dve.tensor_scalar(tmp[:, 0:2 * B // E, :].rearrange("p a e -> p (a e)"), keep[:, :, :].rearrange("p a b -> p (a b)"), -FAR, FAR, ALU.mult, ALU.add))
                        ch.link(dve.tensor_tensor(posf[:, :, :].rearrange("p a b -> p (a b)"), posf[:, :, :].rearrange("p a b -> p (a b)"), tmp[:, 0:2 * B // E, :].rearrange("p a e -> p (a e)"), ALU.add))
                    else:
                        dve.tensor_copy(POS[:, 0:top, :], posf[:, 0:top, :])
                    ch.link(dve.tensor_copy(slot_f[:, :, :].rearrange("p b k -> p k b"), posf[:, 0:top, :]))
                    slots = slot_f[:, :, :].rearrange("p b k -> p (b k)")
                    dve.tensor_copy(pair_row[:, :, :], row_number[:, :].unsqueeze(2).to_broadcast([P, B, top]))
                    ch.link(dve.tensor_copy(slot_i[:, :], slots))
                    ch.link(dve.tensor_scalar(slot_i[:, :], slot_i[:, :], 7, None, ALU.arith_shift_right))
                    ch.link(dve.tensor_copy(slot_tile[:, :], slot_i[:, :]))
                    ch.link(dve.scalar_tensor_tensor(slot_row[:, :], slot_tile[:, :], -float(P), slots, ALU.mult, ALU.add))
                    eights(dve, eight)
                    if not capacity:
                        ch.link(dve.tensor_tensor(tcmp[:, 0:n_tiles, :], iota_tile[0:1, 0:n_tiles].unsqueeze(2).to_broadcast([1, n_tiles, E]),
                                                  small[0:1, 1, :].unsqueeze(1).to_broadcast([1, n_tiles, E]), ALU.is_ge))
                        ch.link(dve.tensor_reduce(tsum[:, 0:n_tiles], tcmp[:, 0:n_tiles, :], AX.X, ALU.add))
                        dve.tensor_scalar(tile_expert[:, 0:n_tiles], tsum[:, 0:n_tiles], float(E - 1), None, ALU.min)
                    dve.wait_ge(pe_done.sem, pv + 2 + (16 if layer == 0 else 0))
                    dve.tensor_copy(SOURCE[:, 0:n_tiles], bank[7][:, 0:n_tiles])
                    dve.wait_ge(act_done.sem, av + 1)
                    ch.link()
                    if top == 2:
                        ch.link(dve.tensor_scalar(tmp[:, :, 0], expo[:, :, 1], 1.0, None, ALU.add))
                        ch.link(dve.reciprocal(WT[:, 0, :], tmp[:, :, 0]))
                        ch.link(dve.tensor_tensor(WT[:, 1, :], WT[:, 0, :], expo[:, :, 1], ALU.mult))
                        if capacity:
                            dve.tensor_tensor(WT[:, :, :], WT[:, :, :], keep[:, :, :], ALU.mult)
                    else:
                        ch.link(dve.tensor_reduce(tmp[:, :, 0], expo[:, :, :], AX.X, ALU.add))
                        dve.reciprocal(WT[:, 0, :], tmp[:, :, 0])

                @block.scalar
                def _(act):
                    act.wait_ge(dve_done.sem, dv + 2)
                    if top == 2:
                        act.activation(expo[:, :, 1], expo[:, :, 0], ACT.Exp).then_inc(act_done.sem, 1)
                    else:
                        act.activation(expo[:, :, :], expo[:, :, :], ACT.Exp).then_inc(act_done.sem, 1)
                    if layer == 0:
                        for i in range(16):
                            act.wait_ge(pe_done.sem, pv + 2 + i)
                            dst = SETA1 if i < 8 else SETA2
                            act.copy(dst[:, (i % 8) * 512:(i % 8 + 1) * 512], bank[2 + i % 6][:, :]).then_inc(act_done.sem, 1)

                @block.tensor
                def _(pe):
                    pe.wait_ge(dve_done.sem, dv + 1)
                    pe.matmul(bank[0][:, 0:B * E], tri[:, :], ohb[:, :, :].rearrange("p b e -> p (b e)"), start=True, stop=True)
                    pe.matmul(bank[1][:, 0:B * E], ones[:, :], ohb[:, :, :].rearrange("p b e -> p (b e)"), start=True, stop=True).then_inc(pe_done.sem, 1)
                    if layer == 0:
                        pe.wait_ge(weights_b.sem, weights_b.value)
                        for i in range(16):
                            if i >= 6:
                                pe.wait_ge(act_done.sem, av + 2 + i - 6)
                            raw = SETB1 if i < 8 else SETB2
                            for j in range(4):
                                c = (i % 8) * 4 + j
                                ins = pe.transpose(bank[2 + i % 6][:, j * P:(j + 1) * P], raw[:, c * P:(c + 1) * P], ident[:, :])
                            ins.then_inc(pe_done.sem, 1)
                        pe.wait_ge(act_done.sem, av + 2 + 15)

                    def eight(i, s, first):
                        pe.wait_ge(pairs_made.sem, i + (pairs0 + 1))
                        for r in range(EIGHT):
                            ins = pe.matmul(bank[7][:, 0:n_tiles], hot_row[:, s, r, :], hot_tile[:, s, r, :], start=first and s == 0 and r == 0, stop=True, skip_group_check=True)
                        ins.then_inc(pairs_summed.sem, 1)
                    eights(pe, eight)
                    pe.drain().then_inc(pe_done.sem, 1)

            dve_done.value += 2
            pe_done.value += 2 + (16 if layer == 0 else 0)
            act_done.value += 1 + (16 if layer == 0 else 0)
            rows_stored.value += 16
            for c in (tiles_marked, pairs_made, pairs_summed):
                c.value += PAIRS // EIGHT

        def experts(layer):
            n_tiles = {0: TILES_TOP2, 1: TILES_CAP, 2: TILES_TOP2, 3: TILES_TOP1}[layer]
            W1, W2 = (SETA1, SETA2) if layer in (0, 2) else (SETB1, SETB2)
            gated = layer in (1, 2)
            NC = 2 if gated else 4
            UNROLL = 4
            with ExitStack() as ph:
                xr = sb_in(ph, "tile_rows", [P, 4, P])
                xt = sb_in(ph, "tile_turned", [P, 2, P])
                hid = sb_in(ph, "hidden", [P, 2, NC * P])
                gat = sb_in(ph, "gate", [P, 2, 256])
                hidT = sb_in(ph, "hidden_turned_sb", [P, 2, NC * P])
                yo = sb_in(ph, "expert_rows_sb", [P, 4, P])
                b1 = sb_in(ph, "expert_b1", [3, E * H1], BF16)
                b1_here = rows_loaded.value + 16
                block = ph.enter_context(nc.Block())

                def tile_of(rows, j):
                    return rows.rearrange("(t p) d -> t p d", p=P)[bass.ds(j, 1), :, :].rearrange("a p d -> (a p) d")

                def run(eng, step):
                    for k in range(-2, 2):
                        step(k, k % UNROLL)
                    with eng.Fori(0, (n_tiles - 4) // UNROLL) as q:
                        for u in range(UNROLL):
                            step(q * UNROLL + (2 + u), (2 + u) % UNROLL)
                    for k in range(n_tiles - 2, n_tiles + 1):
                        step(k, k % UNROLL)

                def exists(j):
                    return not isinstance(j, int) or 0 <= j < n_tiles

                def beyond(j, n):
                    return not isinstance(j, int) or j >= n

                @block.sync
                def _(sp):
                    if not gated:
                        at, width = BIAS_AT[f"L{layer}_ffn_b1"]
                        sp.dma_start(b1[:, :], bias_dram[:, at:at + width]).then_inc(rows_loaded.sem, 16)

                    if layer in (0, 2):
                        load_expert_weights(sp, layer + 1)

                @block.gpsimd
                def _(pool):
                    for j in range(n_tiles):
                        if j >= 4:
                            pool.wait_ge(rows_turned.sem, j + (rows_turned.value - 3))
                        pool.indirect_dma_start(xr[:, j % 4, :], None, xn, bass.IndirectOffsetOnAxis(ap=SOURCE[:, j:j + 1], axis=0)).then_inc(sorted_in[j % 4].sem, 16)

                @block.tensor
                def _(pe):
                    if not gated:
                        pe.wait_ge(rows_loaded.sem, b1_here)
                    if layer:
                        done = weights_a if layer == 2 else weights_b
                        pe.wait_ge(done.sem, done.value)

                    def turn_rows(j, u):
                        if exists(j):
                            if isinstance(j, int):
                                pe.wait_ge(sorted_in[u].sem, sorted_in[u].value + 16 * (j // 4 + 1))
                            else:
                                pe.wait_ge(sorted_in[u].sem, (j - u) * 4 + (sorted_in[u].value + 16))
                            pe.transpose(bank[u % 2][:, 0:P], xr[:, u, :], ident[:, :]).then_inc(rows_turned.sem, 1)

                    def expert_of(j):
                        if layer == 1 or not exists(j):
                            return None
                        return pe.value_load(tile_expert[0:1, bass.ds(j, 1)], min_val=0, max_val=E - 1)

                    def hidden(j, u, e):
                        if exists(j):
                            if layer == 1:
                                off = (j // 2) * H1 if isinstance(j, int) else (j - u % 2) * (H1 // 2)
                            else:
                                off = e * H1
                            pe.wait_ge(rows_turned_kept.sem, j + (rows_turned_kept.value + 1))
                            out_ = bank[2 + u % 2]
                            ins = pe.matmul(out_[:, :], xt[:, u % 2, :], W1[:, bass.ds(off, H1)], start=True, stop=gated)
                            if not gated:
                                ins = pe.matmul(out_[:, :], ones[0:3, :], b1[:, bass.ds(off, H1)], start=False, stop=True)
                            ins.then_inc(hidden_made.sem, 1)

                    def turn_hidden(j, u):
                        if exists(j):
                            pe.wait_ge(hidden_kept.sem, j + (hidden_kept.value + 1))
                            for c in range(NC):
                                ins = pe.transpose(bank[4 + u % 2][:, c * P:(c + 1) * P], hid[:, u % 2, c * P:(c + 1) * P], ident[:, :])
                            ins.then_inc(hidden_turned.sem, 1)

                    def rows_out(j, u, e):
                        if exists(j):
                            if layer == 1:
                                off = (j // 2) * NC * P if isinstance(j, int) else (j - u % 2) * (NC * P // 2)
                            else:
                                off = e * (NC * P)
                            pe.wait_ge(hidden_turned_kept.sem, j + (hidden_turned_kept.value + 1))
                            if beyond(j, 2):
                                pe.wait_ge(expert_kept.sem, j + (expert_kept.value - 1))
                            out_ = bank[6 + u % 2]
                            for c in range(NC):
                                ins = pe.matmul(out_[:, 0:P], hidT[:, u % 2, c * P:(c + 1) * P], W2[:, bass.ds(off + c * P, P)],
                                                start=(c == 0), stop=(gated and c == NC - 1))
                            if not gated:
                                ins = pe.matmul(out_[:, 0:P], ones[0:3, :], rows3[:, bass.ds(e * P + R_B2[f"L{layer}"], P)], start=False, stop=True)
                            ins.then_inc(expert_made.sem, 1)

                    def step(k, u):
                        if u == 2:
                            known.clear()
                        turn_rows(k + 2, (u + 2) % 4)
                        hidden(k + 1, (u + 1) % 4, known[(u + 1) % 4] if (u + 1) % 4 in known else expert_of(k + 1))
                        if u in (2, 3):
                            known[(u + 3) % 4] = expert_of(k - 1)
                        if u != 1:
                            known[(u + 2) % 4] = expert_of(k + 2)
                        turn_hidden(k, u)
                        rows_out(k - 1, (u + 3) % 4, known[(u + 3) % 4] if (u + 3) % 4 in known else expert_of(k - 1))
                    known = {}
                    run(pe, step)

                @block.scalar
                def _(act):
                    def store(j, s):
                        if exists(j):
                            act.wait_ge(expert_kept.sem, j + (expert_kept.value + 1))
                            act.dma_start(tile_of(ys, j), yo[:, s, :]).then_inc(expert_out[s].sem, 16)

                    def step(k, u):
                        store(k - 2, (u + 2) % 4)
                        j, s = k + 1, (u + 1) % 2
                        if exists(j):
                            act.wait_ge(hidden_made.sem, j + (hidden_made.value + 1))
                            if gated:
                                half = 256 if layer == 1 else 0
                                act.activation(gat[:, s, :], bank[2 + s][:, half:half + 256], ACT.Silu).then_inc(gates_kept.sem, 1)
                            else:
                                act.activation(hid[:, s, :], bank[2 + s][:, :], ACT.Gelu).then_inc(hidden_kept.sem, 1)
                    run(act, step)
                    store(n_tiles - 1, 3)
                    for s in range(4):
                        act.wait_ge(expert_out[s].sem, expert_out[s].value + 16 * (n_tiles // 4))

                @block.vector
                def _(dve):
                    def step(k, u):
                        j, s = k + 2, u % 2
                        if exists(j):
                            dve.wait_ge(rows_turned.sem, j + (rows_turned.value + 1))
                            dve.tensor_copy(xt[:, s, :], bank[s][:, 0:P]).then_inc(rows_turned_kept.sem, 1)
                        j, s = k + 1, (u + 1) % 2
                        if gated and exists(j):
                            dve.wait_ge(gates_kept.sem, j + (gates_kept.value + 1))
                            half = 0 if layer == 1 else 256
                            dve.tensor_tensor(hid[:, s, :], bank[2 + s][:, half:half + 256], gat[:, s, :], ALU.mult).then_inc(hidden_kept.sem, 1)
                        j, s = k, u % 2
                        if exists(j):
                            dve.wait_ge(hidden_turned.sem, j + (hidden_turned.value + 1))
                            dve.tensor_copy(hidT[:, s, :], bank[4 + s][:, 0:NC * P]).then_inc(hidden_turned_kept.sem, 1)
                        j, s = k - 1, (u + 3) % 4
                        if exists(j):
                            dve.wait_ge(expert_made.sem, j + (expert_made.value + 1))
                            if isinstance(j, int):
                                if j >= 4:
                                    dve.wait_ge(expert_out[s].sem, expert_out[s].value + 16 * (j // 4))
                            else:
                                dve.wait_ge(expert_out[s].sem, (j - s) * 4 + expert_out[s].value)
                            dve.tensor_copy(yo[:, s, :], bank[6 + s % 2][:, 0:P]).then_inc(expert_kept.sem, 1)
                    run(dve, step)

            for c in (rows_turned, hidden_made, hidden_turned, expert_made, rows_turned_kept, hidden_kept, hidden_turned_kept, expert_kept):
                c.value += n_tiles
            if gated:
                gates_kept.value += n_tiles
            else:
                rows_loaded.value += 16
            for s in range(4):
                sorted_in[s].value += 16 * (n_tiles // 4)
                expert_out[s].value += 16 * (n_tiles // 4)

        def gather_group(pool, g, top):
            for t in range(g * G, (g + 1) * G):
                for k in range(top):
                    dst = (XN, Y1)[k]
                    pool.indirect_dma_start(dst[:, t, :], None, ys, bass.IndirectOffsetOnAxis(ap=POS[:, k, t:t + 1], axis=0)).then_inc(gathered[g % 2].sem, 16)

        def group_is_here(pool, g, top):
            pool.wait_ge(gathered[g % 2].sem, gathered[g % 2].value + 16 * G * top * (g // 2 + 1))
            pool.sem_inc(rows_here.sem, 1)

        def close_gathers(top):
            for c in gathered:
                c.value += 16 * G * top * NG // 2
            rows_here.value += NG

        def load_expert_weights(sp, layer):
            W1, W2 = (SETA1, SETA2) if layer in (0, 2) else (SETB1, SETB2)
            done = weights_a if layer in (0, 2) else weights_b
            w1v = W1[:, :].rearrange("p (e f) -> p e f", e=E)
            if layer == 1:
                srcs = [(w1v[:, :, 0:256], A["L1_ffn_W"].rearrange("e d f -> d e f")),
                        (w1v[:, :, 256:512], A["L1_ffn_V"].rearrange("e d f -> d e f")),
                        (W2[:, 0:E * 256].rearrange("p (c d) -> p c d", d=P), A["L1_ffn_W_out"].rearrange("e (c p) d -> p (e c) d", p=P))]
            elif layer == 2:
                srcs = [(w1v, A["L2_ffn_gate_up_w"].rearrange("e d f -> d e f")),
                        (W2[:, 0:E * 256].rearrange("p (c d) -> p c d", d=P), A["L2_ffn_down_w"].rearrange("e (c p) d -> p (e c) d", p=P))]
            else:
                srcs = [(w1v, A["L3_ffn_w1"].rearrange("e d f -> d e f")),
                        (W2[:, :].rearrange("p (c d) -> p c d", d=P), A["L3_ffn_w2"].rearrange("e (c p) d -> p (e c) d", p=P))]
            for dst, src in srcs:
                sp.dma_start(dst, src).then_inc(done.sem, 16)
            done.value += 16 * len(srcs)

        def combine_and_store(top):
            with nc.Block() as block:
                @block.gpsimd
                def _(pool):
                    gather_turns(pool, top)

                @block.vector
                def _(dve):
                    ch = Chain(dve)
                    with dve.Fori(0, NG) as g:
                        dve.wait_ge(rows_here.sem, g + (rows_here.value + 1))
                        combine(dve, ch, g, top)
                        dve.sem_inc(combined.sem, 1)

                @block.sync
                def _(sp):
                    with sp.Fori(0, NG) as g:
                        sp.wait_ge(combined.sem, g + 1)
                        sp.dma_start(out[bass.ds(g * G, G), :, :].rearrange("t p d -> p t d"), group(X, g)).then_inc(stored.sem, 16)
                    sp.wait_ge(stored.sem, 16 * NG)
            close_gathers(top)

        def gather_turns(pool, top, before_turn=None):
            for g in range(NG + 1):
                if g < NG:
                    if before_turn and g % W == 0:
                        before_turn(g // W)
                    gather_group(pool, g, top)
                if g >= 1:
                    group_is_here(pool, g - 1, top)

        def attention_1(top_before):
            with ExitStack() as ph:
                VX = P + 16
                SS = streams(pe=["k", "v", "turn_u", "q", "turn_q", "kv", "out", "turn_o", "proj"],
                             act=["v_kept", "k_exp", "u_turned", "q_exp", "q_turned", "o_turned"],
                             dve=["k_less", "k_soft", "u_normed", "q_less", "q_soft", "kv_masked", "o"])
                one = sb_in(ph, "one_column", [P, 1])
                T = []
                for w in range(W):
                    t = {"ctx": carve(SETA1, 2 * w * G * P, [P, G, P]), "v": carve(SETA1, (2 * w + 1) * G * P, [P, G, P]),
                         "k": carve(SETA2, 2 * w * G * P, [P, G * P]), "q": carve(SETA2, (2 * w + 1) * G * P, [P, G * P]),
                         "u": sb_in(ph, "u_rows1", [P, G, P]), "uT": sb_in(ph, "u_turned1", [P, G, P]),
                         "qT": sb_in(ph, "q_turned", [P, G, P]), "kvm": sb_in(ph, "kv_masked", [P, G, VX]),
                         "red": sb_in(ph, "head_sums", [P, 2, G * 16]), "dinv": sb_in(ph, "d_inv", [P, G * 16]),
                         "A": bank[2 * w], "B": bank[2 * w + 1]}
                    t["tl"] = tail_tiles(ph, t["u"], t["uT"])
                    T.append(t)
                st = norm_tiles(ph)
                block = ph.enter_context(nc.Block())

                @block.gpsimd
                def _(pool):
                    def copy_ctx(i):
                        for w in range(W):
                            if i:
                                pool.wait_ge(SS[w].pe.sem, SS[w].PE.at(i - 1, "v"))
                            pool.tensor_copy(flat(T[w]["ctx"]), flat(group(CTT, i * W + w))).then_inc(ctx_copied[w].sem, 1)
                    gather_turns(pool, top_before, copy_ctx)

                @block.vector
                def _(dve):
                    ch = Chain(dve)

                    def heads(ap):
                        return ap.rearrange("p (h c) -> p h c", c=8)

                    def wide(ap):
                        return ap.unsqueeze(2).to_broadcast([P, G * 16, 8])

                    def soft_heads(i, S, t, src, name, at):
                        dst, red = t[name], t["red"]
                        dve.wait_ge(S.pe.sem, S.PE.at(i, name))
                        ch.link(dve.tensor_reduce(red[:, at, :], heads(src), AX.X, ALU.max))
                        dve.tensor_tensor(heads(dst), heads(src), wide(red[:, at, :]), ALU.subtract).then_inc(S.dve.sem, S.DVE.tick(f"{name}_less"))
                        yield
                        dve.wait_ge(S.act.sem, S.ACT.at(i, f"{name}_exp"))
                        ch.link(dve.tensor_reduce(red[:, at + 1, :], heads(dst), AX.X, ALU.add))
                        ch.link(dve.reciprocal(red[:, at + 1, :], red[:, at + 1, :]))
                        dve.tensor_tensor(heads(dst), heads(dst), wide(red[:, at + 1, :]), ALU.mult).then_inc(S.dve.sem, S.DVE.tick(f"{name}_soft"))
                        yield

                    def body(w, i, S, t):
                        g, A_, B_ = i * W + w, t["A"], t["B"]
                        yield from soft_heads(i, S, t, A_[:, :], "q", 0)
                        dve.wait_ge(S.pe.sem, S.PE.at(i, "kv"))
                        dve.tensor_tensor(t["kvm"][:, :, 0:P], A_[:, :].rearrange("p (j c) -> p j c", c=P), blocks[:, 0:P].unsqueeze(1).to_broadcast([P, G, P]), ALU.mult)
                        dve.tensor_tensor(t["kvm"][:, :, P:VX], B_[:, 0:G].unsqueeze(2).to_broadcast([P, G, 16]),
                                          blocks[:, P:VX].unsqueeze(1).to_broadcast([P, G, 16]), ALU.mult).then_inc(S.dve.sem, S.DVE.tick("kv_masked"))
                        yield
                        dve.wait_ge(S.pe.sem, S.PE.at(i, "out"))
                        ch.link(dve.reciprocal(t["dinv"][:, :], B_[:, 0:G * 16]))
                        o = flat(t["u"][:, :, :])
                        ch.link(dve.tensor_tensor(heads(o), heads(A_[:, :]), wide(t["dinv"][:, :]), ALU.mult))
                        dve.tensor_tensor(o, o, t["q"], ALU.add).then_inc(S.dve.sem, S.DVE.tick("o"))
                        yield
                        dve.wait_ge(S.pe.sem, S.PE.at(i, "proj"))
                        dve.tensor_tensor(flat(group(X, g)), flat(group(X, g)), A_[:, :], ALU.add)
                        yield
                    dve.memset(one[:, :], 1.0)
                    with dve.Fori(0, TURNS) as i:
                        weave(soft_heads(i, SS[w], T[w], T[w]["A"][:, :], "k", 0) for w in range(W))
                        combine_turn(dve, ch, i, top_before)
                        norm_all(dve, ch, st, lambda w: x_tile(i * W + w), lambda w: tile_in(T[w]["u"]),
                                 lambda w, ins: ins.then_inc(SS[w].dve.sem, SS[w].DVE.tick("u_normed")),
                                 lambda w: dve.wait_ge(SS[w].act.sem, turn_before(SS[w].ACT, i)))
                        weave(body(w, i, SS[w], T[w]) for w in range(W))
                        ch.link()
                        tail_norms(dve, ch, i, SS, st, T)
                        weave(tail_dve(dve, ch, i * W + w, i, SS[w], T[w]["tl"], T[w]["A"]) for w in range(W))

                @block.scalar
                def _(act):
                    def body(w, i, S, t):
                        g, A_, B_ = i * W + w, t["A"], t["B"]

                        def keep(step, name, dst):
                            act.wait_ge(S.pe.sem, S.PE.at(i, step))
                            act.copy(flat(t[dst][:, :, :]), B_[:, :]).then_inc(S.act.sem, S.ACT.tick(name))

                        def exp(name):
                            act.wait_ge(S.dve.sem, S.DVE.at(i, f"{name}_less"))
                            act.activation(t[name], t[name], ACT.Exp).then_inc(S.act.sem, S.ACT.tick(f"{name}_exp"))
                        keep("v", "v_kept", "v")
                        yield
                        exp("k")
                        yield
                        keep("turn_u", "u_turned", "uT")
                        yield
                        exp("q")
                        yield
                        keep("turn_q", "q_turned", "qT")
                        yield
                        keep("turn_o", "o_turned", "uT")
                        yield
                        yield from tail_act(act, g, i, S, t["tl"], B_)
                    with act.Fori(0, TURNS) as i:
                        weave(body(w, i, SS[w], T[w]) for w in range(W))

                @block.tensor
                def _(pe):
                    def biased(out_, which, lhs, w):
                        for j in range(G):
                            pe.matmul(out_[:, j * P:(j + 1) * P], ones[0:3, :], rows3[:, R_SMALL + which * P:R_SMALL + (which + 1) * P],
                                      start=(j == 0), stop=False, skip_group_check=True)
                        for j in range(G):
                            ins = pe.matmul(out_[:, j * P:(j + 1) * P], lhs[:, j, :], w, start=False, stop=True, skip_group_check=True)
                        return ins

                    def body(w, i, S, t):
                        g, A_, B_ = i * W + w, t["A"], t["B"]
                        pe.wait_ge(S.dve.sem, turn_before(S.DVE, i))
                        pe.wait_ge(ctx_copied[w].sem, i + (ctx_copied[w].value + 1))
                        biased(A_, 1, t["ctx"], wsmall[:, 3, :]).then_inc(S.pe.sem, S.PE.tick("k"))
                        biased(B_, 2, t["ctx"], wsmall[:, 4, :]).then_inc(S.pe.sem, S.PE.tick("v"))
                        yield
                        pe.wait_ge(S.act.sem, S.ACT.at(i, "v_kept"))
                        pe.wait_ge(S.dve.sem, S.DVE.at(i, "u_normed"))
                        turn_group(pe, B_, tile_in(t["u"])).then_inc(S.pe.sem, S.PE.tick("turn_u"))
                        yield
                        pe.wait_ge(S.act.sem, S.ACT.at(i, "u_turned"))
                        biased(A_, 0, t["uT"], wsmall[:, 2, :]).then_inc(S.pe.sem, S.PE.tick("q"))
                        yield
                        pe.wait_ge(S.dve.sem, S.DVE.at(i, "q_soft"))
                        turn_group(pe, B_, lambda j: t["q"][:, j * P:(j + 1) * P]).then_inc(S.pe.sem, S.PE.tick("turn_q"))
                        for j in range(G):
                            pe.matmul(A_[:, j * P:(j + 1) * P], t["k"][:, j * P:(j + 1) * P], t["v"][:, j, :], start=True, stop=True)
                        yield
                        pe.wait_ge(S.act.sem, S.ACT.at(i, "q_turned"))
                        for j in range(G):
                            ins = pe.matmul(B_[:, j:j + 1], t["k"][:, j * P:(j + 1) * P], one[:, :], start=True, stop=True)
                        ins.then_inc(S.pe.sem, S.PE.tick("kv"))
                        yield
                        pe.wait_ge(S.dve.sem, S.DVE.at(i, "kv_masked"))
                        for j in range(G):
                            pe.matmul(A_[:, j * P:(j + 1) * P], t["qT"][:, j, :], t["kvm"][:, j, 0:P], start=True, stop=True)
                            ins = pe.matmul(B_[:, j * 16:(j + 1) * 16], t["qT"][:, j, :], t["kvm"][:, j, P:VX], start=True, stop=True)
                        ins.then_inc(S.pe.sem, S.PE.tick("out"))
                        yield
                        pe.wait_ge(S.dve.sem, S.DVE.at(i, "o"))
                        turn_group(pe, B_, tile_in(t["u"])).then_inc(S.pe.sem, S.PE.tick("turn_o"))
                        yield
                        pe.wait_ge(S.act.sem, S.ACT.at(i, "o_turned"))
                        biased(A_, 3, t["uT"], wsmall[:, 5, :]).then_inc(S.pe.sem, S.PE.tick("proj"))
                        yield
                        yield from tail_pe(pe, i, S, t["tl"], 1, B_, A_)
                    with pe.Fori(0, TURNS) as i:
                        weave(body(w, i, SS[w], T[w]) for w in range(W))
                close_streams(SS, ctx=True)
                close_gathers(top_before)

        HEADS, HD = 16, 64
        INNER = HEADS * HD
        KVT = SETB[:, :].rearrange("p (b k) -> p b k", k=2 * P)

        def attention_2_norms(top_before):
            with ExitStack() as ph:
                SS = streams(pe=["turn_c", "turn_l"], act=["c_kept", "l_kept"], dve=["c", "l"], tail=False)
                T = [{"u": sb_in(ph, "u_rows2", [P, G, P]), "c": sb_in(ph, "ctx_normed", [P, G, P]),
                      "A": bank[2 * w], "B": bank[2 * w + 1]} for w in range(W)]
                st = norm_tiles(ph)
                block = ph.enter_context(nc.Block())

                @block.sync
                def _(sp):
                    load_expert_weights(sp, 2)

                @block.gpsimd
                def _(pool):
                    gather_turns(pool, top_before)

                @block.vector
                def _(dve):
                    ch = Chain(dve)

                    def last_turned(w):
                        dve.wait_ge(SS[w].pe.sem, turn_before(SS[w].PE, i))

                    def signal(name):
                        return lambda w, ins: ins.then_inc(SS[w].dve.sem, SS[w].DVE.tick(name))
                    with dve.Fori(0, TURNS) as i:
                        norm_all(dve, ch, st, lambda w: (lambda j: flat(CT[:, bass.ds((i * W + w) * G + j, 1), :])), lambda w: tile_in(T[w]["c"]),
                                 signal("c"), last_turned)
                        combine_turn(dve, ch, i, top_before)
                        norm_all(dve, ch, st, lambda w: x_tile(i * W + w), lambda w: tile_in(T[w]["u"]), lambda w, ins: None)
                        ch.link()
                        norm_all(dve, ch, st, lambda w: tile_in(T[w]["u"]), lambda w: tile_in(T[w]["u"]), signal("l"))
                        ch.link()

                @block.tensor
                def _(pe):
                    def body(w, i, S, t):
                        for src, b_, step, normed in (("c", t["A"], "turn_c", "c"), ("u", t["B"], "turn_l", "l")):
                            pe.wait_ge(S.dve.sem, S.DVE.at(i, normed))
                            pe.wait_ge(S.act.sem, turn_before(S.ACT, i))
                            turn_group(pe, b_, tile_in(t[src])).then_inc(S.pe.sem, S.PE.tick(step))
                            yield
                    with pe.Fori(0, TURNS) as i:
                        weave(body(w, i, SS[w], T[w]) for w in range(W))

                @block.scalar
                def _(act):
                    def body(w, i, S, t):
                        for b_, dst, step, kept, at in ((t["A"], 0, "turn_c", "c_kept", 2), (t["B"], P, "turn_l", "l_kept", 4)):
                            act.wait_ge(S.pe.sem, S.PE.at(i, step))
                            act.activation(KVT[:, bass.ds((i * W + w) * G, G), dst:dst + P], b_[:, :].rearrange("p (j d) -> p j d", d=P), ACT.Identity, scale=cols[:, at:at + 1],
                                           bias=cols[:, at + 1:at + 2]).then_inc(S.act.sem, S.ACT.tick(kept))
                            yield
                    with act.Fori(0, TURNS) as i:
                        weave(body(w, i, SS[w], T[w]) for w in range(W))
                close_streams(SS)
                close_gathers(top_before)

        def attention_2():
            with ExitStack() as ph:
                wqk = carve(SETA2, 2048, [P, HEADS, P])
                wvo = carve(flat(Y1[:, :, :]), 2048, [P, HEADS, P])
                raw = {"q_k_v": flat(Y1[:, 0:24, :]), "o": flat(XN[:, 24:32, :])}
                ycopy = sb_in(ph, "y_turned_copy", [P, 2, P])
                yrows = sb_in(ph, "y_rows", [P, 4, 2 * P], F32R)
                yparts = sb_in(ph, "y_turned_parts", [P, 4, 2 * P], F32R)
                turned = carve(flat(XN[:, :, :]), 0, [P, 24 * P])
                probs = carve(flat(XN[:, :, :]), 0, [P, 2 * 4, 256]).rearrange("p (s h) k -> p s h k", s=2)
                probsT = [sb_in(ph, f"probs_turned_{n}", [P, 2, 2, 512], F32R) for n in ("hi", "lo")]
                queries = [sb_in(ph, f"queries_{n}", [P, 4, P], F32R) for n in ("hi", "lo")]
                mixed = carve(flat(XN[:, :, :]), 2048, [P, 2 * 4, P]).rearrange("p (s h) q -> p s h q", s=2)
                nmax = sb_in(ph, "neg_max2", [P, 2, 4])
                sums = sb_in(ph, "sums2", [P, 2, 4])
                rinv = sb_in(ph, "rinv2", [P, 2, 4])

                with nc.Block() as block:
                    p0, a0 = pe_done.value, act_done.value

                    @block.sync
                    def _(sp):
                        sp.dma_start(raw["q_k_v"][:, 0:INNER], A["L2_xattn_Wq"]).then_inc(weights_x.sem, 16)
                        sp.dma_start(raw["q_k_v"][:, INNER:3 * INNER], A["L2_xattn_Wkv"]).then_inc(weights_x.sem, 16)
                        sp.dma_start(raw["o"].rearrange("p (c d) -> p c d", d=P), A["L2_xattn_Wo"].rearrange("(c p) d -> p c d", p=P)).then_inc(weights_x.sem, 16)

                    @block.tensor
                    def _(pe):
                        pe.wait_ge(weights_x.sem, 48)
                        for k in range(6):
                            for c in range(4):
                                ins = pe.transpose(bank[k][:, c * P:(c + 1) * P], raw["q_k_v"][:, (4 * k + c) * P:(4 * k + c + 1) * P], ident[:, :])
                            ins.then_inc(pe_done.sem, 1)
                        pe.wait_ge(act_done.sem, a0 + 6)
                        for k in range(8):
                            for i in range(4):
                                h = 8 * (k % 4 // 2) + 2 * i + k % 2
                                e = slice((h % 2) * HD, (h % 2 + 1) * HD)
                                at = [(n * 8 + h // 2) * P for n in range(3)]
                                q_, k_, v_ = (turned[e, a:a + P] for a in at)
                                lhs, rhs = (q_, k_) if k < 4 else (v_, raw["o"][e, (h // 2) * P:(h // 2 + 1) * P])
                                ins = pe.matmul(bank[k][:, i * P:(i + 1) * P], lhs, rhs, start=True, stop=True)
                            ins.then_inc(pe_done.sem, 1)

                    @block.scalar
                    def _(act):
                        for k in range(6):
                            act.wait_ge(pe_done.sem, p0 + k + 1)
                            act.copy(turned[:, k * 512:(k + 1) * 512], bank[k][:, :]).then_inc(act_done.sem, 1)
                        for k in range(8):
                            act.wait_ge(pe_done.sem, p0 + 6 + k + 1)
                            dst = (wqk if k < 4 else wvo)[:, :, :].rearrange("p (q i r) d -> p q i r d", q=2, r=2)[:, k % 4 // 2, :, k % 2, :]
                            src = bank[k][:, :].rearrange("p (i d) -> p i d", d=P)
                            ins = act.mul(dst, src, float(HD) ** -0.5) if k < 4 else act.copy(dst, src)
                        ins.then_inc(act_done.sem, 1)
                pe_done.value += 14
                act_done.value += 7

                UNITS = 4 * B
                FIRST, LAST = -3, UNITS + 1
                STEPS = LAST - FIRST + 1
                S_BANKS, T_BANK, Z_BANK, Q_BANK, Y_BANK = (0, 2), 4, 5, 6, 7
                PEs = Steps(pe_done, ["probs_turned_0", "scores", "queries", "probs_turned_1", "mixed", "out"])
                ACs = Steps(act_done, ["probs_hi_0", "queries_hi", "probs_hi_1", "exp", "mixed_kept"])
                D = Steps(dve_done, ["normalised", "probs_lo_0", "max", "queries_lo", "probs_lo_1"])
                PARTS = ((0, 0), (0, 1), (1, 0))
                block = ph.enter_context(nc.Block())

                def at(S, m, name):
                    return S.at(m - FIRST, name)

                def there(n):
                    return not isinstance(n, int) or 0 <= n < UNITS

                def signal(eng, S, sem, name, ins):
                    (ins or eng.drain()).then_inc(sem.sem, S.tick(name))

                def all_steps(step):
                    def run(eng):
                        for m in range(FIRST, 4):
                            step(eng, m // 4, m // 4 % 2, m % 4, m)
                        with eng.Fori(0, B // 2 - 1) as i:
                            for s in (1, 0):
                                for u in range(4):
                                    b = i * 2 + (2 - s)
                                    step(eng, b, s, u, b * 4 + u)
                        for m in range(UNITS - 4, LAST + 1):
                            step(eng, m // 4, m // 4 % 2, m % 4, m)
                    return run

                def batch_unit(b, u, ahead):
                    return b + (u + ahead) // 4, (u + ahead) % 4

                @block.gpsimd
                def _(pool):
                    def copy(b, s):
                        y = flat(KVT[:, bass.ds(b, 1), :])
                        pool.tensor_copy(yparts[:, 2 * s, :], y)
                        pool.tensor_copy(flat(ycopy[:, :, :]), y)
                        pool.drain()
                        pool.tensor_tensor(yparts[:, 2 * s + 1, :], y, yparts[:, 2 * s, :].bitcast(F32), ALU.subtract).then_inc(pool_done.sem, 1)
                    copy(0, 0)
                    pool.wait_ge(y_turned.sem, y_turned.value + 1)
                    copy(1, 1)
                    with pool.Fori(1, B // 2) as i:
                        for s in range(2):
                            pool.wait_ge(y_turned.sem, i * 2 + (s + y_turned.value))
                            copy(i * 2 + s, s)

                def pe_step(pe, b, s, u, m):
                    par = u % 2
                    b2, u2 = batch_unit(b, u, 2)
                    b3, u3 = batch_unit(b, u, 3)
                    b0, u0 = batch_unit(b, u, -2)
                    s2, s1 = (s + (u + 2) // 4) % 2, (s + (u - 1) // 4) % 2

                    def turn_probs(c):
                        if not there(m):
                            return None
                        for h in range(4):
                            ins = pe.transpose(bank[T_BANK][:, h * P:(h + 1) * P], probs[:, par, h, c * P:(c + 1) * P], ident[:, :])
                        return ins
                    if isinstance(m, int) and m == FIRST:
                        pe.wait_ge(dve_done.sem, D.base)
                    else:
                        pe.wait_ge(dve_done.sem, at(D, m - 1, "probs_lo_1"))
                    signal(pe, PEs, pe_done, "probs_turned_0", turn_probs(0))

                    ins = None
                    if there(m + 2):
                        if u2 == 0:
                            pe.wait_ge(pool_done.sem, b2 + (pool_done.value + 1))
                        for h in range(4):
                            for i, (q, y) in enumerate(PARTS):
                                ins = pe.matmul(bank[S_BANKS[par] + h // 2][:, (h % 2) * 256:(h % 2 + 1) * 256], queries[q][:, h, :], yparts[:, 2 * s2 + y, :],
                                                start=(i == 0), stop=(i == 2))
                    signal(pe, PEs, pe_done, "scores", ins)

                    if u == 2 and there(m + 2):
                        if not (isinstance(b, int) and b < 1):
                            pe.wait_ge(y_added.sem, b + y_added.value)
                        for c in range(2):
                            ins = pe.transpose(bank[Y_BANK][:, c * P:(c + 1) * P], ycopy[:, c, :], ident[:, :])
                        ins.then_inc(y_turned.sem, 1)

                    ins = None
                    if there(m + 3):
                        for h in range(4):
                            ins = pe.matmul(bank[Q_BANK][:, h * P:(h + 1) * P], wqk[:, 4 * u3 + h, :], flat(KVT[:, bass.ds(b3, 1), P:2 * P]), start=True, stop=True)
                    signal(pe, PEs, pe_done, "queries", ins)

                    if there(m):
                        pe.wait_ge(dve_done.sem, at(D, m, "probs_lo_0"))
                    signal(pe, PEs, pe_done, "probs_turned_1", turn_probs(1))

                    ins = None
                    if there(m - 1):
                        pe.wait_ge(act_done.sem, at(ACs, m - 1, "mixed_kept"))
                        for c in range(2):
                            for i, (y, p) in enumerate(PARTS):
                                ins = pe.matmul(bank[Z_BANK][:, :], yrows[:, 2 * s1 + y, c * P:(c + 1) * P], probsT[p][:, (u + 1) % 2, c, :],
                                                start=(c == 0 and i == 0), stop=(c == 1 and i == 2))
                    signal(pe, PEs, pe_done, "mixed", ins)

                    ins = None
                    if u == 2 and there(m + 2):
                        pe.wait_ge(y_kept.sem, b + (y_kept.value + 2))
                    if there(m - 2):
                        pe.wait_ge(act_done.sem, at(ACs, m - 1, "mixed_kept"))
                        if u0 == 0 and not (isinstance(b0, int) and b0 == 0):
                            pe.wait_ge(y_added.sem, b0 + y_added.value)
                        for h in range(4):
                            ins = pe.matmul(bank[Y_BANK][:, 0:P], mixed[:, par, h, :], wvo[:, 4 * u0 + h, :], start=(u0 == 0 and h == 0), stop=(u0 == 3 and h == 3),
                                            skip_group_check=True)
                    signal(pe, PEs, pe_done, "out", ins)

                def act_step(act, b, s, u, m):
                    par = u % 2

                    def keep(n, made, bank_, dst, name):
                        ins = None
                        if there(n):
                            act.wait_ge(pe_done.sem, at(PEs, m, made))
                            ins = act.copy(dst, bank[bank_][:, :])
                        signal(act, ACs, act_done, name, ins)
                    keep(m, "probs_turned_0", T_BANK, probsT[0][:, par, 0, :], "probs_hi_0")
                    if u == 2 and there(m + 2):
                        act.wait_ge(y_turned.sem, b + (y_turned.value + 2))
                        act.copy(yrows[:, 2 * (1 - s), :], bank[Y_BANK][:, 0:2 * P]).then_inc(y_hi.sem, 1)
                    keep(m + 3, "queries", Q_BANK, flat(queries[0][:, :, :]), "queries_hi")
                    keep(m, "probs_turned_1", T_BANK, probsT[0][:, par, 1, :], "probs_hi_1")
                    ins = None
                    if there(m + 2):
                        act.wait_ge(dve_done.sem, at(D, m, "max"))
                        for h in range(4):
                            ins = act.activation(probs[:, par, h, :], bank[S_BANKS[par] + h // 2][:, (h % 2) * 256:(h % 2 + 1) * 256], ACT.Exp,
                                                 bias=nmax[:, par, h:h + 1], accum_out=sums[:, par, h:h + 1])
                    signal(act, ACs, act_done, "exp", ins)
                    keep(m - 1, "mixed", Z_BANK, flat(mixed[:, (u + 1) % 2, :, :]), "mixed_kept")

                def add_rows(dve, b, m):
                    dve.wait_ge(pe_done.sem, at(PEs, m - 1, "out"))
                    xt = flat(X[:, bass.ds(b - 1, 1), :])
                    dve.tensor_tensor(xt, xt, bank[Y_BANK][:, 0:P], ALU.add).then_inc(y_added.sem, 1)

                def dve_step(dve, b, s, u, m):
                    par = u % 2

                    def keep_rest(n, hi_made, bank_, hi, lo, name):
                        ins = None
                        if there(n):
                            dve.wait_ge(act_done.sem, at(ACs, m, hi_made))
                            ins = dve.tensor_tensor(lo, bank[bank_][:, :], hi.bitcast(F32), ALU.subtract)
                        signal(dve, D, dve_done, name, ins)
                    if u == 2 and there(m - 3):
                        add_rows(dve, b, m)
                    ins = None
                    if there(m + 1):
                        p = (u + 1) % 2
                        dve.wait_ge(act_done.sem, at(ACs, m - 1, "exp"))
                        dve.reciprocal(rinv[:, p, :], sums[:, p, :])
                        dve.drain()
                        ins = dve.tensor_tensor(probs[:, p, :, :], probs[:, p, :, :], rinv[:, p, :].unsqueeze(2).to_broadcast([P, 4, 256]), ALU.mult)
                    signal(dve, D, dve_done, "normalised", ins)
                    keep_rest(m, "probs_hi_0", T_BANK, probsT[0][:, par, 0, :], probsT[1][:, par, 0, :], "probs_lo_0")
                    ins = None
                    if there(m + 2):
                        dve.wait_ge(pe_done.sem, at(PEs, m, "scores"))
                        ins = dve.tensor_reduce(nmax[:, par, :], ps[:, S_BANKS[par]:S_BANKS[par] + 2, :].rearrange("p r (h k) -> p (r h) k", k=256), AX.X, ALU.max, negate=True)
                    signal(dve, D, dve_done, "max", ins)
                    if u == 2 and there(m + 2):
                        dve.wait_ge(y_hi.sem, b + (y_hi.value + 2))
                        dve.tensor_tensor(yrows[:, 2 * (1 - s) + 1, :], bank[Y_BANK][:, 0:2 * P], yrows[:, 2 * (1 - s), :].bitcast(F32), ALU.subtract).then_inc(y_kept.sem, 1)
                    keep_rest(m + 3, "queries_hi", Q_BANK, flat(queries[0][:, :, :]), flat(queries[1][:, :, :]), "queries_lo")
                    keep_rest(m, "probs_hi_1", T_BANK, probsT[0][:, par, 1, :], probsT[1][:, par, 1, :], "probs_lo_1")

                @block.tensor
                def _(pe):
                    pe.wait_ge(act_done.sem, act_done.value)
                    all_steps(pe_step)(pe)

                @block.scalar
                def _(act):
                    all_steps(act_step)(act)

                @block.vector
                def _(dve):
                    all_steps(dve_step)(dve)
                    add_rows(dve, B, LAST + 1)
                for c in (PEs, ACs, D):
                    c.close(STEPS)
                for c in (pool_done, y_turned, y_hi, y_kept, y_added):
                    c.value += B

        def tail_only(layer):
            with ExitStack() as ph:
                SS = streams()
                T = [{"tl": tail_tiles(ph, sb_in(ph, "tail_rows", [P, G, P]), sb_in(ph, "tail_turned", [P, G, P]))} for w in range(W)]
                st = norm_tiles(ph)
                block = ph.enter_context(nc.Block())

                @block.vector
                def _(dve):
                    ch = Chain(dve)
                    with dve.Fori(0, TURNS) as i:
                        tail_norms(dve, ch, i, SS, st, T, lambda w: dve.wait_ge(SS[w].act.sem, turn_before(SS[w].ACT, i)))
                        weave(tail_dve(dve, ch, i * W + w, i, SS[w], T[w]["tl"], bank[2 * w]) for w in range(W))

                @block.tensor
                def _(pe):
                    with pe.Fori(0, TURNS) as i:
                        weave(tail_pe(pe, i, SS[w], T[w]["tl"], layer, bank[2 * w + 1], bank[2 * w]) for w in range(W))

                @block.scalar
                def _(act):
                    with act.Fori(0, TURNS) as i:
                        weave(tail_act(act, i * W + w, i, SS[w], T[w]["tl"], bank[2 * w + 1]) for w in range(W))
                close_streams(SS)

        def attention_3(top_before):
            SCALE = float(P) ** -0.5
            with ExitStack() as ph:
                SS = streams(pe=["k", "turn_u", "q", "scores", "turn_p", "mixed"],
                             act=["k_kept", "u_turned", "q_kept", "exp", "p_turned"], dve=["u_normed", "max"])
                T = []
                for w in range(W):
                    t = {"kT": carve(SETA1, 2 * w * G * P, [P, G, P]), "qT": carve(SETA1, (2 * w + 1) * G * P, [P, G, P]),
                         "probs": carve(SETA2, 2 * w * G * P, [P, G, P]), "probsT": carve(SETA2, (2 * w + 1) * G * P, [P, G, P]),
                         "u": sb_in(ph, "u_rows3", [P, G, P]), "uT": sb_in(ph, "u_turned3", [P, G, P]),
                         "sums": sb_in(ph, "sums3", [P, G]), "nmax": sb_in(ph, "neg_max3", [P, G]), "rinv": sb_in(ph, "rinv3", [P, G]),
                         "A": bank[2 * w], "B": bank[2 * w + 1]}
                    t["tl"] = tail_tiles(ph, t["u"], t["uT"])
                    T.append(t)
                st = norm_tiles(ph)
                mask_here = masks_loaded.value + 16
                block = ph.enter_context(nc.Block())

                @block.sync
                def _(sp):
                    sp.dma_start(mask[:, :], mask_dram[1:2, :]).then_inc(masks_loaded.sem, 16)

                @block.gpsimd
                def _(pool):
                    gather_turns(pool, top_before)

                @block.tensor
                def _(pe):
                    def body(w, i, S, t):
                        g, A_, B_ = i * W + w, t["A"], t["B"]
                        pe.wait_ge(S.dve.sem, turn_before(S.DVE, i))
                        pe.matmul(A_[:, :], wsmall[:, 7, :], flat(group(CTT, g)), start=True, stop=True).then_inc(S.pe.sem, S.PE.tick("k"))
                        yield
                        pe.wait_ge(S.dve.sem, S.DVE.at(i, "u_normed"))
                        turn_group(pe, B_, tile_in(t["u"])).then_inc(S.pe.sem, S.PE.tick("turn_u"))
                        yield
                        pe.wait_ge(S.act.sem, S.ACT.at(i, "u_turned"))
                        pe.matmul(B_[:, :], wsmall[:, 6, :], flat(t["uT"][:, :, :]), start=True, stop=True).then_inc(S.pe.sem, S.PE.tick("q"))
                        pe.matmul(A_[:, :], ones[0:1, :], mask[:, bass.ds(g * (G * P), G * P)], start=True, stop=False, skip_group_check=True)
                        yield
                        pe.wait_ge(S.act.sem, S.ACT.at(i, "q_kept"))
                        for j in range(G):
                            ins = pe.matmul(A_[:, j * P:(j + 1) * P], t["qT"][:, j, :], t["kT"][:, j, :], start=False, stop=True, skip_group_check=True)
                        ins.then_inc(S.pe.sem, S.PE.tick("scores"))
                        yield
                        pe.wait_ge(S.act.sem, S.ACT.at(i, "exp"))
                        turn_group(pe, B_, tile_in(t["probs"])).then_inc(S.pe.sem, S.PE.tick("turn_p"))
                        yield
                        pe.wait_ge(S.act.sem, S.ACT.at(i, "p_turned"))
                        for j in range(G):
                            ins = pe.matmul(A_[:, j * P:(j + 1) * P], t["probsT"][:, j, :], flat(CT[:, bass.ds(g * G + j, 1), :]), start=True, stop=True)
                        ins.then_inc(S.pe.sem, S.PE.tick("mixed"))
                        yield
                        yield from tail_pe(pe, i, S, t["tl"], 3, B_, A_)
                    pe.wait_ge(masks_loaded.sem, mask_here)
                    with pe.Fori(0, TURNS) as i:
                        weave(body(w, i, SS[w], T[w]) for w in range(W))

                @block.scalar
                def _(act):
                    def body(w, i, S, t):
                        g, A_, B_ = i * W + w, t["A"], t["B"]
                        act.wait_ge(S.pe.sem, S.PE.at(i, "k"))
                        act.activation(flat(t["kT"]), A_[:, :], ACT.Identity, bias=cols[:, 1:2]).then_inc(S.act.sem, S.ACT.tick("k_kept"))
                        yield
                        act.wait_ge(S.pe.sem, S.PE.at(i, "turn_u"))
                        act.copy(flat(t["uT"][:, :, :]), B_[:, :]).then_inc(S.act.sem, S.ACT.tick("u_turned"))
                        yield
                        act.wait_ge(S.pe.sem, S.PE.at(i, "q"))
                        act.activation(flat(t["qT"]), B_[:, :], ACT.Identity, bias=cols[:, 0:1]).then_inc(S.act.sem, S.ACT.tick("q_kept"))
                        yield
                        act.wait_ge(S.dve.sem, S.DVE.at(i, "max"))
                        for j in range(G):
                            ins = act.activation(t["probs"][:, j, :], A_[:, j * P:(j + 1) * P], ACT.Exp, bias=t["nmax"][:, j:j + 1], scale=SCALE, accum_out=t["sums"][:, j:j + 1])
                        ins.then_inc(S.act.sem, S.ACT.tick("exp"))
                        yield
                        act.wait_ge(S.pe.sem, S.PE.at(i, "turn_p"))
                        act.copy(flat(t["probsT"]), B_[:, :]).then_inc(S.act.sem, S.ACT.tick("p_turned"))
                        yield
                        yield from tail_act(act, g, i, S, t["tl"], B_)
                    with act.Fori(0, TURNS) as i:
                        weave(body(w, i, SS[w], T[w]) for w in range(W))

                @block.vector
                def _(dve):
                    ch = Chain(dve)

                    def body(w, i, S, t):
                        g, A_ = i * W + w, t["A"]
                        dve.wait_ge(S.pe.sem, S.PE.at(i, "scores"))
                        ch.link(dve.tensor_reduce(t["nmax"][:, :], A_[:, :].rearrange("p (j l) -> p j l", j=G), AX.X, ALU.max, negate=True))
                        dve.tensor_scalar(t["nmax"][:, :], t["nmax"][:, :], SCALE, None, ALU.mult).then_inc(S.dve.sem, S.DVE.tick("max"))
                        yield
                        dve.wait_ge(S.act.sem, S.ACT.at(i, "exp"))
                        ch.link(dve.reciprocal(t["rinv"][:, :], t["sums"][:, :]))
                        yield
                        dve.wait_ge(S.pe.sem, S.PE.at(i, "mixed"))
                        for j in range(G):
                            xt = x_tile(g)(j)
                            dve.scalar_tensor_tensor(xt, A_[:, j * P:(j + 1) * P], t["rinv"][:, j:j + 1], xt, ALU.mult, ALU.add)
                        yield
                    with dve.Fori(0, TURNS) as i:
                        combine_turn(dve, ch, i, top_before)
                        norm_all(dve, ch, st, lambda w: x_tile(i * W + w), lambda w: tile_in(T[w]["u"]),
                                 lambda w, ins: ins.then_inc(SS[w].dve.sem, SS[w].DVE.tick("u_normed")),
                                 lambda w: dve.wait_ge(SS[w].act.sem, turn_before(SS[w].ACT, i)))
                        weave(body(w, i, SS[w], T[w]) for w in range(W))
                        ch.link()
                        tail_norms(dve, ch, i, SS, st, T)
                        weave(tail_dve(dve, ch, i * W + w, i, SS[w], T[w]["tl"], T[w]["A"]) for w in range(W))
                close_streams(SS)
                close_gathers(top_before)

        route(0, 2, 0)
        experts(0)
        attention_1(2)
        route(1, 2, CAPACITY)
        experts(1)
        attention_2_norms(2)
        attention_2()
        tail_only(2)
        route(2, 2, 0)
        experts(2)
        attention_3(2)
        route(3, 1, 0)
        experts(3)
        combine_and_store(1)


_INS = ['x', 'ctx_1024', 'mask_BxS2_if1', 'mask_BxS2_ik1', 'L0_xattn_W0', 'L0_xattn_W1', 'L0_ffn_router_w', 'L0_ffn_w1', 'L0_ffn_b1', 'L0_ffn_w2', 'L0_ffn_b2', 'L1_xattn_Wq', 'L1_xattn_bq', 'L1_xattn_Wk', 'L1_xattn_bk', 'L1_xattn_Wv', 'L1_xattn_bv', 'L1_xattn_Wp', 'L1_xattn_bp', 'L1_ffn_router_w', 'L1_ffn_router_b', 'L1_ffn_W', 'L1_ffn_V', 'L1_ffn_W_out', 'L2_xattn_ln1_w', 'L2_xattn_ln1_b', 'L2_xattn_ln2_w', 'L2_xattn_ln2_b', 'L2_xattn_Wq', 'L2_xattn_Wkv', 'L2_xattn_Wo', 'L2_ffn_gate_w', 'L2_ffn_gate_up_w', 'L2_ffn_down_w', 'L3_xattn_Wq_w', 'L3_xattn_Wq_b', 'L3_xattn_Wk_w', 'L3_xattn_Wk_b', 'L3_ffn_gate_w', 'L3_ffn_w1', 'L3_ffn_b1', 'L3_ffn_w2', 'L3_ffn_b2']


def kernel(**inputs):
    import numpy as _np
    import concourse.bacc as _bacc
    from concourse import mybir as _mybir
    from concourse.bass_utils import run_bass_kernel_spmd as _run

    nc = _bacc.Bacc("TRN2", target_bir_lowering=False, num_devices=1)
    arrays, handles = {}, {}
    for name in _INS:
        a = _np.ascontiguousarray(inputs[name])
        arrays[f"in_{name}_dram"] = a
        handles[name] = nc.dram_tensor(f"in_{name}_dram", a.shape, _mybir.dt.from_np(a.dtype), kind="ExternalInput").ap()
    out = nc.dram_tensor("out_0_dram", (B, P, P), _mybir.dt.float32, kind="ExternalOutput").ap()
    build(nc, handles, out)
    r = _run(nc, [arrays], core_ids=[0])
    return r.results[0]["out_0_dram"]
```
